# Optimizing a Trainium2 kernel written in Bass

```python
import numpy as np
import jax
import jax.numpy as jnp

def _softmax(x, axis=-1):
    return jax.nn.softmax(x, axis=axis)

def _gelu(x):
    return jax.nn.gelu(x, approximate=True)

def _silu(x):
    return jax.nn.silu(x)

def _sigmoid(x):
    return jax.nn.sigmoid(x)

def _layernorm(x, axis=-1, eps=1e-05):
    m = jnp.mean(x, axis=axis, keepdims=True)
    v = jnp.var(x, axis=axis, keepdims=True)
    return (x - m) / jnp.sqrt(v + eps)

def _scatter_add(tgt, idx, src, axis=0):
    return tgt.at[idx].add(src)

def _segment_sum(src, seg, n):
    return jax.ops.segment_sum(src, seg, n)
kernel_name = 'mk_vit_tower_cls_d1_tok_img768_r4_3cee4f'

def setup_inputs(seed: int=0):
    np.random.seed(seed)
    _w = jnp.asarray

    def _rec_inputs():
        import jax
        import jax.numpy as jnp
        _rk = jax.random.key(seed)
        x = -0.000356955 + 1 * jax.random.normal(jax.random.fold_in(_rk, 1), (64, 3, 224, 224), jnp.float32)
        cls_tok = 0.02 * jax.random.normal(jax.random.fold_in(_rk, 5), (1, 1, 192), jnp.float32)
        return (x, cls_tok)
    x, cls_tok = _rec_inputs()

    def _L0_tok_setup():
        import jax, jax.numpy as jnp
        import numpy as np
        N_PATCHES = 14
        HIDDEN_D = 192
        N_HEADS = 12
        D_HEAD = HIDDEN_D // N_HEADS
        SEQ = N_PATCHES ** 2 + 1
        INPUT_D = 3 * 16 * 16
        LN_EPS = 1e-05

        def positional_embeddings(seq_len, d):
            i = jnp.arange(seq_len, dtype=jnp.float32)[:, None]
            j = jnp.arange(d, dtype=jnp.float32)[None, :]
            even = (jnp.arange(d) % 2 == 0)[None, :]
            denom_even = jnp.power(10000.0, j / d)
            denom_odd = jnp.power(10000.0, (j - 1.0) / d)
            return jnp.where(even, jnp.sin(i / denom_even), jnp.cos(i / denom_odd))

        def _forward(images, W_map, b_map, class_token, ln_w, ln_b, Wq, bq, Wk, bk, Wv, bv):
            n = images.shape[0]
            patches = images.reshape(n, N_PATCHES ** 2, INPUT_D)
            tokens = jnp.einsum('npi,di->npd', patches, W_map) + b_map
            cls = jnp.broadcast_to(class_token[None], (n, 1, HIDDEN_D))
            tokens = jnp.concatenate([cls, tokens], axis=1)
            tokens = tokens + positional_embeddings(SEQ, HIDDEN_D)[None]
            mean = jnp.mean(tokens, axis=(-2, -1), keepdims=True)
            var = jnp.var(tokens, axis=(-2, -1), keepdims=True)
            x = (tokens - mean) / jnp.sqrt(var + LN_EPS) * ln_w + ln_b
            xh = x.reshape(n, SEQ, N_HEADS, D_HEAD)
            q = jnp.einsum('bshd,hed->bshe', xh, Wq) + bq[None, None]
            k = jnp.einsum('bshd,hed->bshe', xh, Wk) + bk[None, None]
            v = jnp.einsum('bshd,hed->bshe', xh, Wv) + bv[None, None]
            att = jax.nn.softmax(jnp.einsum('bshd,bthd->bhst', q, k) / jnp.sqrt(jnp.float32(D_HEAD)), axis=-1)
            msa = jnp.einsum('bhst,bthd->bshd', att, v).reshape(n, SEQ, HIDDEN_D)
            return tokens + msa
        key = jax.random.key(seed)
        ks = jax.random.split(key, 12)
        s = 0.02
        return {'images': jax.random.normal(ks[0], (128, 3, 224, 224), dtype=jnp.float32), 'W_map': jax.random.normal(ks[1], (HIDDEN_D, INPUT_D), dtype=jnp.float32) * s, 'b_map': jax.random.normal(ks[2], (HIDDEN_D,), dtype=jnp.float32) * s, 'class_token': jax.random.uniform(ks[3], (1, HIDDEN_D), dtype=jnp.float32), 'ln_w': jnp.ones((SEQ, HIDDEN_D), dtype=jnp.float32), 'ln_b': jnp.zeros((SEQ, HIDDEN_D), dtype=jnp.float32), 'Wq': jax.random.normal(ks[4], (N_HEADS, D_HEAD, D_HEAD), dtype=jnp.float32) * s, 'bq': jax.random.normal(ks[5], (N_HEADS, D_HEAD), dtype=jnp.float32) * s, 'Wk': jax.random.normal(ks[6], (N_HEADS, D_HEAD, D_HEAD), dtype=jnp.float32) * s, 'bk': jax.random.normal(ks[7], (N_HEADS, D_HEAD), dtype=jnp.float32) * s, 'Wv': jax.random.normal(ks[8], (N_HEADS, D_HEAD, D_HEAD), dtype=jnp.float32) * s, 'bv': jax.random.normal(ks[9], (N_HEADS, D_HEAD), dtype=jnp.float32) * s}
    _L0_tok_all = _L0_tok_setup()
    _L0_tok_in = {k: v for k, v in _L0_tok_all.items() if k in ('W_map', 'b_map', 'class_token', 'ln_w', 'ln_b', 'Wq', 'bq', 'Wk', 'bk', 'Wv', 'bv')}
    del _L0_tok_all

    def _L0_attn_setup():
        import jax, jax.numpy as jnp
        import numpy as np
        import math
        H = 12
        LOGIT_SCALE_MAX = math.log(1.0 / 0.01)

        def _normalize(t, eps=1e-12):
            n = jnp.linalg.norm(t, axis=-1, keepdims=True)
            return t / jnp.maximum(n, eps)
        key = jax.random.key(seed)
        ks = jax.random.split(key, 4)
        L, N, C = (256, 8, 192)
        scale = (C // H) ** (-0.5)
        return {'x': jax.random.normal(ks[0], (L, N, C), jnp.float32), 'in_proj_weight': jax.random.normal(ks[1], (3 * C, C), jnp.float32) * scale, 'in_proj_bias': jnp.zeros((3 * C,), jnp.float32), 'logit_scale': jnp.full((H, 1, 1), jnp.log(10.0), jnp.float32), 'head_scale': jnp.ones((H, 1, 1), jnp.float32), 'out_w': jax.random.normal(ks[2], (C, C), jnp.float32) * scale, 'out_b': jnp.zeros((C,), jnp.float32)}
    _L0_attn_all = _L0_attn_setup()
    _L0_attn_in = {k: v for k, v in _L0_attn_all.items() if k in ('in_proj_weight', 'in_proj_bias', 'logit_scale', 'head_scale', 'out_w', 'out_b')}
    del _L0_attn_all

    def _L0_ffn_setup():
        import jax, jax.numpy as jnp
        import numpy as np
        B, S, D = (2, 256, 192)
        I = 96
        E = 8
        G = 4
        TOPK_GROUPS = 2
        K = 2
        ROUTE_SCALE = 1.0
        ALPHA, LIMIT = (1.702, 7.0)

        def swiglu(h):
            xg = jnp.minimum(h[..., ::2], LIMIT)
            xl = jnp.clip(h[..., 1::2], -LIMIT, LIMIT)
            return xg * jax.nn.sigmoid(ALPHA * xg) * (xl + 1.0)

        def gate(x, gate_w, gate_b):
            scores = jax.nn.softmax(jnp.einsum('td,ed->te', x, gate_w).astype(jnp.float32), axis=-1)
            original_scores = scores
            s = scores + gate_b
            T = x.shape[0]
            sg = s.reshape(T, G, E // G)
            group_scores = jnp.sum(jax.lax.top_k(sg, 2)[0], axis=-1)
            _, gidx = jax.lax.top_k(group_scores, TOPK_GROUPS)
            keep = jnp.any(jax.nn.one_hot(gidx, G, dtype=jnp.bool_), axis=1)
            sg = jnp.where(keep[:, :, None], sg, -jnp.inf)
            s = sg.reshape(T, E)
            _, idx = jax.lax.top_k(s, K)
            w = jnp.take_along_axis(original_scores, idx, axis=1) * ROUTE_SCALE
            return (w.astype(x.dtype), idx)

        def expert_ffn(x, W1, B1, W3, B3, W2, B2):
            h1 = jnp.einsum('td,edh->teh', x, W1) + B1
            h3 = jnp.einsum('td,edh->teh', x, W3) + B3
            g = swiglu(h1 * h3)
            return jnp.einsum('tei,eid->ted', g, W2) + B2

        def shared_ffn(x, Ws1, Bs1, Ws3, Bs3, Ws2, Bs2):
            h = (x @ Ws1 + Bs1) * (x @ Ws3 + Bs3)
            return swiglu(h) @ Ws2 + Bs2
        key = jax.random.key(seed)
        ks = jax.random.split(key, 16)
        sc = 0.02
        inp = {'x': jax.random.normal(ks[0], (B, S, D), jnp.float32), 'gate_w': jax.random.normal(ks[1], (E, D), jnp.float32) * sc, 'gate_b': jax.random.normal(ks[2], (E,), jnp.float32) * sc, 'W1': jax.random.normal(ks[3], (E, D, 2 * I), jnp.float32) * sc, 'B1': jax.random.normal(ks[4], (E, 2 * I), jnp.float32) * sc, 'W3': jax.random.normal(ks[5], (E, D, 2 * I), jnp.float32) * sc, 'B3': jax.random.normal(ks[6], (E, 2 * I), jnp.float32) * sc, 'W2': jax.random.normal(ks[7], (E, I, D), jnp.float32) * sc, 'B2': jax.random.normal(ks[8], (E, D), jnp.float32) * sc, 'Ws1': jax.random.normal(ks[9], (D, 2 * I), jnp.float32) * sc, 'Bs1': jax.random.normal(ks[10], (2 * I,), jnp.float32) * sc, 'Ws3': jax.random.normal(ks[11], (D, 2 * I), jnp.float32) * sc, 'Bs3': jax.random.normal(ks[12], (2 * I,), jnp.float32) * sc, 'Ws2': jax.random.normal(ks[13], (I, D), jnp.float32) * sc, 'Bs2': jax.random.normal(ks[14], (D,), jnp.float32) * sc}
        return inp
    _L0_ffn_all = _L0_ffn_setup()
    _L0_ffn_in = {k: v for k, v in _L0_ffn_all.items() if k in ('gate_w', 'gate_b', 'W1', 'B1', 'W3', 'B3', 'W2', 'B2', 'Ws1', 'Bs1', 'Ws3', 'Bs3', 'Ws2', 'Bs2')}
    del _L0_ffn_all
    return {'x': x, 'cls_tok': cls_tok, 'L0_tok_W_map': _L0_tok_in['W_map'], 'L0_tok_b_map': _L0_tok_in['b_map'], 'L0_tok_class_token': _L0_tok_in['class_token'], 'L0_tok_ln_w': _L0_tok_in['ln_w'], 'L0_tok_ln_b': _L0_tok_in['ln_b'], 'L0_tok_Wq': _L0_tok_in['Wq'], 'L0_tok_bq': _L0_tok_in['bq'], 'L0_tok_Wk': _L0_tok_in['Wk'], 'L0_tok_bk': _L0_tok_in['bk'], 'L0_tok_Wv': _L0_tok_in['Wv'], 'L0_tok_bv': _L0_tok_in['bv'], 'L0_attn_in_proj_weight': _L0_attn_in['in_proj_weight'], 'L0_attn_in_proj_bias': _L0_attn_in['in_proj_bias'], 'L0_attn_logit_scale': _L0_attn_in['logit_scale'], 'L0_attn_head_scale': _L0_attn_in['head_scale'], 'L0_attn_out_w': _L0_attn_in['out_w'], 'L0_attn_out_b': _L0_attn_in['out_b'], 'L0_ffn_gate_w': _L0_ffn_in['gate_w'], 'L0_ffn_gate_b': _L0_ffn_in['gate_b'], 'L0_ffn_W1': _L0_ffn_in['W1'], 'L0_ffn_B1': _L0_ffn_in['B1'], 'L0_ffn_W3': _L0_ffn_in['W3'], 'L0_ffn_B3': _L0_ffn_in['B3'], 'L0_ffn_W2': _L0_ffn_in['W2'], 'L0_ffn_B2': _L0_ffn_in['B2'], 'L0_ffn_Ws1': _L0_ffn_in['Ws1'], 'L0_ffn_Bs1': _L0_ffn_in['Bs1'], 'L0_ffn_Ws3': _L0_ffn_in['Ws3'], 'L0_ffn_Bs3': _L0_ffn_in['Bs3'], 'L0_ffn_Ws2': _L0_ffn_in['Ws2'], 'L0_ffn_Bs2': _L0_ffn_in['Bs2']}

def reference(x, cls_tok, L0_tok_W_map, L0_tok_b_map, L0_tok_class_token, L0_tok_ln_w, L0_tok_ln_b, L0_tok_Wq, L0_tok_bq, L0_tok_Wk, L0_tok_bk, L0_tok_Wv, L0_tok_bv, L0_attn_in_proj_weight, L0_attn_in_proj_bias, L0_attn_logit_scale, L0_attn_head_scale, L0_attn_out_w, L0_attn_out_b, L0_ffn_gate_w, L0_ffn_gate_b, L0_ffn_W1, L0_ffn_B1, L0_ffn_W3, L0_ffn_B3, L0_ffn_W2, L0_ffn_B2, L0_ffn_Ws1, L0_ffn_Bs1, L0_ffn_Ws3, L0_ffn_Bs3, L0_ffn_Ws2, L0_ffn_Bs2):
    import jax
    import jax.numpy as jnp

    def _L0_tok_ref(images, W_map, b_map, class_token, ln_w, ln_b, Wq, bq, Wk, bk, Wv, bv):
        import jax, jax.numpy as jnp
        import numpy as np
        N_PATCHES = 14
        HIDDEN_D = 192
        N_HEADS = 12
        D_HEAD = HIDDEN_D // N_HEADS
        SEQ = N_PATCHES ** 2 + 1
        INPUT_D = 3 * 16 * 16
        LN_EPS = 1e-05

        def positional_embeddings(seq_len, d):
            i = jnp.arange(seq_len, dtype=jnp.float32)[:, None]
            j = jnp.arange(d, dtype=jnp.float32)[None, :]
            even = (jnp.arange(d) % 2 == 0)[None, :]
            denom_even = jnp.power(10000.0, j / d)
            denom_odd = jnp.power(10000.0, (j - 1.0) / d)
            return jnp.where(even, jnp.sin(i / denom_even), jnp.cos(i / denom_odd))

        def _forward(images, W_map, b_map, class_token, ln_w, ln_b, Wq, bq, Wk, bk, Wv, bv):
            n = images.shape[0]
            patches = images.reshape(n, N_PATCHES ** 2, INPUT_D)
            tokens = jnp.einsum('npi,di->npd', patches, W_map) + b_map
            cls = jnp.broadcast_to(class_token[None], (n, 1, HIDDEN_D))
            tokens = jnp.concatenate([cls, tokens], axis=1)
            tokens = tokens + positional_embeddings(SEQ, HIDDEN_D)[None]
            mean = jnp.mean(tokens, axis=(-2, -1), keepdims=True)
            var = jnp.var(tokens, axis=(-2, -1), keepdims=True)
            x = (tokens - mean) / jnp.sqrt(var + LN_EPS) * ln_w + ln_b
            xh = x.reshape(n, SEQ, N_HEADS, D_HEAD)
            q = jnp.einsum('bshd,hed->bshe', xh, Wq) + bq[None, None]
            k = jnp.einsum('bshd,hed->bshe', xh, Wk) + bk[None, None]
            v = jnp.einsum('bshd,hed->bshe', xh, Wv) + bv[None, None]
            att = jax.nn.softmax(jnp.einsum('bshd,bthd->bhst', q, k) / jnp.sqrt(jnp.float32(D_HEAD)), axis=-1)
            msa = jnp.einsum('bhst,bthd->bshd', att, v).reshape(n, SEQ, HIDDEN_D)
            return tokens + msa
        return _forward(images, W_map, b_map, class_token, ln_w, ln_b, Wq, bq, Wk, bk, Wv, bv)

    def _L0_attn_ref(x, in_proj_weight, in_proj_bias, logit_scale, head_scale, out_w, out_b):
        import jax, jax.numpy as jnp
        import numpy as np
        import math
        H = 12
        LOGIT_SCALE_MAX = math.log(1.0 / 0.01)

        def _normalize(t, eps=1e-12):
            n = jnp.linalg.norm(t, axis=-1, keepdims=True)
            return t / jnp.maximum(n, eps)
        L, N, C = x.shape
        D = C // H
        qkv = x @ in_proj_weight.T + in_proj_bias
        q, k, v = jnp.split(qkv, 3, axis=-1)

        def to_heads(t):
            return t.reshape(L, N, H, D).transpose(1, 2, 0, 3)
        q, k, v = (to_heads(q), to_heads(k), to_heads(v))
        attn = jnp.einsum('nhld,nhmd->nhlm', _normalize(q), _normalize(k))
        ls = jnp.exp(jnp.minimum(logit_scale, LOGIT_SCALE_MAX))
        attn = attn * ls[None]
        attn = jax.nn.softmax(attn, axis=-1)
        o = jnp.einsum('nhlm,nhmd->nhld', attn, v)
        o = o * head_scale[None]
        o = o.transpose(2, 0, 1, 3).reshape(L, N, C)
        return o @ out_w.T + out_b

    def _L0_ffn_ref(x, gate_w, gate_b, W1, B1, W3, B3, W2, B2, Ws1, Bs1, Ws3, Bs3, Ws2, Bs2):
        import jax, jax.numpy as jnp
        import numpy as np
        B, S, D = (2, 256, 192)
        I = 96
        E = 8
        G = 4
        TOPK_GROUPS = 2
        K = 2
        ROUTE_SCALE = 1.0
        ALPHA, LIMIT = (1.702, 7.0)

        def swiglu(h):
            xg = jnp.minimum(h[..., ::2], LIMIT)
            xl = jnp.clip(h[..., 1::2], -LIMIT, LIMIT)
            return xg * jax.nn.sigmoid(ALPHA * xg) * (xl + 1.0)

        def gate(x, gate_w, gate_b):
            scores = jax.nn.softmax(jnp.einsum('td,ed->te', x, gate_w).astype(jnp.float32), axis=-1)
            original_scores = scores
            s = scores + gate_b
            T = x.shape[0]
            sg = s.reshape(T, G, E // G)
            group_scores = jnp.sum(jax.lax.top_k(sg, 2)[0], axis=-1)
            _, gidx = jax.lax.top_k(group_scores, TOPK_GROUPS)
            keep = jnp.any(jax.nn.one_hot(gidx, G, dtype=jnp.bool_), axis=1)
            sg = jnp.where(keep[:, :, None], sg, -jnp.inf)
            s = sg.reshape(T, E)
            _, idx = jax.lax.top_k(s, K)
            w = jnp.take_along_axis(original_scores, idx, axis=1) * ROUTE_SCALE
            return (w.astype(x.dtype), idx)

        def expert_ffn(x, W1, B1, W3, B3, W2, B2):
            h1 = jnp.einsum('td,edh->teh', x, W1) + B1
            h3 = jnp.einsum('td,edh->teh', x, W3) + B3
            g = swiglu(h1 * h3)
            return jnp.einsum('tei,eid->ted', g, W2) + B2

        def shared_ffn(x, Ws1, Bs1, Ws3, Bs3, Ws2, Bs2):
            h = (x @ Ws1 + Bs1) * (x @ Ws3 + Bs3)
            return swiglu(h) @ Ws2 + Bs2
        inp_shape = x.shape
        xt = x.reshape(-1, D)
        w, idx = gate(xt, gate_w, gate_b)
        combine = jnp.einsum('tk,tke->te', w, jax.nn.one_hot(idx, E, dtype=w.dtype))
        per_expert = expert_ffn(xt, W1, B1, W3, B3, W2, B2)
        routed = jnp.einsum('ted,te->td', per_expert, combine)
        out = routed + shared_ffn(xt, Ws1, Bs1, Ws3, Bs3, Ws2, Bs2)
        return out.reshape(inp_shape)
    h = _L0_tok_ref(x, L0_tok_W_map, L0_tok_b_map, L0_tok_class_token, L0_tok_ln_w, L0_tok_ln_b, L0_tok_Wq, L0_tok_bq, L0_tok_Wk, L0_tok_bk, L0_tok_Wv, L0_tok_bv)
    h = jnp.concatenate([jnp.broadcast_to(cls_tok, (h.shape[0], 1, h.shape[2])), h], axis=1)
    h = h + _L0_attn_ref(_layernorm(h, axis=-1), L0_attn_in_proj_weight, L0_attn_in_proj_bias, L0_attn_logit_scale, L0_attn_head_scale, L0_attn_out_w, L0_attn_out_b)
    h = h + _L0_ffn_ref(_layernorm(h, axis=-1), L0_ffn_gate_w, L0_ffn_gate_b, L0_ffn_W1, L0_ffn_B1, L0_ffn_W3, L0_ffn_B3, L0_ffn_W2, L0_ffn_B2, L0_ffn_Ws1, L0_ffn_Bs1, L0_ffn_Ws3, L0_ffn_Bs3, L0_ffn_Ws2, L0_ffn_Bs2)
    return h

_drawn_inputs = setup_inputs


def setup_inputs(seed=0):
    import zlib

    import numpy as np

    out = dict(_drawn_inputs(seed))
    spreads = {'L0_tok_ln_w': (1.0, 0.6),
     'L0_tok_ln_b': (0.0, 0.8),
     'L0_attn_in_proj_bias': (0.0, 0.1),
     'L0_attn_logit_scale': (2.3025851249694824, 0.2),
     'L0_attn_head_scale': (1.0, 0.2),
     'L0_attn_out_b': (0.0, 0.8)}
    factors = {'L0_tok_Wq': 8.0,
     'L0_tok_bq': 8.0,
     'L0_tok_Wk': 8.0,
     'L0_tok_bk': 64.0,
     'L0_ffn_gate_w': 8.0,
     'L0_ffn_gate_b': 8.0,
     'L0_ffn_W1': 8.0,
     'L0_ffn_B1': 8.0,
     'L0_ffn_W3': 8.0,
     'L0_ffn_B3': 8.0,
     'L0_ffn_W2': 8.0,
     'L0_ffn_B2': 64.0,
     'L0_ffn_Ws1': 8.0,
     'L0_ffn_Bs1': 8.0,
     'L0_ffn_Ws3': 8.0,
     'L0_ffn_Bs3': 8.0,
     'L0_ffn_Ws2': 8.0,
     'L0_ffn_Bs2': 57.851}
    for name, (base, spread) in spreads.items():
        noise = np.random.default_rng([zlib.crc32(name.encode()), seed]).standard_normal(out[name].shape)
        drawn = base * np.exp(spread * noise) if base else spread * noise
        out[name] = jnp.asarray(drawn.astype(out[name].dtype))
    for name, factor in factors.items():
        out[name] = (out[name] * factor).astype(out[name].dtype)
    return out
```

```python
from contextlib import ExitStack

import numpy as np

import concourse.bass as bass
from concourse import mybir
from concourse.alu_op_type import AluOpType as ALU

ACT = mybir.ActivationFunctionType
AX = mybir.AxisListType
F32 = mybir.dt.float32
F32R = mybir.dt.float32r
BF16 = mybir.dt.bfloat16
I32 = mybir.dt.int32

IMAGES = 64
PATCHES = 196
PIX = 768
PC = PIX // 128
D = 192
HALF = D // 2
K1 = HALF + 1
H = 12
DH = D // H
SEQ = PATCHES + 2
B = SEQ // 2
PB = PATCHES // 2
HP = H // 2
EXPERTS = 8
EX = EXPERTS + 1
INNER = 96
ROWS = EX * INNER
CH = -(-ROWS // 128)
KINDS = 4
PART = KINDS * ROWS // 2
LIMIT = 7.0
ALPHA = 1.702
EPS = 1e-5
NORM_EPS = 1e-12
SCALE_MAX = float(np.log(100.0))
HALVES_COPIES = 4
RSQRT_GUESS = float(0x5F3759DF)
NEWTON = 3
BIG = 3.0e38
T = 128
TILES = SEQ * IMAGES // T
GT = 3
GROUPS = TILES // GT
GC = GT * T


def chunk_rows(j):
    return min(128, ROWS - 128 * j)


def vit_block(nc, x, ident, base, pos, ln_w, ln_b, mean_w, keep, tri4, tri8, expand, w_map, w_qkv1, w_qkv2,
              logit, w_out, head_scale, gate_w, gate_b, w_up, w_down, b_down, h1_dram, out):
    with ExitStack() as ctx:
        def sb(name, shape, dt=F32):
            return ctx.enter_context(nc.sbuf_tensor(name, shape, dt))

        def sem(name):
            return ctx.enter_context(nc.semaphore(name))

        bank = [ctx.enter_context(nc.psum_tensor(f"bank{n}", [128, 512], F32)) for n in range(8)]

        ident_sb = sb("ident_sb", [128, 128])
        neg_ident = sb("neg_ident", [128, 128], BF16)
        embed_add = sb("embed_add", [B, 2, D])
        pos_sb = sb("pos_sb", [B, 2, D])
        ln_w_sb = sb("ln_w_sb", [B, 2, D])
        ln_b_sb = sb("ln_b_sb", [B, 2, D])
        mean_w_sb = sb("mean_w_sb", [B, 2, B])
        keep_sb = sb("keep_sb", [B, 2])
        tri4_sb = sb("tri4_sb", [T, 4, 4])
        tri8_sb = sb("tri8_sb", [T, EXPERTS, EXPERTS])
        expand_sb = sb("expand_sb", [EX, CH, 128])
        w_map_sb = sb("w_map_sb", [128, PC, D])
        w_qkv1_sb = sb("w_qkv1_sb", [K1, 2, 3 * HALF])
        w_qkv2_sb = sb("w_qkv2_sb", [K1, 2, 3 * D])
        logit_sb = sb("logit_sb", [T, H])
        logit_scale = sb("logit_scale", [T, H])
        w_out_sb = sb("w_out_sb", [K1, 2, D])
        head_scale_sb = sb("head_scale_sb", [K1, 2])
        w_out_scaled = sb("w_out_scaled", [K1, 2, D])
        gate_w_sb = sb("gate_w_sb", [K1, 2, EXPERTS])
        gate_b_sb = sb("gate_b_sb", [T, EXPERTS])
        w_up_hi = sb("w_up_hi", [K1, 2, KINDS * ROWS], F32R)
        w_up_lo = sb("w_up_lo", [K1, 2, KINDS * ROWS], F32R)
        w_down_sb = sb("w_down_sb", [128, CH, D])
        b_down_sb = sb("b_down_sb", [EX, D])

        patches_or_rows = sb("patches_or_rows", [128, 4 * PIX])
        patches = patches_or_rows[0:PB, :].rearrange("p (u b n) -> p u b n", u=2, b=2)
        patches_t = sb("patches_t", [128, PC, SEQ])
        patches_t_flat = patches_t[:, :, :].rearrange("p c s -> p (c s)")
        tok = sb("tok", [B, 2, D])
        stats = sb("stats", [B, 2, 6])
        mv = sb("mv", [B, 2, 2])
        dev = sb("dev", [B, 2])
        var = sb("var", [B, 2])
        veps = sb("veps", [B, 2])
        half_y = sb("half_y", [B, 48])
        rstd = sb("rstd", [B, 2])
        xn = sb("xn", [B, 2, D])
        x_t = sb("x_t", [K1, 2, SEQ])
        qkn = sb("qkn", [B, 2, 2 * H, DH])
        stack = sb("stack", [B, 2, 2 * H, HALVES_COPIES, DH], F32R)
        k_st = sb("k_st", [128, HP, SEQ], F32R)
        q_bd = sb("q_bd", [128, HP, 2, SEQ], F32R)
        v_ones = sb("v_ones", [B, 2, H, 32])
        row_max = sb("row_max", [B, 2, H], BF16)
        probs = sb("probs", [B, 2, 2 * SEQ])
        o_t = sb("o_t", [128, 3, SEQ])
        r_den = sb("r_den", [B, 2, H])
        o_n = sb("o_n", [B, 2, D])
        h1 = sb("h1", [B, 2, D])

        h_in = sb("h_in", [T, GT, D])
        stats2 = sb("stats2", [T, 6])
        mv2 = sb("mv2", [T, 2])
        veps2 = sb("veps2", [T, 1])
        rstd2 = sb("rstd2", [T, 1])
        half_y2 = sb("half_y2", [T, 2 * H])
        xn2 = sb("xn2", [T, D])
        xn3 = patches_t_flat[:, GC + GT * D:GC + GT * D + D]
        x_t2 = sb("x_t2", [K1, 2, T])
        qk2 = sb("qk2", [T, 2 * H, DH])
        qk_sq = sb("qk_sq", [T, 2 * H, DH])
        norm2 = sb("norm2", [T, 2 * H])
        rnorm = sb("rnorm", [T, 2 * H])
        qkn2 = sb("qkn2", [T, 2 * H, DH])
        stack2 = sb("stack2", [T, 2 * H, HALVES_COPIES, DH], F32R)
        k_st2 = sb("k_st2", [128, HP, T], F32R)
        q_bd2 = sb("q_bd2", [128, HP, 2, T], F32R)
        v_ones2 = sb("v_ones2", [T, H, 32])
        row_max2 = sb("row_max2", [T, H], BF16)
        probs2 = sb("probs2", [T, H, T])
        o_t2 = sb("o_t2", [128, 3, T])
        r_den2 = sb("r_den2", [T, H])
        o_n2 = sb("o_n2", [T, D])
        h2 = sb("h2", [T, GT, D])

        x3_t = sb("x3_t", [K1, 2, GT, T])
        x3_hi = sb("x3_hi", [K1, 2, GT, T], F32R)
        x3_lo = sb("x3_lo", [K1, 2, GT, T], F32R)
        g_max = sb("g_max", [T, GT])
        g_exp = sb("g_exp", [T, GT, EXPERTS])
        g_sum = sb("g_sum", [T, GT])
        g_rec = sb("g_rec", [T, GT])
        g_prob = sb("g_prob", [T, GT, EXPERTS])
        g_s = sb("g_s", [T, GT, EXPERTS])
        g_grp = sb("g_grp", [T, GT, 4])
        g_cmp = sb("g_cmp", [T, GT, 64])
        g_eq = sb("g_eq", [T, GT, 64])
        g_rank = sb("g_rank", [T, GT, EXPERTS])
        g_keep = sb("g_keep", [T, GT, EXPERTS])
        combine = sb("combine", [T, GT, EX])
        combine_t = sb("combine_t", [EX, GC])
        g_t = sb("g_t", [128, CH, GC])
        w_up_part = g_t[0:K1, :, :].rearrange("p c s -> p (c s)")[:, 0:PART]
        h1_even, h1_odd, x_gate, th = (
            patches_or_rows[:, n * 2 * GC:(n + 1) * 2 * GC].rearrange("p (r s) -> p r s", r=2) for n in range(4))
        h_odd = patches_t_flat[:, 0:GC]
        y_sb = patches_t_flat[:, GC:GC + GT * D].rearrange("p (u d) -> p u d", u=GT)

        s_const = sem("s_const")
        s_w_part = sem("s_w_part")
        s_w_split = sem("s_w_split")
        s_setup_v = sem("s_setup_v")
        s_setup_p = sem("s_setup_p")
        s_setup_a = sem("s_setup_a")
        s_patches = [sem("s_patches0"), sem("s_patches1")]
        s_pt_ps = sem("s_pt_ps")
        s_pt_a = sem("s_pt_a")
        s_pt_v = sem("s_pt_v")
        s_emb_ps = sem("s_emb_ps")
        s_v = sem("s_v")
        s_a = sem("s_a")
        s_ln1_ps = sem("s_ln1_ps")
        s_part = sem("s_part")
        s_xn = sem("s_xn")
        s_xt_ps = sem("s_xt_ps")
        s_xt = sem("s_xt")
        s_qkv_ps = sem("s_qkv_ps")
        s_qk = sem("s_qk")
        s_vo = sem("s_vo")
        s_qkn = sem("s_qkn")
        s_hi = sem("s_hi")
        s_lo = sem("s_lo")
        s_st_ps = sem("s_st_ps")
        s_k_st = sem("s_k_st")
        s_q_bd = sem("s_q_bd")
        s_sc_ps = sem("s_sc_ps")
        s_max = sem("s_max")
        s_sct_ps = sem("s_sct_ps")
        s_probs = sem("s_probs")
        s_pv = sem("s_pv")
        s_ot = sem("s_ot")
        s_otok_ps = sem("s_otok_ps")
        s_h1 = sem("s_h1")
        s_h1_stored = sem("s_h1_stored")
        s_h_in = [sem(f"s_h_in{u}") for u in range(GT)]
        s_xn2 = sem("s_xn2")
        s_xt2_ps = sem("s_xt2_ps")
        s_xt2 = sem("s_xt2")
        s_qkv2_ps = sem("s_qkv2_ps")
        s_qk2 = sem("s_qk2")
        s_v2 = sem("s_v2")
        s_qkn2 = sem("s_qkn2")
        s_hi2 = sem("s_hi2")
        s_lo2 = sem("s_lo2")
        s_st2_ps = sem("s_st2_ps")
        s_k_st2 = sem("s_k_st2")
        s_q_bd2 = sem("s_q_bd2")
        s_sc2_ps = sem("s_sc2_ps")
        s_max2 = sem("s_max2")
        s_sct2_ps = sem("s_sct2_ps")
        s_probs2 = sem("s_probs2")
        s_pv2 = sem("s_pv2")
        s_ot2 = sem("s_ot2")
        s_otok2_ps = sem("s_otok2_ps")
        s_on2 = sem("s_on2")
        s_ont_ps = sem("s_ont_ps")
        s_ont = sem("s_ont")
        s_proj_ps = sem("s_proj_ps")
        s_h2 = sem("s_h2")
        s_x3n = sem("s_x3n")
        s_x3t_ps = sem("s_x3t_ps")
        s_x3t = sem("s_x3t")
        s_x3_split = sem("s_x3_split")
        s_gate_ps = sem("s_gate_ps")
        s_gate_exp = sem("s_gate_exp")
        s_combine = sem("s_combine")
        s_ct_ps = sem("s_ct_ps")
        s_ct = sem("s_ct")
        s_c_ps = sem("s_c_ps")
        s_c = sem("s_c")
        s_up_ps = sem("s_up_ps")
        s_up_copy = sem("s_up_copy")
        s_up_read = sem("s_up_read")
        s_xg = sem("s_xg")
        s_th = sem("s_th")
        s_g = sem("s_g")
        s_down_ps = sem("s_down_ps")
        s_y = sem("s_y")
        s_stored = sem("s_stored")

        block = ctx.enter_context(nc.Block())

        CONSTS = [(ident_sb[:, :], ident), (embed_add[:, :, :], base), (pos_sb[:, :, :], pos),
                  (ln_w_sb[:, :, :], ln_w), (ln_b_sb[:, :, :], ln_b), (mean_w_sb[:, :, :], mean_w),
                  (keep_sb[:, :], keep), (tri4_sb[:, :, :], tri4), (tri8_sb[:, :, :], tri8),
                  (expand_sb[:, :, :], expand), (w_map_sb[:, :, :], w_map), (w_qkv1_sb[:, :, :], w_qkv1),
                  (w_qkv2_sb[:, :, :], w_qkv2), (logit_sb[:, :], logit), (w_out_sb[:, :, :], w_out),
                  (head_scale_sb[:, :], head_scale), (gate_w_sb[:, :, :], gate_w), (gate_b_sb[:, :], gate_b),
                  (w_down_sb[:, :, :], w_down), (b_down_sb[:, :], b_down)]
        CONST_LANDED = 16 * len(CONSTS)

        def patch_src(image):
            return x[bass.ds(image, 1), :, :].rearrange("a (b p) n -> p (a b) n", p=PB)

        def positions(array, tile):
            return array[:, bass.ds(tile * 2, 2), :].rearrange("i t d -> t i d")

        @block.sync
        def _(sp):
            for dst, src in CONSTS:
                sp.dma_start(dst, src).then_inc(s_const, 16)
            for u in range(2):
                sp.dma_start(patches[:, u, :, :], patch_src(u)).then_inc(s_patches[u], 16)
            for n in range(4):
                if n >= 1:
                    sp.wait_ge(s_w_split, 2 * n)
                sp.dma_start(w_up_part, w_up[:, n // 2, (n % 2) * PART:(n % 2) * PART + PART]).then_inc(s_w_part, 16)

            def store_h1(t):
                sp.wait_ge(s_h1, t + 1)
                sp.dma_start(h1_dram[bass.ds(t, 1), :, :].rearrange("a (b p) n -> p (a b) n", p=B),
                             h1[:, :, :]).then_inc(s_h1_stored, 16)

            with sp.Fori(0, IMAGES // 2 - 1) as i:
                for u in range(2):
                    sp.wait_ge(s_pt_ps, i * 6 + 3 * u + 3)
                    sp.dma_start(patches[:, u, :, :], patch_src(i * 2 + (2 + u))).then_inc(s_patches[u], 16)
                    store_h1(i * 2 + u)
            for u in range(2):
                store_h1(IMAGES - 2 + u)

            sp.wait_ge(s_h1_stored, 16 * IMAGES + 16)
            for u in range(GT):
                for e in range(2):
                    sp.dma_start(h_in[64 * e:64 * e + 64, u, :], h1_dram[:, 2 * u + e, :]).then_inc(s_h_in[u], 16)

            def store(i):
                sp.wait_ge(s_y, i + 2)
                for u in range(GT):
                    for e in range(2):
                        sp.dma_start(out[:, bass.ds(i * (2 * GT) + (2 * u + e), 1), :].rearrange("i t d -> i (t d)"),
                                     y_sb[64 * e:64 * e + 64, u, :]).then_inc(s_stored, 16)

            with sp.Fori(0, GROUPS - 1) as i:
                for u in range(GT):
                    sp.wait_ge(s_h2, i * GT + (u + 1))
                    for e in range(2):
                        sp.dma_start(h_in[64 * e:64 * e + 64, u, :],
                                     h1_dram[:, bass.ds(i * (2 * GT) + (2 * GT + 2 * u + e), 1), :].rearrange(
                                         "i t d -> i (t d)")).then_inc(s_h_in[u], 16)
                store(i)
            store(GROUPS - 1)
            sp.wait_ge(s_stored, 32 * GT * (GROUPS + 1))

        @block.tensor
        def _(pe):
            pe.wait_ge(s_const, CONST_LANDED)
            pe.wait_ge(s_setup_v, 1)
            pe.wait_ge(s_setup_p, 1)

            def image(t, patches_landed, u):
                pe.wait_ge(s_patches[u], patches_landed)
                for n in range(3):
                    for c in (2 * n, 2 * n + 1):
                        for b in range(2):
                            at = (c % 2) * PATCHES + b * PB
                            last = pe.transpose(bank[n][:, at:at + PB],
                                                patches[:, u, b, c * 128:c * 128 + 128], ident_sb[0:PB, 0:PB])
                    last.then_inc(s_pt_ps, 1)

                pe.wait_ge(s_pt_a, t * 2 + 2)
                pe.wait_ge(s_pt_v, t + 1)
                for b in range(2):
                    for c in range(PC):
                        last = pe.matmul(bank[3][0:B, b * D:b * D + D], patches_t[:, c, b * B:b * B + B],
                                         w_map_sb[:, c, :], start=(b == 0 and c == 0), stop=(c == PC - 1),
                                         skip_group_check=True)
                last.then_inc(s_emb_ps, 1)

                for n, col in enumerate((mv[:, :, 0], var[:, :])):
                    pe.wait_ge(s_part, t * 2 + (n + 1))
                    for b in range(2):
                        last = pe.matmul(bank[4][0:B, n:n + 1], mean_w_sb[:, b, :], col[:, b:b + 1],
                                         start=(b == 0), stop=(b == 1))
                    last.then_inc(s_ln1_ps, 1)

                pe.wait_ge(s_xn, t + 1)
                for half in range(2):
                    for b in range(2):
                        last = pe.transpose(bank[5][0:HALF, half * SEQ + b * B:half * SEQ + b * B + B],
                                            xn[:, b, half * HALF:half * HALF + HALF], ident_sb[0:B, 0:B])
                last.then_inc(s_xt_ps, 1)

                pe.wait_ge(s_xt, t * 2 + 2)
                for b in range(2):
                    for half in range(2):
                        x_blk = x_t[:, half, b * B:b * B + B]
                        qk_out = bank[2 * b][0:B, 0:2 * D].rearrange("p (s n) -> p s n", s=2)[
                            :, :, half * HALF:half * HALF + HALF]
                        pe.matmul(qk_out, x_blk, w_qkv1_sb[:, half, 0:2 * HALF].rearrange("p (s n) -> p s n", s=2),
                                  start=(half == 0), stop=True, skip_group_check=True)
                        last = pe.matmul(bank[2 * b + 1][0:B, half * HALF:half * HALF + HALF], x_blk,
                                         w_qkv1_sb[:, half, 2 * HALF:3 * HALF],
                                         start=(half == 0), stop=True, skip_group_check=True)
                    last.then_inc(s_qkv_ps, 1)

                pe.wait_ge(s_hi, t * 4 + 4)
                pe.wait_ge(s_lo, t * 4 + 4)
                for n in range(2 * HP):
                    p, q_side = n // 2, n % 2
                    head = 2 * p + (0 if q_side else H)
                    if n >= 4:
                        pe.wait_ge(s_q_bd if q_side else s_k_st, t * HP + ((n - 4) // 2 + 1))
                    for b in range(2):
                        last = pe.transpose(bank[4 + n % 4][:, b * B:b * B + B],
                                            stack[:, b, head:head + 2, :, :].bitcast(F32).rearrange(
                                                "p h c d -> p (h c d)"), ident_sb[0:B, 0:B])
                    last.then_inc(s_st_ps, 1)

                for n in range(2 * HP):
                    p, b = n // 2, n % 2
                    pe.wait_ge(s_k_st, t * HP + (p + 1))
                    pe.wait_ge(s_q_bd, t * HP + (p + 1))
                    if n >= 3:
                        pe.wait_ge(s_max, t * (2 * HP) + (n - 2))
                    for e in range(2):
                        last = pe.matmul(bank[n % 3][0:B, e * SEQ:e * SEQ + SEQ], q_bd[:, p, e, b * B:b * B + B],
                                         k_st[:, p, :], start=(e == 0), stop=True, skip_group_check=True)
                    last.then_inc(s_sc_ps, 1)

                pe.wait_ge(s_max, t * (2 * HP) + 2 * HP)
                o_bank = (3, 6, 7)

                def scores_t(n):
                    j, b, pp = n // 4, n // 2 % 2, n % 2
                    p = 2 * j + pp
                    if n >= 2:
                        pe.wait_ge(s_probs, t * 12 + (n - 1))
                    sc = bank[4 + n % 2]
                    pe.matmul(sc[0:B, 0:2 * SEQ], k_st[:, p, b * B:b * B + B],
                              q_bd[:, p, :, :].rearrange("p e s -> p (e s)"), start=True, stop=False,
                              skip_group_check=True)
                    for e in range(2):
                        for qb in range(2):
                            at = e * SEQ + qb * B
                            last = pe.matmul(sc[0:B, at:at + B],
                                             row_max[:, qb, 2 * p + e:2 * p + e + 1].broadcast_to([B, B]),
                                             neg_ident[0:B, 0:B], start=False, stop=True, skip_group_check=True)
                    last.then_inc(s_sct_ps, 1)

                def values(n):
                    j, b, pp = n // 4, n // 2 % 2, n % 2
                    pe.wait_ge(s_probs, t * 12 + (n + 1))
                    for e in range(2):
                        head = 4 * j + 2 * pp + e
                        row = 32 * (head % 4)
                        last = pe.matmul(bank[o_bank[j]][row:row + 32, 0:SEQ], v_ones[:, b, head, :],
                                         probs[:, n % 2, e * SEQ:e * SEQ + SEQ], start=(b == 0), stop=(b == 1),
                                         skip_group_check=True)
                    last.then_inc(s_pv, 1)

                pe.wait_ge(s_vo, t * 2 + 2)
                scores_t(0)
                for n in range(12):
                    if n < 11:
                        scores_t(n + 1)
                    values(n)

                pe.wait_ge(s_ot, t * 3 + 3)
                for b in range(2):
                    for j in range(3):
                        last = pe.transpose(bank[4 + b][0:B, j * 128:j * 128 + 128], o_t[:, j, b * B:b * B + B],
                                            ident_sb[:, :])
                    last.then_inc(s_otok_ps, 1)

            def tile(i, u):
                t = i * GT + u

                pe.wait_ge(s_xn2, t + 1)
                for half in range(2):
                    last = pe.transpose(bank[5][0:HALF, half * T:half * T + T],
                                        xn2[:, half * HALF:half * HALF + HALF], ident_sb[:, :])
                last.then_inc(s_xt2_ps, 1)

                pe.wait_ge(s_xt2, t + 1)
                for half in range(2):
                    pe.matmul(bank[0][:, 0:2 * D], x_t2[:, half, :], w_qkv2_sb[:, half, 0:2 * D],
                              start=(half == 0), stop=(half == 1))
                    last = pe.matmul(bank[1][:, 0:D], x_t2[:, half, :], w_qkv2_sb[:, half, 2 * D:3 * D],
                                     start=(half == 0), stop=(half == 1))
                last.then_inc(s_qkv2_ps, 1)

                pe.wait_ge(s_hi2, t * 2 + 2)
                pe.wait_ge(s_lo2, t * 2 + 2)
                for side in range(2):
                    for p in range(HP):
                        head = 2 * p + (0 if side else H)
                        last = pe.transpose(bank[4 + 2 * side + p // 4][:, (p % 4) * T:(p % 4) * T + T],
                                            stack2[:, head:head + 2, :, :].bitcast(F32).rearrange(
                                                "p h c d -> p (h c d)"), ident_sb[:, :])
                    last.then_inc(s_st2_ps, 1)

                pe.wait_ge(s_k_st2, t * 2 + 2)
                pe.wait_ge(s_q_bd2, t + 1)
                for p in range(HP):
                    for e in range(2):
                        at = (2 * (p % 2) + e) * T
                        last = pe.matmul(bank[p // 2][:, at:at + T], q_bd2[:, p, e, :], k_st2[:, p, :],
                                         start=(p % 2 == 0 and e == 0), stop=True, skip_group_check=True)
                    if p % 2 == 1:
                        last.then_inc(s_sc2_ps, 1)

                pe.wait_ge(s_max2, t * 3 + 3)
                for n in range(3):
                    for p in (2 * n, 2 * n + 1):
                        at = (p % 2) * 2 * T
                        pe.matmul(bank[4 + n][:, at:at + 2 * T], k_st2[:, p, :],
                                  q_bd2[:, p, :, :].rearrange("p e s -> p (e s)"), start=(p % 2 == 0), stop=False,
                                  skip_group_check=True)
                    for e in range(4):
                        head = 4 * n + e
                        last = pe.matmul(bank[4 + n][:, e * T:e * T + T],
                                         row_max2[:, head:head + 1].broadcast_to([T, T]), neg_ident[:, :],
                                         start=False, stop=True, skip_group_check=True)
                    last.then_inc(s_sct2_ps, 1)

                pe.wait_ge(s_v2, t + 1)
                for n in range(3):
                    pe.wait_ge(s_probs2, t * 3 + (n + 1))
                    for e in range(4):
                        last = pe.matmul(bank[3][32 * e:32 * e + 32, n * T:n * T + T], v_ones2[:, 4 * n + e, :],
                                         probs2[:, 4 * n + e, :], start=True, stop=True, skip_group_check=True)
                last.then_inc(s_pv2, 1)

                pe.wait_ge(s_ot2, t + 1)
                for j in range(3):
                    last = pe.transpose(bank[7][:, j * 128:j * 128 + 128], o_t2[:, j, :], ident_sb[:, :])
                last.then_inc(s_otok2_ps, 1)

                pe.wait_ge(s_on2, t + 1)
                for half in range(2):
                    last = pe.transpose(bank[5][0:HALF, half * T:half * T + T],
                                        o_n2[:, half * HALF:half * HALF + HALF], ident_sb[:, :])
                last.then_inc(s_ont_ps, 1)
                pe.wait_ge(s_ont, t + 1)
                for half in range(2):
                    last = pe.matmul(bank[0][:, 0:D], x_t2[:, half, :], w_out_scaled[:, half, :],
                                     start=(half == 0), stop=(half == 1))
                last.then_inc(s_proj_ps, 1)

                pe.wait_ge(s_x3n, t + 1)
                for half in range(2):
                    last = pe.transpose(bank[1][0:HALF, half * T:half * T + T],
                                        xn3[:, half * HALF:half * HALF + HALF], ident_sb[:, :])
                last.then_inc(s_x3t_ps, 1)

            def experts(i):
                pe.wait_ge(s_x3t, i * GT + GT)
                for u in range(GT):
                    for half in range(2):
                        last = pe.matmul(bank[4][:, u * EXPERTS:u * EXPERTS + EXPERTS],
                                         x3_t[:, half, u, :], gate_w_sb[:, half, :],
                                         start=(u == 0 and half == 0), stop=(half == 1), skip_group_check=True)
                last.then_inc(s_gate_ps, 1)

                pe.wait_ge(s_combine, i + 1)
                for u in range(GT):
                    last = pe.transpose(bank[6][0:EX, u * T:u * T + T], combine[:, u, :], ident_sb[:, :])
                last.then_inc(s_ct_ps, 1)
                pe.wait_ge(s_ct, i + 1)
                for j in range(CH):
                    if j >= 2:
                        pe.wait_ge(s_c, i * CH + (j - 1))
                    pe.matmul(bank[(5, 7)[j % 2]][:, 0:GC], expand_sb[:, j, :], combine_t[:, :],
                              start=True, stop=True).then_inc(s_c_ps, 1)

                pe.wait_ge(s_x3_split, i * 2 + 2)
                pe.wait_ge(s_c, i * CH + CH)
                xh = [x3_hi[:, half, :, :].rearrange("p u s -> p (u s)") for half in range(2)]
                xl = [x3_lo[:, half, :, :].rearrange("p u s -> p (u s)") for half in range(2)]
                for j in range(CH):
                    m = chunk_rows(j)
                    if j >= 2:
                        pe.wait_ge(s_up_read, i * CH + (j - 1))
                    for kind in range(KINDS):
                        at = kind * ROWS + 128 * j
                        dst = bank[4 * (j % 2) + kind][0:m, 0:GC]
                        for half in range(2):
                            pe.matmul(dst, w_up_hi[:, half, at:at + m], xh[half], start=(half == 0), stop=False)
                            pe.matmul(dst, w_up_hi[:, half, at:at + m], xl[half], start=False, stop=False)
                            last = pe.matmul(dst, w_up_lo[:, half, at:at + m], xh[half],
                                             start=False, stop=(half == 1))
                    last.then_inc(s_up_ps, 1)

                pe.wait_ge(s_up_read, i * CH + CH)
                pe.wait_ge(s_g, i * CH + CH)
                for u in range(GT):
                    dst = bank[u // 2][:, (u % 2) * D:(u % 2) * D + D]
                    for j in range(CH):
                        m = chunk_rows(j)
                        pe.matmul(dst, g_t[0:m, j, u * T:u * T + T], w_down_sb[0:m, j, :],
                                  start=(u % 2 == 0 and j == 0), stop=False, skip_group_check=True)
                    last = pe.matmul(dst, combine_t[:, u * T:u * T + T], b_down_sb[:, :], start=False, stop=True,
                                     skip_group_check=True)
                last.then_inc(s_down_ps, 1)

            with pe.Fori(0, IMAGES // 2) as i:
                for u in range(2):
                    image(i * 2 + u, i * 16 + 16, u)
            with pe.Fori(0, GROUPS) as i:
                pe.wait_ge(s_y, i + 1)
                for u in range(GT):
                    tile(i, u)
                experts(i)

        @block.scalar
        def _(act):
            act.wait_ge(s_const, CONST_LANDED)
            act.wait_ge(s_setup_v, 1)
            act.activation(logit_scale[:, :], logit_sb[:, :], ACT.Exp).then_inc(s_setup_a, 1)

            def image(t):
                for n in (0, 2):
                    act.wait_ge(s_pt_ps, t * 3 + (n + 1))
                    act.activation(patches_t[:, 2 * n:2 * n + 2, 2:SEQ], bank[n][:, 0:2 * PATCHES].rearrange(
                        "p (c s) -> p c s", c=2), ACT.Copy).then_inc(s_pt_a, 1)

                act.wait_ge(s_xt_ps, t + 1)
                src = bank[5][0:HALF, 0:2 * SEQ].rearrange("p (h s) -> p h s", h=2)
                act.activation(x_t[0:HALF, :, 1:SEQ], src[:, :, 1:SEQ], ACT.Copy).then_inc(s_xt, 1)
                act.activation(x_t[0:HALF, :, 0:1], src[:, :, 1:2], ACT.Copy).then_inc(s_xt, 1)

                for b in range(2):
                    act.wait_ge(s_qkv_ps, t * 2 + (b + 1))
                    src = bank[2 * b][0:B, 0:2 * D]
                    flat = qkn[:, b, :, :].rearrange("p h d -> p (h d)")
                    act.activation(flat[:, 0:D], src[:, 0:D], ACT.Copy, scale=DH ** -0.5).then_inc(s_qk, 1)
                    act.activation(flat[:, D:2 * D], src[:, D:2 * D], ACT.Copy).then_inc(s_qk, 1)

                act.wait_ge(s_qk, t * 4 + 4)
                for b in range(2):
                    for side, rows in enumerate((slice(0, 2), slice(0, 4, 2))):
                        heads = slice(side * H, side * H + H)
                        src = qkn[:, b, heads, :][:, :, None, :].broadcast_to([B, H, 2, DH])
                        act.activation(stack[:, b, heads, rows, :], src, ACT.Copy).then_inc(s_hi, 1)

                for p in range(HP):
                    act.wait_ge(s_st_ps, t * (2 * HP) + (2 * p + 1))
                    act.activation(k_st[:, p, :], bank[4 + (2 * p) % 4][:, 0:SEQ], ACT.Copy).then_inc(s_k_st, 1)

                for n in range(12):
                    act.wait_ge(s_sct_ps, t * 12 + (n + 1))
                    if n >= 2:
                        act.wait_ge(s_pv, t * 12 + (n - 1))
                    act.activation(probs[:, n % 2, :], bank[4 + n % 2][0:B, 0:2 * SEQ], ACT.Exp)\
                        .then_inc(s_probs, 1)

                act.wait_ge(s_pv, t * 12 + 12)
                for j in range(3):
                    act.activation(o_t[:, j, :], bank[(3, 6, 7)[j]][:, 0:SEQ], ACT.Copy).then_inc(s_ot, 1)

            def copy_halves(dst, src_bank):
                return act.activation(dst, src_bank[0:HALF, 0:2 * T].rearrange("p (h s) -> p h s", h=2), ACT.Copy)

            def tile(i, u):
                t = i * GT + u
                act.wait_ge(s_xt2_ps, t + 1)
                copy_halves(x_t2[0:HALF, :, :], bank[5]).then_inc(s_xt2, 1)

                act.wait_ge(s_qkv2_ps, t + 1)
                act.activation(qk2[:, :, :].rearrange("p h d -> p (h d)"), bank[0][:, 0:2 * D], ACT.Copy)\
                    .then_inc(s_qk2, 1)

                act.wait_ge(s_qkn2, t + 1)
                for side, rows in enumerate((slice(0, 2), slice(0, 4, 2))):
                    heads = slice(side * H, side * H + H)
                    src = qkn2[:, heads, :][:, :, None, :].broadcast_to([T, H, 2, DH])
                    act.activation(stack2[:, heads, rows, :], src, ACT.Copy).then_inc(s_hi2, 1)

                act.wait_ge(s_st2_ps, t * 2 + 1)
                act.activation(k_st2[:, 0:4, :].rearrange("p h s -> p (h s)"), bank[4][:, 0:4 * T], ACT.Copy)\
                    .then_inc(s_k_st2, 1)
                act.activation(k_st2[:, 4:6, :].rearrange("p h s -> p (h s)"), bank[5][:, 0:2 * T], ACT.Copy)\
                    .then_inc(s_k_st2, 1)

                for n in range(3):
                    act.wait_ge(s_sct2_ps, t * 3 + (n + 1))
                    for e in range(2):
                        own = slice(64 * e, 64 * e + 64)
                        last = act.activation(probs2[own, 4 * n:4 * n + 4, own],
                                              bank[4 + n][own, :].rearrange("p (h s) -> p h s", h=4)[:, :, own],
                                              ACT.Exp)
                    last.then_inc(s_probs2, 1)

                act.wait_ge(s_pv2, t + 1)
                act.activation(o_t2[:, :, :].rearrange("p j s -> p (j s)"), bank[3][:, 0:3 * T], ACT.Copy)\
                    .then_inc(s_ot2, 1)

                act.wait_ge(s_ont_ps, t + 1)
                copy_halves(x_t2[0:HALF, :, :], bank[5]).then_inc(s_ont, 1)

                act.wait_ge(s_x3t_ps, t + 1)
                copy_halves(x3_t[0:HALF, :, u, :], bank[1]).then_inc(s_x3t, 1)

            with act.Fori(0, IMAGES // 2) as i:
                for u in range(2):
                    image(i * 2 + u)
            with act.Fori(0, GROUPS) as i:
                for u in range(GT):
                    tile(i, u)

                act.wait_ge(s_x3t, i * GT + GT)
                act.activation(x3_hi[:, :, :, :].rearrange("p h u s -> p (h u s)"),
                               x3_t[:, :, :, :].rearrange("p h u s -> p (h u s)"), ACT.Copy)\
                    .then_inc(s_x3_split, 1)

                act.wait_ge(s_gate_exp, i * 2 + 1)
                act.activation(g_exp[:, :, :], g_s[:, :, :], ACT.Exp).then_inc(s_gate_exp, 1)

                act.wait_ge(s_ct_ps, i + 1)
                act.activation(combine_t[:, :], bank[6][0:EX, 0:GC], ACT.Copy).then_inc(s_ct, 1)
                for j in range(CH):
                    act.wait_ge(s_c_ps, i * CH + (j + 1))
                    act.activation(g_t[:, j, :], bank[(5, 7)[j % 2]][:, 0:GC], ACT.Copy).then_inc(s_c, 1)

                def tanh(j):
                    m = chunk_rows(j)
                    act.wait_ge(s_xg, i * CH + (j + 1))
                    act.activation(th[0:m, j % 2, :], x_gate[0:m, j % 2, :], ACT.Tanh, scale=ALPHA / 2)\
                        .then_inc(s_th, 1)

                for j in range(CH):
                    m = chunk_rows(j)
                    act.wait_ge(s_up_ps, i * CH + (j + 1))
                    if j >= 2:
                        act.wait_ge(s_up_read, i * CH + (j - 1))
                    act.activation(h1_even[0:m, j % 2, :], bank[4 * (j % 2)][0:m, 0:GC], ACT.Copy)\
                        .then_inc(s_up_copy, 1)
                    act.activation(h1_odd[0:m, j % 2, :], bank[4 * (j % 2) + 2][0:m, 0:GC], ACT.Copy)\
                        .then_inc(s_up_copy, 1)
                    if j >= 1:
                        tanh(j - 1)
                tanh(CH - 1)

        @block.gpsimd
        def _(pool):
            pool.memset(v_ones[:, :, :, :].rearrange("p b h d -> p (b h d)"), 1.0).then_inc(s_setup_p, 1)
            pool.memset(v_ones2[:, :, :].rearrange("p h d -> p (h d)"), 1.0).then_inc(s_setup_p, 1)
            pool.memset(probs2[:, :, :].rearrange("p h s -> p (h s)"), 0.0).then_inc(s_setup_p, 1)
            pool.wait_ge(s_setup_p, 3)
            pool.memset(v_ones[0:1, 0, :, :], 0.0).then_inc(s_setup_p, 1)

        @block.vector
        def _(dve):
            steps = [0]

            dve.memset(q_bd[:, :, :, :].rearrange("p h e s -> p (h e s)").bitcast(F32), 0.0)
            dve.memset(q_bd2[:, :, :, :].rearrange("p h e s -> p (h e s)").bitcast(F32), 0.0)
            dve.memset(patches_t[:, :, 0:2], 0.0)
            dve.memset(x_t[HALF:K1, :, :], 1.0)
            dve.memset(x_t2[HALF:K1, :, :], 1.0)
            dve.memset(x3_t[HALF:K1, :, :, :], 1.0)
            dve.memset(combine[:, :, EXPERTS:EX], 1.0)
            dve.wait_ge(s_const, CONST_LANDED)
            dve.tensor_scalar(neg_ident[:, :], ident_sb[:, :], -1.0, None, ALU.mult)
            for half in range(2):
                dve.tensor_scalar(w_out_scaled[:, half, :], w_out_sb[:, half, :], head_scale_sb[:, half:half + 1],
                                  None, ALU.mult)
            dve.tensor_tensor(embed_add[:, :, :], embed_add[:, :, :], pos_sb[:, :, :], ALU.add)
            dve.tensor_scalar(logit_sb[:, :], logit_sb[:, :], SCALE_MAX, None, ALU.min).then_inc(s_v, 1)
            for n in range(4):
                hi, lo = (w[:, n // 2, (n % 2) * PART:(n % 2) * PART + PART] for w in (w_up_hi, w_up_lo))
                dve.wait_ge(s_w_part, 16 * n + 16)
                dve.tensor_copy(hi, w_up_part).then_inc(s_w_split, 1)
                dve.wait_ge(s_w_split, 2 * n + 1)
                dve.tensor_tensor(lo, w_up_part, hi, ALU.subtract).then_inc(s_w_split, 1)
            dve.wait_ge(s_w_split, 8)
            dve.wait_ge(s_setup_p, 4)
            dve.sem_inc(s_y, 1)
            dve.sem_inc(s_stored, 32 * GT)
            dve.sem_inc(s_h1_stored, 16)
            dve.sem_inc(s_setup_v, 1)
            dve.wait_ge(s_setup_a, 1)

            base = [1]

            def link(ins):
                steps[0] += 1
                ins.then_inc(s_v, 1)
                dve.wait_ge(s_v, base[0] + steps[0])

            def rsqrt(y, v, w):
                link(dve.tensor_scalar(y.bitcast(I32), v.bitcast(I32), -0.5, RSQRT_GUESS, ALU.mult, ALU.add))
                for _ in range(NEWTON):
                    link(dve.scalar_tensor_tensor(out=w, in0=y, scalar=-0.5, in1=y, op0=ALU.mult, op1=ALU.mult))
                    link(dve.tensor_tensor(w, w, v, ALU.mult))
                    link(dve.scalar_tensor_tensor(out=y, in0=w, scalar=1.5, in1=y, op0=ALU.add, op1=ALU.mult))

            def low_parts(dst, src, rows, sem_hi, count, sem_lo):
                for side, (hi, lo) in enumerate(((slice(0, 2), slice(2, 4)), (slice(0, 4, 2), slice(1, 4, 2)))):
                    heads = slice(side * H, side * H + H)
                    dve.wait_ge(sem_hi, count + (side + 1))
                    dve.tensor_tensor(dst[:, heads, lo, :],
                                      src[:, heads, :][:, :, None, :].broadcast_to([rows, H, 2, DH]),
                                      dst[:, heads, hi, :], ALU.subtract).then_inc(sem_lo, 1)

            def image(t):
                dve.wait_ge(s_pt_ps, t * 3 + 2)
                dve.tensor_copy(patches_t[:, 2:4, 2:SEQ], bank[1][:, 0:2 * PATCHES].rearrange(
                    "p (c s) -> p c s", c=2)).then_inc(s_pt_v, 1)

                dve.wait_ge(s_emb_ps, t + 1)
                link(dve.tensor_tensor(tok[:, :, :].rearrange("p b d -> p (b d)"), bank[3][0:B, 0:2 * D],
                                       embed_add[:, :, :].rearrange("p b d -> p (b d)"), ALU.add))

                for b in range(2):
                    link(dve.bn_stats(stats[:, b, :], tok[:, b, :]))
                dve.memset(veps[:, 1:2], EPS)
                for b in range(2):
                    ins = dve.bn_aggr(mv[:, b, :], stats[:, b, :])
                ins.then_inc(s_part, 1)
                dve.wait_ge(s_ln1_ps, t * 2 + 1)
                link(dve.tensor_copy(veps[:, 0:1], bank[4][0:B, 0:1]))
                link(dve.tensor_scalar(dev[:, :], mv[:, :, 0], veps[:, 0:1], None, ALU.subtract))
                link(dve.tensor_tensor(dev[:, :], dev[:, :], dev[:, :], ALU.mult))
                dve.tensor_tensor(var[:, :], dev[:, :], mv[:, :, 1], ALU.add).then_inc(s_part, 1)
                dve.wait_ge(s_ln1_ps, t * 2 + 2)
                link(dve.tensor_tensor(veps[:, 1:2], bank[4][0:B, 1:2], veps[:, 1:2], ALU.add))
                rsqrt(rstd[:, 0:1], veps[:, 1:2], half_y[:, 0:1])
                link(dve.tensor_scalar(xn[:, :, :], tok[:, :, :], veps[:, 0:1], rstd[:, 0:1],
                                       ALU.subtract, ALU.mult))
                link(dve.tensor_tensor(xn[:, :, :], xn[:, :, :], ln_w_sb[:, :, :], ALU.mult))
                dve.tensor_tensor(xn[:, :, :], xn[:, :, :], ln_b_sb[:, :, :], ALU.add).then_inc(s_xn, 1)

                for b in range(2):
                    dve.wait_ge(s_qkv_ps, t * 2 + (b + 1))
                    dve.tensor_scalar(v_ones[:, b, :, 0:DH], bank[2 * b + 1][0:B, 0:D].rearrange(
                        "p (h d) -> p h d", h=H), keep_sb[:, b:b + 1], None, ALU.mult).then_inc(s_vo, 1)

                dve.wait_ge(s_qk, t * 4 + 4)
                for b in range(2):
                    low_parts(stack[:, b, :, :, :], qkn[:, b, :, :], B, s_hi, t * 4 + 2 * b, s_lo)

                for p in range(HP):
                    dve.wait_ge(s_st_ps, t * (2 * HP) + (2 * p + 2))
                    src = bank[4 + (2 * p + 1) % 4]
                    dve.tensor_copy(q_bd[0:64, p, 0, :], src[0:64, 0:SEQ])
                    dve.tensor_copy(q_bd[64:128, p, 1, :], src[64:128, 0:SEQ]).then_inc(s_q_bd, 1)

                for n in range(2 * HP):
                    p, b = n // 2, n % 2
                    dve.wait_ge(s_sc_ps, t * (2 * HP) + (n + 1))
                    dve.tensor_reduce(row_max[:, b, 2 * p:2 * p + 2], bank[n % 3][0:B, 0:2 * SEQ].rearrange(
                        "p (e s) -> p e s", e=2), AX.X, ALU.max).then_inc(s_max, 1)

                for b in range(2):
                    dve.wait_ge(s_otok_ps, t * 2 + (b + 1))
                    src = bank[4 + b][0:B, 0:3 * 128].rearrange("p (h d) -> p h d", h=H)
                    link(dve.reciprocal(r_den[:, b, :], src[:, :, DH]))
                    link(dve.tensor_tensor(o_n[:, b, :].rearrange("p (h d) -> p h d", h=H), src[:, :, 0:DH],
                                           r_den[:, b, :][:, :, None].broadcast_to([B, H, DH]), ALU.mult))

                dve.wait_ge(s_h1_stored, t * 16 + 16)
                for b in range(2):
                    last = dve.scalar_tensor_tensor(out=h1[:, b, :], in0=o_n[:, b, :], scalar=keep_sb[:, b:b + 1],
                                                    in1=tok[:, b, :], op0=ALU.mult, op1=ALU.add)
                last.then_inc(s_h1, 1)

            def layer_norm(dst, h, done):
                link(dve.bn_stats(stats2[:, :], h))
                dve.memset(veps2[:, :], EPS)
                link(dve.bn_aggr(mv2[:, :], stats2[:, :]))
                link(dve.tensor_tensor(veps2[:, :], mv2[:, 1:2], veps2[:, :], ALU.add))
                rsqrt(rstd2[:, :], veps2[:, :], half_y2[:, 0:1])
                dve.tensor_scalar(dst[:, :], h, mv2[:, 0:1], rstd2[:, 0:1], ALU.subtract, ALU.mult).then_inc(done, 1)

            def tile(i, u):
                t = i * GT + u
                dve.wait_ge(s_h_in[u], i * 32 + 32)
                layer_norm(xn2, h_in[:, u, :], s_xn2)

                dve.wait_ge(s_qkv2_ps, t + 1)
                dve.tensor_copy(v_ones2[:, :, 0:DH], bank[1][:, 0:D].rearrange("p (h d) -> p h d", h=H))\
                    .then_inc(s_v2, 1)

                dve.wait_ge(s_qk2, t + 1)
                link(dve.tensor_tensor(qk_sq[:, :, :], qk2[:, :, :], qk2[:, :, :], ALU.mult))
                link(dve.tensor_reduce(norm2[:, :], qk_sq[:, :, :], AX.X, ALU.add))
                link(dve.tensor_scalar(norm2[:, :], norm2[:, :], NORM_EPS ** 2, None, ALU.max))
                rsqrt(rnorm[:, :], norm2[:, :], half_y2[:, :])
                link(dve.tensor_tensor(rnorm[:, 0:H], rnorm[:, 0:H], logit_scale[:, :], ALU.mult))
                dve.tensor_tensor(qkn2[:, :, :], qk2[:, :, :], rnorm[:, :][:, :, None].broadcast_to([T, 2 * H, DH]),
                                  ALU.mult).then_inc(s_qkn2, 1)
                dve.wait_ge(s_qkn2, t + 1)
                low_parts(stack2, qkn2, T, s_hi2, t * 2, s_lo2)

                dve.wait_ge(s_st2_ps, t * 2 + 2)
                for first, n in ((0, 4), (4, 2)):
                    src = bank[6 + first // 4][:, 0:n * T].rearrange("p (h s) -> p h s", h=n)
                    for e in range(2):
                        own = slice(64 * e, 64 * e + 64)
                        last = dve.tensor_copy(q_bd2[own, first:first + n, e, :], src[own, :, :])
                last.then_inc(s_q_bd2, 1)

                for n in range(3):
                    dve.wait_ge(s_sc2_ps, t * 3 + (n + 1))
                    for e in range(2):
                        own = slice(64 * e, 64 * e + 64)
                        last = dve.tensor_reduce(row_max2[own, 4 * n:4 * n + 4], bank[n][own, :].rearrange(
                            "p (h s) -> p h s", h=4)[:, :, own], AX.X, ALU.max)
                    last.then_inc(s_max2, 1)

                dve.wait_ge(s_otok2_ps, t + 1)
                src = bank[7][:, 0:3 * 128].rearrange("p (h d) -> p h d", h=H)
                link(dve.reciprocal(r_den2[:, :], src[:, :, DH]))
                dve.tensor_tensor(o_n2[:, :].rearrange("p (h d) -> p h d", h=H), src[:, :, 0:DH],
                                  r_den2[:, :][:, :, None].broadcast_to([T, H, DH]), ALU.mult).then_inc(s_on2, 1)

                dve.wait_ge(s_proj_ps, t + 1)
                dve.tensor_tensor(h2[:, u, :], bank[0][:, 0:D], h_in[:, u, :], ALU.add).then_inc(s_h2, 1)
                dve.wait_ge(s_h2, t + 1)
                layer_norm(xn3, h2[:, u, :], s_x3n)

            def experts(i):
                dve.wait_ge(s_x3_split, i * 2 + 1)
                dve.tensor_tensor(x3_lo[:, :, :, :].rearrange("p h u s -> p (h u s)"),
                                  x3_t[:, :, :, :].rearrange("p h u s -> p (h u s)"),
                                  x3_hi[:, :, :, :].rearrange("p h u s -> p (h u s)"), ALU.subtract)\
                    .then_inc(s_x3_split, 1)

                def spread(ap, n):
                    return ap[:, :, None].broadcast_to([T, GT, n])

                dve.wait_ge(s_gate_ps, i + 1)
                logits = bank[4][:, 0:GT * EXPERTS].rearrange("p (n e) -> p n e", n=GT)
                link(dve.tensor_reduce(g_max[:, :], logits, AX.X, ALU.max))
                dve.tensor_tensor(g_s[:, :, :], logits, spread(g_max[:, :], EXPERTS), ALU.subtract)\
                    .then_inc(s_gate_exp, 1)
                dve.wait_ge(s_gate_exp, i * 2 + 2)
                link(dve.tensor_reduce(g_sum[:, :], g_exp[:, :, :], AX.X, ALU.add))
                link(dve.reciprocal(g_rec[:, :], g_sum[:, :]))
                link(dve.tensor_tensor(g_prob[:, :, :], g_exp[:, :, :], spread(g_rec[:, :], EXPERTS), ALU.mult))
                link(dve.tensor_tensor(g_s[:, :, :], g_prob[:, :, :],
                                       gate_b_sb[:, None, :].broadcast_to([T, GT, EXPERTS]), ALU.add))

                def top2(values, tri, n, keep):
                    cmp = g_cmp[:, :, 0:n * n].rearrange("p r (a c) -> p r a c", a=n)
                    eq = g_eq[:, :, 0:n * n].rearrange("p r (a c) -> p r a c", a=n)
                    for r in range(GT):
                        other = values[:, r, :][:, None, :].broadcast_to([T, n, n])
                        own = values[:, r, :][:, :, None].broadcast_to([T, n, n])
                        dve.tensor_tensor(cmp[:, r, :, :], other, own, ALU.is_gt)
                        last = dve.tensor_tensor(eq[:, r, :, :], other, own, ALU.is_equal)
                    link(last)
                    for r in range(GT):
                        last = dve.tensor_tensor(eq[:, r, :, :], eq[:, r, :, :], tri, ALU.mult)
                    link(last)
                    link(dve.tensor_tensor(g_cmp[:, :, 0:n * n], g_cmp[:, :, 0:n * n], g_eq[:, :, 0:n * n], ALU.add))
                    link(dve.tensor_reduce(g_rank[:, :, 0:n], cmp, AX.X, ALU.add))
                    link(dve.tensor_scalar(keep, g_rank[:, :, 0:n], 1.5, None, ALU.is_lt))

                pairs = g_s[:, :, :].rearrange("p n (g e) -> p n g e", e=2)
                link(dve.tensor_tensor(g_grp[:, :, :], pairs[:, :, :, 0], pairs[:, :, :, 1], ALU.add))
                top2(g_grp, tri4_sb[:, :, :], 4, g_grp[:, :, :])
                kept = g_keep[:, :, :].rearrange("p n (g e) -> p n g e", e=2)
                for e in range(2):
                    last = dve.tensor_copy(kept[:, :, :, e], g_grp[:, :, :])
                link(last)
                link(dve.tensor_tensor(g_s[:, :, :], g_s[:, :, :], g_keep[:, :, :], ALU.mult))
                link(dve.tensor_scalar(g_keep[:, :, :], g_keep[:, :, :], BIG, -BIG, ALU.mult, ALU.add))
                link(dve.tensor_tensor(g_s[:, :, :], g_s[:, :, :], g_keep[:, :, :], ALU.add))
                top2(g_s, tri8_sb[:, :, :], EXPERTS, g_keep[:, :, :])
                dve.tensor_tensor(combine[:, :, 0:EXPERTS], g_prob[:, :, :], g_keep[:, :, :], ALU.mult)\
                    .then_inc(s_combine, 1)

                for j in range(CH):
                    m = chunk_rows(j)
                    xg = x_gate[0:m, j % 2, :]
                    lin = h_odd[0:m, :]
                    dve.wait_ge(s_up_copy, i * (2 * CH) + (2 * j + 2))
                    dve.tensor_tensor(xg, h1_even[0:m, j % 2, :], bank[4 * (j % 2) + 1][0:m, 0:GC], ALU.mult)
                    dve.tensor_tensor(lin, h1_odd[0:m, j % 2, :], bank[4 * (j % 2) + 3][0:m, 0:GC], ALU.mult)\
                        .then_inc(s_up_read, 1)
                    dve.wait_ge(s_up_read, i * CH + (j + 1))
                    dve.tensor_scalar(xg, xg, LIMIT, None, ALU.min).then_inc(s_xg, 1)
                    link(dve.tensor_scalar(lin, lin, 1.0, 1.0 - LIMIT, ALU.add, ALU.max))
                    link(dve.scalar_tensor_tensor(out=lin, in0=lin, scalar=1.0 + LIMIT, in1=xg,
                                                  op0=ALU.min, op1=ALU.mult))
                    dve.wait_ge(s_th, i * CH + (j + 1))
                    link(dve.scalar_tensor_tensor(out=lin, in0=th[0:m, j % 2, :], scalar=1.0, in1=lin,
                                                  op0=ALU.add, op1=ALU.mult))
                    dve.tensor_tensor(g_t[0:m, j, :], lin, g_t[0:m, j, :], ALU.mult).then_inc(s_g, 1)
                    dve.wait_ge(s_g, i * CH + (j + 1))

                dve.wait_ge(s_stored, i * (32 * GT) + 32 * GT)
                dve.wait_ge(s_down_ps, i + 1)
                dve.tensor_tensor(y_sb[:, 0:2, :].rearrange("p u d -> p (u d)"), bank[0][:, 0:2 * D],
                                  h2[:, 0:2, :].rearrange("p u d -> p (u d)"), ALU.add)
                dve.tensor_tensor(y_sb[:, 2, :], bank[1][:, 0:D], h2[:, 2, :], ALU.add).then_inc(s_y, 1)

            with dve.Fori(0, IMAGES // 2) as i:
                base[0] = i * STEPS_OF_2_IMAGES + 1
                for u in range(2):
                    image(i * 2 + u)
            assert steps[0] == STEPS_OF_2_IMAGES, steps[0]
            steps[0] = 0
            with dve.Fori(0, GROUPS) as i:
                base[0] = i * STEPS_OF_A_GROUP + (IMAGES // 2 * STEPS_OF_2_IMAGES + 1)
                for u in range(GT):
                    tile(i, u)
                experts(i)
            assert steps[0] == STEPS_OF_A_GROUP, steps[0]


STEPS_OF_2_IMAGES = 46
STEPS_OF_A_GROUP = 164


def kernel(**inputs):
    import concourse.bacc as bacc
    from concourse.bass_utils import run_bass_kernel_spmd

    f = {k: np.asarray(v) for k, v in inputs.items()}
    f32 = np.float32

    i, j = np.arange(SEQ - 1, dtype=f32)[:, None], np.arange(D, dtype=f32)[None, :]
    even = (np.arange(D) % 2 == 0)[None, :]
    angle = np.where(even, i / np.power(f32(1e4), j / f32(D)), i / np.power(f32(1e4), (j - f32(1)) / f32(D)))
    table = np.where(even, np.sin(angle), np.cos(angle)).astype(f32)

    def tokens(rows):
        return np.ascontiguousarray(rows.reshape(2, B, -1).transpose(1, 0, 2))

    def halves(w, bias):
        full = np.zeros((K1, 2, w.shape[1]), f32)
        full[0:HALF] = w.reshape(2, HALF, -1).transpose(1, 0, 2)
        if bias is not None:
            full[HALF, 0] = bias
        return full

    pos = tokens(np.concatenate([np.zeros((1, D), f32), table]))
    base = tokens(np.concatenate([f["cls_tok"].reshape(1, D), f["L0_tok_class_token"].reshape(1, D),
                                  np.broadcast_to(f["L0_tok_b_map"], (PATCHES, D))]))
    ln_w = tokens(np.concatenate([f["L0_tok_ln_w"][0:1], f["L0_tok_ln_w"]]))
    ln_b = tokens(np.concatenate([f["L0_tok_ln_b"][0:1], f["L0_tok_ln_b"]]))
    keep = np.ones((B, 2), f32)
    keep[0, 0] = 0
    mean_w = np.full((B, 2, B), 1.0 / (SEQ - 1), f32)
    mean_w[0, 0, :] = 0
    tri = [np.ascontiguousarray(np.broadcast_to(np.tril(np.ones((n, n), f32), -1), (T, n, n))) for n in (4, 8)]
    expand = np.zeros((EX, CH * 128), f32)
    for e in range(EX):
        expand[e, e * INNER:(e + 1) * INNER] = 0.5
    w_map = np.ascontiguousarray(f["L0_tok_W_map"].T.reshape(PC, 128, D).transpose(1, 0, 2))

    w_qkv1 = np.zeros((K1, 2, 3, HALF), f32)
    for s, name in enumerate("qkv"):
        w, bias = f[f"L0_tok_W{name}"], f[f"L0_tok_b{name}"].reshape(2, HALF)
        for h in range(H):
            r = DH * (h % HP)
            w_qkv1[r:r + DH, h // HP, s, r:r + DH] = w[h].T
        w_qkv1[HALF, :, s, :] = bias
    w_qkv1 = w_qkv1.reshape(K1, 2, 3 * HALF)
    w_qkv2 = halves(f["L0_attn_in_proj_weight"].T, f["L0_attn_in_proj_bias"])
    logit = np.ascontiguousarray(np.broadcast_to(f["L0_attn_logit_scale"].reshape(1, H), (T, H)))
    w_out = halves(f["L0_attn_out_w"].T, f["L0_attn_out_b"])
    head_scale = np.ones((K1, 2), f32)
    head_scale[0:HALF] = np.repeat(f["L0_attn_head_scale"].reshape(2, HP), DH, axis=1).T
    gate_w = halves(f["L0_ffn_gate_w"].T, None)
    gate_b = np.ascontiguousarray(np.broadcast_to(f["L0_ffn_gate_b"], (T, EXPERTS)))

    def up(name):
        w = np.concatenate([f[f"L0_ffn_W{name}"], f[f"L0_ffn_Ws{name}"][None]])
        bias = np.concatenate([f[f"L0_ffn_B{name}"], f[f"L0_ffn_Bs{name}"][None]])
        return w.transpose(1, 0, 2), bias

    parts = [up("1"), up("3")]
    w_up = np.stack([w[:, :, odd::2].reshape(D, ROWS) for odd in range(2) for w, _ in parts], 1)
    b_up = np.stack([bias[:, odd::2].reshape(ROWS) for odd in range(2) for _, bias in parts])
    w_up = halves(w_up.reshape(D, KINDS * ROWS), b_up.reshape(KINDS * ROWS))
    w_down = np.zeros((CH * 128, D), f32)
    w_down[0:ROWS] = np.concatenate([f["L0_ffn_W2"], f["L0_ffn_Ws2"][None]]).reshape(ROWS, D)
    w_down = np.ascontiguousarray(w_down.reshape(CH, 128, D).transpose(1, 0, 2))
    b_down = np.concatenate([f["L0_ffn_B2"], f["L0_ffn_Bs2"][None]])

    arrays = {
        "x": f["x"].reshape(IMAGES, PATCHES, PIX), "ident": np.eye(128, dtype=f32), "base": base, "pos": pos,
        "ln_w": ln_w, "ln_b": ln_b, "mean_w": mean_w, "keep": keep, "tri4": tri[0], "tri8": tri[1],
        "expand": expand.reshape(EX, CH, 128), "w_map": w_map, "w_qkv1": w_qkv1, "w_qkv2": w_qkv2,
        "logit": logit, "w_out": w_out, "head_scale": head_scale, "gate_w": gate_w, "gate_b": gate_b,
        "w_up": w_up, "w_down": w_down, "b_down": b_down,
    }
    nc = bacc.Bacc("TRN2", target_bir_lowering=False, num_devices=1)
    in_map, args = {}, []
    for name, a in arrays.items():
        a = np.ascontiguousarray(a)
        in_map[f"in_{name}"] = a
        args.append(nc.dram_tensor(f"in_{name}", a.shape, mybir.dt.from_np(a.dtype), kind="ExternalInput").ap())
    out = nc.dram_tensor("out", (IMAGES, SEQ, D), F32, kind="ExternalOutput").ap()
    h1_dram = nc.dram_tensor("h1_dram", (IMAGES, SEQ, D), F32, kind="Internal").ap()
    vit_block(nc, *args, h1_dram, out)
    result = run_bass_kernel_spmd(nc, [in_map], core_ids=[0])
    return result.results[0]["out"]
```

```python
from contextlib import ExitStack

import numpy as np

import concourse.bass as bass
from concourse import mybir
from concourse.alu_op_type import AluOpType as ALU

ACT = mybir.ActivationFunctionType
AX = mybir.AxisListType
F32 = mybir.dt.float32
F32R = mybir.dt.float32r
BF16 = mybir.dt.bfloat16
I32 = mybir.dt.int32

IMAGES = 64
PATCHES = 196
PIX = 768
PC = PIX // 128
D = 192
HALF = D // 2
K1 = HALF + 1
H = 12
DH = D // H
SEQ = PATCHES + 2
B = SEQ // 2
PB = PATCHES // 2
HP = H // 2
EXPERTS = 8
EX = EXPERTS + 1
INNER = 96
ROWS = EX * INNER
CH = -(-ROWS // 128)
KINDS = 4
PART = KINDS * ROWS // 2
LIMIT = 7.0
ALPHA = 1.702
EPS = 1e-5
NORM_EPS = 1e-12
SCALE_MAX = float(np.log(100.0))
HALVES_COPIES = 4
RSQRT_GUESS = float(0x5F3759DF)
NEWTON = 3
BIG = 3.0e38
T = 128
TILES = SEQ * IMAGES // T
GT = 3
GROUPS = TILES // GT
GC = GT * T
LOW = 64
EX2 = LOW + EX
UNITS = 5
PHASE2_FILLS = 5
WORK = 17664
WORK_R = 13056


def chunk_rows(j):
    return min(128, ROWS - 128 * j)


def vit_block(nc, x, ident, base, pos, ln_w, ln_b, mean_w, keep, tri4, tri8, expand, w_map, w_qkv1, w_qkv2,
              logit, w_out, head_scale, gate_w, gate_b, w_up, w_down, b_down, h1_dram, out):
    with ExitStack() as ctx:
        def sb(name, shape, dt=F32):
            return ctx.enter_context(nc.sbuf_tensor(name, shape, dt))

        def sem(name):
            return ctx.enter_context(nc.semaphore(name))

        bank = [ctx.enter_context(nc.psum_tensor(f"bank{n}", [128, 512], F32)) for n in range(8)]

        ident_sb = sb("ident_sb", [128, 128])
        neg_ident = sb("neg_ident", [128, 128], BF16)
        mean_w_sb = sb("mean_w_sb", [B, 2, B])
        keep_sb = sb("keep_sb", [B, 2])
        tri4_sb = sb("tri4_sb", [T, 4, 4])
        tri8_sb = sb("tri8_sb", [T, EXPERTS, EXPERTS])
        expand_sb = sb("expand_sb", [EX2, CH, 128], F32R)
        w_qkv2_sb = sb("w_qkv2_sb", [K1, 2, 3 * D])
        logit_sb = sb("logit_sb", [T, H])
        logit_scale = sb("logit_scale", [T, H])
        head_scale_sb = sb("head_scale_sb", [K1, 2])
        w_out_scaled = sb("w_out_scaled", [K1, 2, D])
        gate_w_sb = sb("gate_w_sb", [K1, 2, EXPERTS])
        gate_b_sb = sb("gate_b_sb", [T, EXPERTS])
        w_up_hi = sb("w_up_hi", [K1, 2, KINDS * ROWS], F32R)
        w_up_lo = sb("w_up_lo", [K1, 2, KINDS * ROWS], F32R)
        w_down_sb = sb("w_down_sb", [128, CH, D])
        b_down_sb = sb("b_down_sb", [EX2, D])

        work = sb("work", [128, WORK])
        work_r = sb("work_r", [128, WORK_R], F32R)

        def cutter(store, size):
            used = [0]

            def take(rows, *shape):
                n = int(np.prod(shape))
                assert used[0] + n <= size, used[0] + n
                flat = store[0:rows, used[0]:used[0] + n]
                used[0] += n
                names = "abcd"[0:len(shape)]
                return flat.rearrange(f"p ({' '.join(names)}) -> p {' '.join(names)}", **dict(zip(names, shape)))
            return take

        take, take_r = cutter(work, WORK), cutter(work_r, WORK_R)
        embed_add = take(B, 2, D)
        ln_w_sb = take(B, 2, D)
        ln_b_sb = take(B, 2, D)
        w_map_sb = take(128, PC, D)
        w_qkv1_sb = take(K1, 2, 3 * HALF)
        patches = take(PB, 2, 2, PIX)
        patches_t = take(128, PC, SEQ)
        tok = take(B, 2, 2, D)
        xn = take(B, 2, D)
        x_t = take(K1, 2, SEQ)
        qkn = take(B, 2, 2 * H, DH)
        v_ones = take(B, 4, H, 32)
        v_ones = v_ones[:, :, :, :].rearrange("p (u b) h d -> p u b h d", u=2)
        probs = take(B, 2, 2 * SEQ)
        o_t = take(128, 3, SEQ)
        o_n = take(B, 2, D)
        h1 = take(B, 2, D)
        pos_sb = take(B, 2, D)
        w_out_sb = take(K1, 2, D)
        w_up_part = take(K1, PART)
        expand_part = take(EX2, CH, 128)
        stack = take_r(B, 2, 2 * H, HALVES_COPIES, DH)
        k_st = take_r(128, 2, HP, SEQ)
        q_bd = take_r(128, 2, HP, 2, SEQ)
        stats = sb("stats", [B, 2, 6])
        mv = sb("mv", [B, 2, 2])
        dev = sb("dev", [B, 2])
        var = sb("var", [B, 2])
        veps = sb("veps", [B, 2])
        half_y = sb("half_y", [B, 1])
        rstd = sb("rstd", [B, 2])
        row_max = sb("row_max", [B, 2, 2, H], BF16)
        r_den = sb("r_den", [B, 2, H])

        take, take_r = cutter(work, WORK), cutter(work_r, WORK_R)
        h_in = take(T, GT, D)
        h_res = take(T, GT, D)
        xn2 = take(T, GT, D)
        x_t2 = take(K1, GT, 2, T)
        qk2 = take(T, GT, 2 * H, DH)
        qkn2 = take(T, GT, 2 * H, DH)
        v_ones2 = take(T, GT, H, 32)
        probs2 = take(T, GT, 4, T)
        o_t2 = take(128, GT, 3, T)
        o_n2 = take(T, GT, D)
        h2 = take(T, GT, D)
        stack2 = take_r(T, GT, 2 * H, HALVES_COPIES, DH)
        k_st2 = take_r(128, GT, HP, T)
        q_bd2 = take_r(128, GT, HP, 2, T)
        k_st2_upper = k_st2[:, :, :, :].bitcast(BF16).rearrange("p u h (s x) -> p u h s x", x=2)
        q_bd2_upper = q_bd2[:, :, :, :, :].bitcast(BF16).rearrange("p u h e (s x) -> p u h e s x", x=2)
        stats2 = sb("stats2", [T, GT, 6])
        mv2 = sb("mv2", [T, GT, 2])
        veps2 = sb("veps2", [T, GT])
        rstd2 = sb("rstd2", [T, GT])
        half_y2 = sb("half_y2", [T, GT * 2 * H])
        norm2 = sb("norm2", [T, GT, 2 * H])
        rnorm = sb("rnorm", [T, GT, 2 * H])
        row_max2 = sb("row_max2", [T, GT, H], BF16)
        r_den2 = sb("r_den2", [T, GT, H])

        x3_t = take(K1, 2, GT, T)
        x3_hi = take_r(K1, 2, GT, T)
        x3_lo = take_r(K1, 2, GT, T)
        h1_even = take(128, 2, GC)
        h1_odd = take(128, 2, GC)
        x_gate = take(128, 2, GC)
        th = take(128, 2, GC)
        lin = take(128, 2, GC)
        g_t = take(128, CH, GC)
        y_sb = take(T, GT, D)
        g_max = sb("g_max", [T, GT])
        g_exp = sb("g_exp", [T, GT, EXPERTS])
        g_sum = sb("g_sum", [T, GT])
        g_rec = sb("g_rec", [T, GT])
        g_prob = sb("g_prob", [T, GT, EXPERTS])
        g_s = sb("g_s", [T, GT, EXPERTS])
        g_grp = sb("g_grp", [T, GT, 4])
        g_cmp = sb("g_cmp", [T, GT, 64])
        g_eq = sb("g_eq", [T, GT, 64])
        g_rank = sb("g_rank", [T, GT, EXPERTS])
        g_keep = sb("g_keep", [T, GT, EXPERTS])
        combine = sb("combine", [T, GT, EX2], F32R)
        combine_t = sb("combine_t", [EX2, GC], F32R)

        s_const = sem("s_const")
        s_w_part = sem("s_w_part")
        s_w_split = sem("s_w_split")
        s_setup_v = sem("s_setup_v")
        s_setup_p = sem("s_setup_p")
        s_setup_a = sem("s_setup_a")
        s_phase2 = sem("s_phase2")
        s_patches = [sem("s_patches0"), sem("s_patches1")]
        s_pt_ps = sem("s_pt_ps")
        s_pt_a = sem("s_pt_a")
        s_pt_v = sem("s_pt_v")
        s_emb_ps = sem("s_emb_ps")
        s_v = sem("s_v")
        s_a = sem("s_a")
        s_ln1_ps = sem("s_ln1_ps")
        s_part = sem("s_part")
        s_xn_unit = sem("s_xn_unit")
        s_xn_w = sem("s_xn_w")
        s_xn = sem("s_xn")
        s_xt_ps = sem("s_xt_ps")
        s_xt = sem("s_xt")
        s_qkv_ps = sem("s_qkv_ps")
        s_qk = sem("s_qk")
        s_v_ps = sem("s_v_ps")
        s_vo = sem("s_vo")
        s_qkn = sem("s_qkn")
        s_hi = sem("s_hi")
        s_lo_q = sem("s_lo_q")
        s_lo_k = sem("s_lo_k")
        s_kt_ps = sem("s_kt_ps")
        s_qt_ps = sem("s_qt_ps")
        s_q_a = sem("s_q_a")
        s_q_v = sem("s_q_v")
        s_k_st = sem("s_k_st")
        s_sc_ps = sem("s_sc_ps")
        s_max = sem("s_max")
        s_sct_ps = sem("s_sct_ps")
        s_probs = sem("s_probs")
        s_pv = sem("s_pv")
        s_ot = sem("s_ot")
        s_on = sem("s_on")
        s_otok_ps = sem("s_otok_ps")
        s_h1 = sem("s_h1")
        s_h1_stored = sem("s_h1_stored")
        s_h_in = [sem(f"s_h_in{u}") for u in range(GT)]
        s_xn2 = sem("s_xn2")
        s_h_res = sem("s_h_res")
        s_xt2_ps = sem("s_xt2_ps")
        s_xt2 = sem("s_xt2")
        s_qkv2_ps = sem("s_qkv2_ps")
        s_qk2 = sem("s_qk2")
        s_v2 = sem("s_v2")
        s_qkn2 = sem("s_qkn2")
        s_hi2 = sem("s_hi2")
        s_lo2 = sem("s_lo2")
        s_st2_ps = sem("s_st2_ps")
        s_k_st2 = sem("s_k_st2")
        s_q_bd2 = sem("s_q_bd2")
        s_sc2_ps = sem("s_sc2_ps")
        s_max2 = sem("s_max2")
        s_sct2_ps = sem("s_sct2_ps")
        s_probs2 = sem("s_probs2")
        s_pv2 = sem("s_pv2")
        s_ot2 = sem("s_ot2")
        s_otok2_ps = sem("s_otok2_ps")
        s_on2 = sem("s_on2")
        s_ont_ps = sem("s_ont_ps")
        s_ont = sem("s_ont")
        s_proj_ps = sem("s_proj_ps")
        s_h2 = sem("s_h2")
        s_x3n = sem("s_x3n")
        s_x3t_ps = sem("s_x3t_ps")
        s_x3t = sem("s_x3t")
        s_x3_split = sem("s_x3_split")
        s_gate_ps = sem("s_gate_ps")
        s_gate_exp = sem("s_gate_exp")
        s_combine = sem("s_combine")
        s_ct_ps = sem("s_ct_ps")
        s_ct = sem("s_ct")
        s_c_ps = sem("s_c_ps")
        s_c = sem("s_c")
        s_up_ps = sem("s_up_ps")
        s_up_copy = sem("s_up_copy")
        s_up_read = sem("s_up_read")
        s_xg = sem("s_xg")
        s_th = sem("s_th")
        s_gated = sem("s_gated")
        s_g = sem("s_g")
        s_down_ps = sem("s_down_ps")
        s_y = sem("s_y")
        s_stored = sem("s_stored")

        block = ctx.enter_context(nc.Block())

        CONSTS = [(ident_sb[:, :], ident), (embed_add[:, :, :], base), (pos_sb[:, :, :], pos),
                  (ln_w_sb[:, :, :], ln_w), (ln_b_sb[:, :, :], ln_b), (mean_w_sb[:, :, :], mean_w),
                  (keep_sb[:, :], keep), (tri4_sb[:, :, :], tri4), (tri8_sb[:, :, :], tri8),
                  (expand_part[:, :, :], expand), (w_map_sb[:, :, :], w_map), (w_qkv1_sb[:, :, :], w_qkv1),
                  (w_qkv2_sb[:, :, :], w_qkv2), (logit_sb[:, :], logit), (w_out_sb[:, :, :], w_out),
                  (head_scale_sb[:, :], head_scale), (gate_w_sb[:, :, :], gate_w), (gate_b_sb[:, :], gate_b),
                  (w_down_sb[:, :, :], w_down), (b_down_sb[:, :], b_down)]
        CONST_LANDED = 16 * len(CONSTS)

        def patch_src(image):
            return x[bass.ds(image, 1), :, :].rearrange("a (b p) n -> p (a b) n", p=PB)

        def positions(array, tile):
            return array[:, bass.ds(tile * 2, 2), :].rearrange("i t d -> t i d")

        @block.sync
        def _(sp):
            for dst, src in CONSTS:
                sp.dma_start(dst, src).then_inc(s_const, 16)
            for u in range(2):
                sp.dma_start(patches[:, u, :, :], patch_src(u)).then_inc(s_patches[u], 16)
            for n in range(4):
                if n >= 1:
                    sp.wait_ge(s_w_split, 2 * n)
                sp.dma_start(w_up_part, w_up[:, n // 2, (n % 2) * PART:(n % 2) * PART + PART]).then_inc(s_w_part, 16)

            def store_h1(t):
                sp.wait_ge(s_h1, t + 1)
                sp.dma_start(h1_dram[bass.ds(t, 1), :, :].rearrange("a (b p) n -> p (a b) n", p=B),
                             h1[:, :, :]).then_inc(s_h1_stored, 16)

            with sp.Fori(0, IMAGES // 2 - 1) as i:
                for u in range(2):
                    sp.wait_ge(s_pt_ps, i * 6 + 3 * u + 3)
                    sp.dma_start(patches[:, u, :, :], patch_src(i * 2 + (2 + u))).then_inc(s_patches[u], 16)
                    store_h1(i * 2 + u)
            for u in range(2):
                store_h1(IMAGES - 2 + u)

            sp.wait_ge(s_h1_stored, 16 * IMAGES + 16)
            for u in range(GT):
                for e in range(2):
                    sp.dma_start(h_in[64 * e:64 * e + 64, u, :], h1_dram[:, 2 * u + e, :]).then_inc(s_h_in[u], 16)

            def store(i):
                sp.wait_ge(s_y, i + 2)
                for u in range(GT):
                    for e in range(2):
                        sp.dma_start(out[:, bass.ds(i * (2 * GT) + (2 * u + e), 1), :].rearrange("i t d -> i (t d)"),
                                     y_sb[64 * e:64 * e + 64, u, :]).then_inc(s_stored, 16)

            with sp.Fori(0, GROUPS - 1) as i:
                sp.wait_ge(s_h_res, i + 1)
                for u in range(GT):
                    for e in range(2):
                        sp.dma_start(h_in[64 * e:64 * e + 64, u, :],
                                     h1_dram[:, bass.ds(i * (2 * GT) + (2 * GT + 2 * u + e), 1), :].rearrange(
                                         "i t d -> i (t d)")).then_inc(s_h_in[u], 16)
                store(i)
            store(GROUPS - 1)
            sp.wait_ge(s_stored, 32 * GT * (GROUPS + 1))

        @block.tensor
        def _(pe):
            pe.wait_ge(s_const, CONST_LANDED)
            pe.wait_ge(s_setup_v, 1)
            pe.wait_ge(s_setup_p, 1)

            def patches_to_columns(t, u, landed, first=False):
                pe.wait_ge(s_patches[u], landed)
                for n in range(3):
                    if n == 2:
                        pe.wait_ge(s_pt_a, t * 2 + 1)
                    elif not first:
                        pe.wait_ge((s_k_st, s_q_v)[n], t * 3)
                        if n == 1:
                            pe.wait_ge(s_q_a, t * 3)
                    for c in (2 * n, 2 * n + 1):
                        for b in range(2):
                            at = (c % 2) * PATCHES + b * PB
                            last = pe.transpose(bank[n % 2][:, at:at + PB],
                                                patches[:, u, b, c * 128:c * 128 + 128], ident_sb[0:PB, 0:PB])
                    last.then_inc(s_pt_ps, 1)

            def embed(t):
                pe.wait_ge(s_pt_a, t * 2 + 2)
                pe.wait_ge(s_pt_v, t + 1)
                for b in range(2):
                    for c in range(PC):
                        last = pe.matmul(bank[1][0:B, b * D:b * D + D], patches_t[:, c, b * B:b * B + B],
                                         w_map_sb[:, c, :], start=(b == 0 and c == 0), stop=(c == PC - 1),
                                         skip_group_check=True)
                last.then_inc(s_emb_ps, 1)

            def moment(t, n):
                pe.wait_ge(s_part, t * 2 + (n + 1))
                for b in range(2):
                    col = (mv[:, b, 0:1], var[:, b:b + 1])[n]
                    last = pe.matmul(bank[0][0:B, n:n + 1], mean_w_sb[:, b, :], col, start=(b == 0), stop=(b == 1))
                last.then_inc(s_ln1_ps, 1)

            def tokens_t(t):
                pe.wait_ge(s_xn, t + 1)
                for half in range(2):
                    for b in range(2):
                        last = pe.transpose(bank[0][0:HALF, half * SEQ + b * B:half * SEQ + b * B + B],
                                            xn[:, b, half * HALF:half * HALF + HALF], ident_sb[0:B, 0:B])
                last.then_inc(s_xt_ps, 1)

            def image_qkv(t):
                pe.wait_ge(s_xt, t * 2 + 2)
                for b in range(2):
                    for half in range(2):
                        last = pe.matmul(bank[1 - b][0:B, 0:2 * D].rearrange("p (s n) -> p s n", s=2)[
                            :, :, half * HALF:half * HALF + HALF], x_t[:, half, b * B:b * B + B],
                                         w_qkv1_sb[:, half, 0:2 * HALF].rearrange("p (s n) -> p s n", s=2),
                                         start=(half == 0), stop=True, skip_group_check=True)
                    last.then_inc(s_qkv_ps, 1)
                pe.wait_ge(s_qk, t * 2 + 1)
                for b in range(2):
                    for half in range(2):
                        at = b * D + half * HALF
                        last = pe.matmul(bank[1][0:B, at:at + HALF], x_t[:, half, b * B:b * B + B],
                                         w_qkv1_sb[:, half, 2 * HALF:3 * HALF],
                                         start=(b == 0 and half == 0), stop=True, skip_group_check=True)
                last.then_inc(s_v_ps, 1)

            def image_heads_t(t):
                pe.wait_ge(s_hi, t * 4 + 4)
                pe.wait_ge(s_lo_q, t * 2 + 2)
                pe.wait_ge(s_lo_k, t * 2 + 2)
                pe.wait_ge(s_vo, t * 2 + 2)
                for n in range(3):
                    for dst, side, done, used in ((bank[0], H, s_kt_ps, (s_k_st,)), (bank[1], 0, s_qt_ps, (s_q_a, s_q_v))):
                        if n >= 1:
                            for copied in used:
                                pe.wait_ge(copied, t * 3 + n)
                        for m in range(2):
                            head = side + 4 * n + 2 * m
                            for b in range(2):
                                last = pe.transpose(dst[:, m * SEQ + b * B:m * SEQ + b * B + B],
                                                    stack[:, b, head:head + 2, :, :].bitcast(F32).rearrange(
                                                        "p h c d -> p (h c d)"), ident_sb[0:B, 0:B])
                        last.then_inc(done, 1)

            def image_scores(t, u, p):
                if p % 2 == 0:
                    for copied in (s_k_st, s_q_a, s_q_v):
                        pe.wait_ge(copied, t * 3 + (p // 2 + 1))
                for b in range(2):
                    if p >= 1:
                        pe.wait_ge(s_max, t * (2 * HP) + (2 * p - 1 + b))
                    for e in range(2):
                        last = pe.matmul(bank[2 + b][0:B, e * SEQ:e * SEQ + SEQ], q_bd[:, u, p, e, b * B:b * B + B],
                                         k_st[:, u, p, :], start=(e == 0), stop=True, skip_group_check=True)
                    last.then_inc(s_sc_ps, 1)

            def image_scores_t(t, u, p):
                pe.wait_ge(s_max, t * (2 * HP) + (2 * p + 2))
                for b in range(2):
                    if p == 0:
                        pe.wait_ge(s_on, t * 2 + (b + 1))
                    else:
                        pe.wait_ge(s_probs, t * (2 * HP) + (2 * p - 1 + b))
                    sc = bank[4 + b]
                    pe.matmul(sc[0:B, 0:2 * SEQ], k_st[:, u, p, b * B:b * B + B],
                              q_bd[:, u, p, :, :].rearrange("p e s -> p (e s)"), start=True, stop=False,
                              skip_group_check=True)
                    for e in range(2):
                        for qb in range(2):
                            at = e * SEQ + qb * B
                            last = pe.matmul(sc[0:B, at:at + B],
                                             row_max[:, u, qb, 2 * p + e:2 * p + e + 1].broadcast_to([B, B]),
                                             neg_ident[0:B, 0:B], start=False, stop=True, skip_group_check=True)
                    last.then_inc(s_sct_ps, 1)

            def image_values(t, u, p):
                j = p // 2
                for b in range(2):
                    pe.wait_ge(s_probs, t * (2 * HP) + (2 * p + b + 1))
                    for e in range(2):
                        head = 2 * p + e
                        row, at = 32 * (head % 4), (j % 2) * SEQ
                        last = pe.matmul(bank[6 + j // 2][row:row + 32, at:at + SEQ], v_ones[:, u, b, head, :],
                                         probs[:, b, e * SEQ:e * SEQ + SEQ], start=(b == 0), stop=(b == 1),
                                         skip_group_check=True)
                    last.then_inc(s_pv, 1)

            def image_rows(t):
                pe.wait_ge(s_ot, t * 2 + 2)
                for b in range(2):
                    for j in range(3):
                        last = pe.transpose(bank[4 + b][0:B, j * 128:j * 128 + 128], o_t[:, j, b * B:b * B + B],
                                            ident_sb[:, :])
                    last.then_inc(s_otok_ps, 1)

            def attend(t, u, nxt, nu, landed):
                image_scores(t, u, 0)
                if nxt is not None:
                    patches_to_columns(nxt, nu, landed)
                image_scores(t, u, 1)
                image_scores_t(t, u, 0)
                if nxt is not None:
                    embed(nxt)
                image_scores(t, u, 2)
                image_values(t, u, 0)
                image_scores_t(t, u, 1)
                image_scores(t, u, 3)
                image_values(t, u, 1)
                if nxt is not None:
                    moment(nxt, 0)
                image_scores_t(t, u, 2)
                image_scores(t, u, 4)
                image_values(t, u, 2)
                if nxt is not None:
                    moment(nxt, 1)
                image_scores_t(t, u, 3)
                image_scores(t, u, 5)
                image_values(t, u, 3)
                if nxt is not None:
                    tokens_t(nxt)
                image_scores_t(t, u, 4)
                image_values(t, u, 4)
                if nxt is not None:
                    image_qkv(nxt)
                image_scores_t(t, u, 5)
                image_values(t, u, 5)
                if nxt is not None:
                    image_heads_t(nxt)
                image_rows(t)

            patches_to_columns(0, 0, 16, first=True)
            embed(0)
            moment(0, 0)
            moment(0, 1)
            tokens_t(0)
            image_qkv(0)
            image_heads_t(0)
            with pe.Fori(0, IMAGES // 2 - 1) as i:
                attend(i * 2, 0, i * 2 + 1, 1, i * 16 + 16)
                attend(i * 2 + 1, 1, i * 2 + 2, 0, i * 16 + 32)
            attend(IMAGES - 2, 0, IMAGES - 1, 1, 16 * (IMAGES // 2))
            attend(IMAGES - 1, 1, None, None, None)

            def rows_t(g):
                for u in range(GT):
                    pe.wait_ge(s_xn2, g * GT + (u + 1))
                    for half in range(2):
                        last = pe.transpose(bank[2 * u + 1][0:HALF, half * T:half * T + T],
                                            xn2[:, u, half * HALF:half * HALF + HALF], ident_sb[:, :])
                    last.then_inc(s_xt2_ps, 1)

            def qkv(g):
                for u in range(GT):
                    pe.wait_ge(s_xt2, g * GT + (u + 1))
                    for half in range(2):
                        pe.matmul(bank[2 * u][:, 0:2 * D], x_t2[:, u, half, :], w_qkv2_sb[:, half, 0:2 * D],
                                  start=(half == 0), stop=(half == 1))
                        last = pe.matmul(bank[2 * u + 1][:, 0:D], x_t2[:, u, half, :],
                                         w_qkv2_sb[:, half, 2 * D:3 * D], start=(half == 0), stop=(half == 1))
                    last.then_inc(s_qkv2_ps, 1)

            def heads_t(g):
                units = ([(H, p) for p in range(4)], [(H, 4), (H, 5), (0, 0), (0, 1)], [(0, p) for p in range(2, 6)])
                for n, unit in enumerate(units):
                    for u in range(GT):
                        if n == 0:
                            pe.wait_ge(s_hi2, g * (2 * GT) + (2 * u + 2))
                            pe.wait_ge(s_lo2, g * (2 * GT) + (2 * u + 2))
                        if n == 2:
                            pe.wait_ge(s_k_st2, g * (2 * GT) + (u + 1))
                        for at, (side, p) in enumerate(unit):
                            head = side + 2 * p
                            last = pe.transpose(bank[2 * u + n % 2][:, at * T:at * T + T],
                                                stack2[:, u, head:head + 2, :, :].bitcast(F32).rearrange(
                                                    "p h c d -> p (h c d)"), ident_sb[:, :])
                        last.then_inc(s_st2_ps, 1)

            def scores(g):
                for n in range(3):
                    for u in range(GT):
                        if n == 0:
                            pe.wait_ge(s_k_st2, g * (2 * GT) + (GT + u + 1))
                            pe.wait_ge(s_q_bd2, g * GT + (u + 1))
                        if n == 2:
                            pe.wait_ge(s_max2, g * (3 * GT) + (u + 1))
                        for m in range(4):
                            p, e = 2 * n + m // 2, m % 2
                            last = pe.matmul(bank[2 * u + n % 2][:, m * T:m * T + T], q_bd2_upper[:, u, p, e, :, 1],
                                             k_st2_upper[:, u, p, :, 1], start=(m == 0), stop=True,
                                             skip_group_check=True)
                        last.then_inc(s_sc2_ps, 1)

            def scores_t(g, n):
                for u in range(GT):
                    if n == 0:
                        pe.wait_ge(s_max2, g * (3 * GT) + (2 * GT + u + 1))
                    if n == 2:
                        pe.wait_ge(s_probs2, g * (3 * GT) + (GT + u + 1))
                    dst = bank[2 * u + min(n, 1)]
                    for m in range(2):
                        p = 2 * n + m
                        pe.matmul(dst[:, m * 2 * T:(m + 1) * 2 * T], k_st2[:, u, p, :],
                                  q_bd2[:, u, p, :, :].rearrange("p e s -> p (e s)"), start=(m == 0), stop=False,
                                  skip_group_check=True)
                    for m in range(4):
                        head = 4 * n + m
                        last = pe.matmul(dst[:, m * T:m * T + T],
                                         row_max2[:, u, head:head + 1].broadcast_to([T, T]), neg_ident[:, :],
                                         start=False, stop=True, skip_group_check=True)
                    last.then_inc(s_sct2_ps, 1)

            def values(g, n):
                for u in range(GT):
                    pe.wait_ge(s_probs2, g * (3 * GT) + (GT * n + u + 1))
                    if n == 0:
                        pe.wait_ge(s_v2, g * GT + (u + 1))
                    for m in range(4):
                        last = pe.matmul(bank[2 * u][32 * m:32 * m + 32, n * T:n * T + T],
                                         v_ones2[:, u, 4 * n + m, :], probs2[:, u, m, :],
                                         start=True, stop=True, skip_group_check=True)
                    last.then_inc(s_pv2, 1)

            def attended_rows(g):
                for u in range(GT):
                    pe.wait_ge(s_ot2, g * GT + (u + 1))
                    for j in range(3):
                        last = pe.transpose(bank[2 * u + 1][:, j * 128:j * 128 + 128], o_t2[:, u, j, :],
                                            ident_sb[:, :])
                    last.then_inc(s_otok2_ps, 1)

            def project(g):
                for u in range(GT):
                    pe.wait_ge(s_on2, g * GT + (u + 1))
                    for half in range(2):
                        last = pe.transpose(bank[2 * u][0:HALF, half * T:half * T + T],
                                            o_n2[:, u, half * HALF:half * HALF + HALF], ident_sb[:, :])
                    last.then_inc(s_ont_ps, 1)
                for u in range(GT):
                    pe.wait_ge(s_ont, g * GT + (u + 1))
                    for half in range(2):
                        last = pe.matmul(bank[2 * u + 1][:, 0:D], x_t2[:, u, half, :], w_out_scaled[:, half, :],
                                         start=(half == 0), stop=(half == 1))
                    last.then_inc(s_proj_ps, 1)

            def experts_input_t(g):
                for u in range(GT):
                    pe.wait_ge(s_x3n, g * GT + (u + 1))
                    for half in range(2):
                        last = pe.transpose(bank[2 * u][0:HALF, half * T:half * T + T],
                                            xn2[:, u, half * HALF:half * HALF + HALF], ident_sb[:, :])
                    last.then_inc(s_x3t_ps, 1)

            def gate(g):
                pe.wait_ge(s_x3t, g * GT + GT)
                pe.wait_ge(s_y, g + 1)
                for u in range(GT):
                    for half in range(2):
                        last = pe.matmul(bank[6][:, u * EXPERTS:u * EXPERTS + EXPERTS],
                                         x3_t[:, half, u, :], gate_w_sb[:, half, :],
                                         start=(u == 0 and half == 0), stop=(half == 1), skip_group_check=True)
                last.then_inc(s_gate_ps, 1)

            def weights_t(g):
                pe.wait_ge(s_combine, g + 1)
                for u in range(GT):
                    last = pe.transpose(bank[7][0:EX2, u * T:u * T + T], combine[:, u, :].bitcast(F32),
                                        ident_sb[:, :])
                last.then_inc(s_ct_ps, 1)

            def up(g, j):
                m = chunk_rows(j)
                xh = [x3_hi[:, half, :, :].rearrange("p u s -> p (u s)") for half in range(2)]
                xl = [x3_lo[:, half, :, :].rearrange("p u s -> p (u s)") for half in range(2)]
                for k in range(UNITS):
                    if j == 0 and k == 0:
                        pe.wait_ge(s_x3_split, g * 2 + 2)
                    elif j == 0 and k == 1:
                        pe.wait_ge(s_ct, g + 1)
                    elif k == 1:
                        pe.wait_ge(s_up_read, g * (2 * CH) + 2 * j)
                    elif k == 3:
                        pe.wait_ge(s_up_read, g * (2 * CH) + (2 * j + 1))
                    else:
                        pe.wait_ge(s_up_copy, g * (3 * CH) + (3 * j + k // 2))
                    dst = bank[6 + (UNITS * j + k) % 2][0:m, 0:GC]
                    if k == 2:
                        last = pe.matmul(dst, expand_sb[:, j, 0:m], combine_t[:, :], start=True, stop=True)
                    else:
                        at = (0, 1, None, 2, 3)[k] * ROWS + 128 * j
                        for half in range(2):
                            pe.matmul(dst, w_up_hi[:, half, at:at + m], xh[half], start=(half == 0), stop=False)
                            pe.matmul(dst, w_up_hi[:, half, at:at + m], xl[half], start=False, stop=False)
                            last = pe.matmul(dst, w_up_lo[:, half, at:at + m], xh[half],
                                             start=False, stop=(half == 1))
                    last.then_inc(s_up_ps, 1)

            def down(g):
                pe.wait_ge(s_up_copy, g * (3 * CH) + 3 * CH)
                pe.wait_ge(s_up_read, g * (2 * CH) + 2 * CH)
                for u in range(GT):
                    dst = bank[6 + u // 2][:, (u % 2) * D:(u % 2) * D + D]
                    for j in range(CH):
                        m = chunk_rows(j)
                        if u == 0:
                            pe.wait_ge(s_g, g * CH + (j + 1))
                        pe.matmul(dst, g_t[0:m, j, u * T:u * T + T], w_down_sb[0:m, j, :],
                                  start=(u % 2 == 0 and j == 0), stop=False, skip_group_check=True)
                    last = pe.matmul(dst, combine_t[:, u * T:u * T + T].bitcast(F32), b_down_sb[:, :],
                                     start=False, stop=True, skip_group_check=True)
                last.then_inc(s_down_ps, 1)

            pe.wait_ge(s_phase2, PHASE2_FILLS)
            rows_t(0)
            qkv(0)
            heads_t(0)
            scores(0)
            scores_t(0, 0)
            scores_t(0, 1)
            values(0, 0)
            scores_t(0, 2)
            values(0, 1)
            values(0, 2)
            attended_rows(0)
            project(0)
            experts_input_t(0)
            with pe.Fori(0, GROUPS - 1) as i:
                gate(i)
                rows_t(i + 1)
                qkv(i + 1)
                weights_t(i)
                up(i, 0)
                up(i, 1)
                up(i, 2)
                heads_t(i + 1)
                up(i, 3)
                scores(i + 1)
                up(i, 4)
                scores_t(i + 1, 0)
                scores_t(i + 1, 1)
                up(i, 5)
                values(i + 1, 0)
                scores_t(i + 1, 2)
                values(i + 1, 1)
                up(i, 6)
                values(i + 1, 2)
                attended_rows(i + 1)
                down(i)
                project(i + 1)
                experts_input_t(i + 1)
            gate(GROUPS - 1)
            weights_t(GROUPS - 1)
            for j in range(CH):
                up(GROUPS - 1, j)
            down(GROUPS - 1)

        @block.scalar
        def _(act):
            act.wait_ge(s_const, CONST_LANDED)
            act.wait_ge(s_setup_v, 1)
            act.activation(logit_scale[:, :], logit_sb[:, :], ACT.Exp).then_inc(s_setup_a, 1)

            def patches_to_columns(t):
                for n in (0, 2):
                    act.wait_ge(s_pt_ps, t * 3 + (n + 1))
                    act.activation(patches_t[:, 2 * n:2 * n + 2, 2:SEQ], bank[0][:, 0:2 * PATCHES].rearrange(
                        "p (c s) -> p c s", c=2), ACT.Copy).then_inc(s_pt_a, 1)

            def tokens_t(t):
                act.wait_ge(s_xt_ps, t + 1)
                src = bank[0][0:HALF, 0:2 * SEQ].rearrange("p (h s) -> p h s", h=2)
                act.activation(x_t[0:HALF, :, 1:SEQ], src[:, :, 1:SEQ], ACT.Copy).then_inc(s_xt, 1)
                act.activation(x_t[0:HALF, :, 0:1], src[:, :, 1:2], ACT.Copy).then_inc(s_xt, 1)

            def image_qk(t):
                for b in range(2):
                    act.wait_ge(s_qkv_ps, t * 2 + (b + 1))
                    act.activation(qkn[:, b, :, :].rearrange("p h d -> p (h d)"), bank[1 - b][0:B, 0:2 * D],
                                   ACT.Copy).then_inc(s_qk, 1)

            def image_high_parts(t):
                act.wait_ge(s_qk, t * 2 + 2)
                for b in range(2):
                    for side, rows in enumerate((slice(0, 2), slice(0, 4, 2))):
                        heads = slice(side * H, side * H + H)
                        src = qkn[:, b, heads, :][:, :, None, :].broadcast_to([B, H, 2, DH])
                        act.activation(stack[:, b, heads, rows, :], src, ACT.Copy).then_inc(s_hi, 1)

            def image_heads_t(t, u):
                for n in range(3):
                    act.wait_ge(s_kt_ps, t * 3 + (n + 1))
                    act.activation(k_st[:, u, 2 * n:2 * n + 2, :].rearrange("p h s -> p (h s)"),
                                   bank[0][:, 0:2 * SEQ], ACT.Copy).then_inc(s_k_st, 1)
                    act.wait_ge(s_qt_ps, t * 3 + (n + 1))
                    act.activation(q_bd[0:64, u, 2 * n:2 * n + 2, 0, :], bank[1][0:64, 0:2 * SEQ].rearrange(
                        "p (h s) -> p h s", h=2), ACT.Copy).then_inc(s_q_a, 1)

            def image_exponentials(t, p):
                for b in range(2):
                    act.wait_ge(s_sct_ps, t * (2 * HP) + (2 * p + b + 1))
                    if p >= 1:
                        act.wait_ge(s_pv, t * (2 * HP) + (2 * p - 1 + b))
                    act.activation(probs[:, b, :], bank[4 + b][0:B, 0:2 * SEQ], ACT.Exp).then_inc(s_probs, 1)

            def image_attended(t, n):
                act.wait_ge(s_pv, t * (2 * HP) + (8, 12)[n])
                own = (slice(0, 2), slice(2, 3))[n]
                act.activation(o_t[:, own, :].rearrange("p j s -> p (j s)"), bank[6 + n][:, 0:(2 - n) * SEQ],
                               ACT.Copy).then_inc(s_ot, 1)

            def attend(t, nxt, nu):
                if nxt is not None:
                    patches_to_columns(nxt)
                for p in range(4):
                    image_exponentials(t, p)
                if nxt is not None:
                    tokens_t(nxt)
                image_exponentials(t, 4)
                image_attended(t, 0)
                if nxt is not None:
                    image_qk(nxt)
                    image_high_parts(nxt)
                image_exponentials(t, 5)
                if nxt is not None:
                    image_heads_t(nxt, nu)
                image_attended(t, 1)

            patches_to_columns(0)
            tokens_t(0)
            image_qk(0)
            image_high_parts(0)
            image_heads_t(0, 0)
            with act.Fori(0, IMAGES // 2 - 1) as i:
                attend(i * 2, i * 2 + 1, 1)
                attend(i * 2 + 1, i * 2 + 2, 0)
            attend(IMAGES - 2, IMAGES - 1, 1)
            attend(IMAGES - 1, None, None)

            def copy_halves(dst, src_bank):
                return act.activation(dst, src_bank[0:HALF, 0:2 * T].rearrange("p (h s) -> p h s", h=2), ACT.Copy)

            def rows_t(g):
                for u in range(GT):
                    act.wait_ge(s_xt2_ps, g * GT + (u + 1))
                    copy_halves(x_t2[0:HALF, u, :, :], bank[2 * u + 1]).then_inc(s_xt2, 1)
                act.wait_ge(s_xn2, g * GT + GT)
                act.activation(h_res[:, :, :], h_in[:, :, :], ACT.Copy).then_inc(s_h_res, 1)

            def qk(g):
                for u in range(GT):
                    act.wait_ge(s_qkv2_ps, g * GT + (u + 1))
                    act.activation(qk2[:, u, :, :].rearrange("p h d -> p (h d)"), bank[2 * u][:, 0:2 * D], ACT.Copy)\
                        .then_inc(s_qk2, 1)

            def high_parts(g):
                for u in range(GT):
                    act.wait_ge(s_qkn2, g * GT + (u + 1))
                    for side, rows in enumerate((slice(0, 2), slice(0, 4, 2))):
                        heads = slice(side * H, side * H + H)
                        src = qkn2[:, u, heads, :][:, :, None, :].broadcast_to([T, H, 2, DH])
                        act.activation(stack2[:, u, heads, rows, :], src, ACT.Copy).then_inc(s_hi2, 1)

            def heads_t(g):
                for u in range(GT):
                    act.wait_ge(s_st2_ps, g * (3 * GT) + (u + 1))
                    act.activation(k_st2[:, u, 0:4, :].rearrange("p h s -> p (h s)"), bank[2 * u][:, :], ACT.Copy)\
                        .then_inc(s_k_st2, 1)
                for u in range(GT):
                    act.wait_ge(s_st2_ps, g * (3 * GT) + (GT + u + 1))
                    act.activation(k_st2[:, u, 4:6, :].rearrange("p h s -> p (h s)"), bank[2 * u + 1][:, 0:2 * T],
                                   ACT.Copy)
                    for e in range(2):
                        own = slice(64 * e, 64 * e + 64)
                        last = act.activation(q_bd2[own, u, 0:2, e, :], bank[2 * u + 1][own, 2 * T:4 * T].rearrange(
                            "p (h s) -> p h s", h=2), ACT.Copy)
                    last.then_inc(s_k_st2, 1)

            def exponentials(g, n):
                for u in range(GT):
                    act.wait_ge(s_sct2_ps, g * (3 * GT) + (GT * n + u + 1))
                    if n >= 1:
                        act.wait_ge(s_pv2, g * (3 * GT) + (GT * (n - 1) + u + 1))
                    for e in range(2):
                        own = slice(64 * e, 64 * e + 64)
                        last = act.activation(probs2[own, u, :, own], bank[2 * u + min(n, 1)][own, :].rearrange(
                            "p (h s) -> p h s", h=4)[:, :, own], ACT.Exp)
                    last.then_inc(s_probs2, 1)

            def attended(g):
                for u in range(GT):
                    act.wait_ge(s_pv2, g * (3 * GT) + (2 * GT + u + 1))
                    act.activation(o_t2[:, u, :, :].rearrange("p j s -> p (j s)"), bank[2 * u][:, 0:3 * T], ACT.Copy)\
                        .then_inc(s_ot2, 1)

            def project(g):
                for u in range(GT):
                    act.wait_ge(s_ont_ps, g * GT + (u + 1))
                    copy_halves(x_t2[0:HALF, u, :, :], bank[2 * u]).then_inc(s_ont, 1)

            def experts_input_t(g):
                for u in range(GT):
                    act.wait_ge(s_x3t_ps, g * GT + (u + 1))
                    copy_halves(x3_t[0:HALF, :, u, :], bank[2 * u]).then_inc(s_x3t, 1)

            def input_high(g):
                act.wait_ge(s_x3t, g * GT + GT)
                act.wait_ge(s_y, g + 1)
                act.activation(x3_hi[:, :, :, :].rearrange("p h u s -> p (h u s)"),
                               x3_t[:, :, :, :].rearrange("p h u s -> p (h u s)"), ACT.Copy)\
                    .then_inc(s_x3_split, 1)

            def gate(g):
                act.wait_ge(s_gate_exp, g * 2 + 1)
                act.activation(g_exp[:, :, :], g_s[:, :, :], ACT.Exp).then_inc(s_gate_exp, 1)

            def weights_t(g):
                act.wait_ge(s_ct_ps, g + 1)
                act.activation(combine_t[:, :], bank[7][0:EX2, 0:GC], ACT.Copy).then_inc(s_ct, 1)

            def tanh(g, j):
                m = chunk_rows(j)
                act.wait_ge(s_xg, g * CH + (j + 1))
                act.activation(th[0:m, j % 2, :], x_gate[0:m, j % 2, :], ACT.Tanh, scale=ALPHA / 2)\
                    .then_inc(s_th, 1)

            def up(g, j):
                m = chunk_rows(j)
                for k, dst in ((0, h1_even[0:m, j % 2, :]), (2, g_t[0:m, j, :]), (3, h1_odd[0:m, j % 2, :])):
                    act.wait_ge(s_up_ps, g * (UNITS * CH) + (UNITS * j + k + 1))
                    act.activation(dst, bank[6 + (UNITS * j + k) % 2][0:m, 0:GC], ACT.Copy).then_inc(s_up_copy, 1)
                tanh(g, j)

            act.wait_ge(s_phase2, PHASE2_FILLS)
            rows_t(0)
            qk(0)
            high_parts(0)
            heads_t(0)
            for n in range(3):
                exponentials(0, n)
            attended(0)
            project(0)
            experts_input_t(0)
            with act.Fori(0, GROUPS - 1) as i:
                input_high(i)
                rows_t(i + 1)
                gate(i)
                qk(i + 1)
                weights_t(i)
                up(i, 0)
                up(i, 1)
                high_parts(i + 1)
                up(i, 2)
                heads_t(i + 1)
                up(i, 3)
                up(i, 4)
                exponentials(i + 1, 0)
                up(i, 5)
                exponentials(i + 1, 1)
                exponentials(i + 1, 2)
                up(i, 6)
                attended(i + 1)
                project(i + 1)
                experts_input_t(i + 1)
            input_high(GROUPS - 1)
            gate(GROUPS - 1)
            weights_t(GROUPS - 1)
            for j in range(CH):
                up(GROUPS - 1, j)

        @block.gpsimd
        def _(pool):
            pool.memset(v_ones[:, :, :, :, :].rearrange("p u b h d -> p (u b h d)"), 1.0).then_inc(s_setup_p, 1)
            pool.wait_ge(s_setup_p, 1)
            for u in range(2):
                pool.memset(v_ones[0:1, u, 0, :, :], 0.0).then_inc(s_setup_p, 1)
                pool.wait_ge(s_setup_p, u + 2)
            pool.wait_ge(s_setup_v, 1)

            def image_affine(t):
                pool.wait_ge(s_xn_unit, t + 1)
                pool.tensor_tensor(xn[:, :, :], xn[:, :, :], ln_w_sb[:, :, :], ALU.mult).then_inc(s_xn_w, 1)
                pool.wait_ge(s_xn_w, t + 1)
                pool.tensor_tensor(xn[:, :, :], xn[:, :, :], ln_b_sb[:, :, :], ALU.add).then_inc(s_xn, 1)

            def image_low_k(t):
                for b in range(2):
                    pool.wait_ge(s_hi, t * 4 + (2 * b + 2))
                    pool.tensor_tensor(stack[:, b, H:2 * H, 1:4:2, :],
                                       qkn[:, b, H:2 * H, :][:, :, None, :].broadcast_to([B, H, 2, DH]),
                                       stack[:, b, H:2 * H, 0:4:2, :], ALU.subtract).then_inc(s_lo_k, 1)

            with pool.Fori(0, IMAGES) as i:
                image_affine(i)
                image_low_k(i)

            pool.wait_ge(s_h1_stored, 16 * IMAGES + 16)
            pool.memset(v_ones2[:, :, :, :].rearrange("p u h d -> p (u h d)"), 1.0).then_inc(s_phase2, 1)
            pool.memset(probs2[:, :, :, :].rearrange("p u h s -> p (u h s)"), 0.0).then_inc(s_phase2, 1)
            pool.memset(q_bd2[:, :, :, :, :].rearrange("p u h e s -> p (u h e s)").bitcast(F32), 0.0)\
                .then_inc(s_phase2, 1)
            pool.wait_ge(s_phase2, 3)
            pool.memset(x_t2[HALF:K1, :, :, :], 1.0).then_inc(s_phase2, 1)
            pool.wait_ge(s_phase2, 4)
            pool.memset(x3_t[HALF:K1, :, :, :], 1.0).then_inc(s_phase2, 1)

            def weigh(g, j):
                m = chunk_rows(j)
                pool.wait_ge(s_up_copy, g * (3 * CH) + (3 * j + 2))
                pool.wait_ge(s_gated, g * CH + (j + 1))
                pool.tensor_tensor(g_t[0:m, j, :], lin[0:m, j % 2, :], g_t[0:m, j, :], ALU.mult).then_inc(s_g, 1)

            with pool.Fori(0, GROUPS - 1) as i:
                for j in range(CH):
                    weigh(i, j)
            for j in range(CH):
                weigh(GROUPS - 1, j)

        @block.vector
        def _(dve):
            steps = [0]

            dve.memset(q_bd[:, :, :, :, :].rearrange("p u h e s -> p (u h e s)").bitcast(F32), 0.0)
            dve.memset(patches_t[:, :, 0:2], 0.0)
            dve.memset(x_t[HALF:K1, :, :], 1.0)
            dve.memset(combine[:, :, EX:EX2].bitcast(F32), 0.0)
            dve.memset(combine[:, :, EXPERTS:EX].bitcast(F32), 1.0)
            dve.wait_ge(s_const, CONST_LANDED)
            dve.tensor_copy(expand_sb[:, :, :], expand_part[:, :, :])
            dve.tensor_scalar(w_qkv1_sb[:, :, 0:HALF], w_qkv1_sb[:, :, 0:HALF], DH ** -0.5, None, ALU.mult)
            dve.tensor_scalar(neg_ident[:, :], ident_sb[:, :], -1.0, None, ALU.mult)
            for half in range(2):
                dve.tensor_scalar(w_out_scaled[:, half, :], w_out_sb[:, half, :], head_scale_sb[:, half:half + 1],
                                  None, ALU.mult)
            dve.tensor_tensor(embed_add[:, :, :], embed_add[:, :, :], pos_sb[:, :, :], ALU.add)
            dve.tensor_scalar(logit_sb[:, :], logit_sb[:, :], SCALE_MAX, None, ALU.min).then_inc(s_v, 1)
            for n in range(4):
                hi, lo = (w[:, n // 2, (n % 2) * PART:(n % 2) * PART + PART] for w in (w_up_hi, w_up_lo))
                dve.wait_ge(s_w_part, 16 * n + 16)
                dve.tensor_copy(hi, w_up_part).then_inc(s_w_split, 1)
                dve.wait_ge(s_w_split, 2 * n + 1)
                dve.tensor_tensor(lo, w_up_part, hi, ALU.subtract).then_inc(s_w_split, 1)
            dve.wait_ge(s_w_split, 8)
            dve.wait_ge(s_setup_p, 3)
            dve.sem_inc(s_y, 1)
            dve.sem_inc(s_on, 2)
            dve.sem_inc(s_stored, 32 * GT)
            dve.sem_inc(s_h1_stored, 16)
            dve.sem_inc(s_setup_v, 1)
            dve.wait_ge(s_setup_a, 1)

            base = [1]

            def link(ins):
                steps[0] += 1
                ins.then_inc(s_v, 1)
                dve.wait_ge(s_v, base[0] + steps[0])

            def rsqrt(y, v, w):
                link(dve.tensor_scalar(y.bitcast(I32), v.bitcast(I32), -0.5, RSQRT_GUESS, ALU.mult, ALU.add))
                for _ in range(NEWTON):
                    link(dve.scalar_tensor_tensor(out=w, in0=y, scalar=-0.5, in1=y, op0=ALU.mult, op1=ALU.mult))
                    link(dve.tensor_tensor(w, w, v, ALU.mult))
                    link(dve.scalar_tensor_tensor(out=y, in0=w, scalar=1.5, in1=y, op0=ALU.add, op1=ALU.mult))

            def low_parts(dst, src, rows, sem_hi, count, sem_lo):
                for side, (hi, lo) in enumerate(((slice(0, 2), slice(2, 4)), (slice(0, 4, 2), slice(1, 4, 2)))):
                    heads = slice(side * H, side * H + H)
                    dve.wait_ge(sem_hi, count + (side + 1))
                    dve.tensor_tensor(dst[:, heads, lo, :],
                                      src[:, heads, :][:, :, None, :].broadcast_to([rows, H, 2, DH]),
                                      dst[:, heads, hi, :], ALU.subtract).then_inc(sem_lo, 1)

            def patches_to_columns(t):
                dve.wait_ge(s_pt_ps, t * 3 + 2)
                dve.tensor_copy(patches_t[:, 2:4, 2:SEQ], bank[1][:, 0:2 * PATCHES].rearrange(
                    "p (c s) -> p c s", c=2)).then_inc(s_pt_v, 1)

            def embed(t, u):
                dve.wait_ge(s_emb_ps, t + 1)
                link(dve.tensor_tensor(tok[:, u, :, :].rearrange("p b d -> p (b d)"), bank[1][0:B, 0:2 * D],
                                       embed_add[:, :, :].rearrange("p b d -> p (b d)"), ALU.add))
                for b in range(2):
                    last = dve.bn_stats(stats[:, b, :], tok[:, u, b, :])
                link(last)
                dve.memset(veps[:, 1:2], EPS)
                for b in range(2):
                    last = dve.bn_aggr(mv[:, b, :], stats[:, b, :])
                last.then_inc(s_part, 1)

            def variance(t):
                dve.wait_ge(s_ln1_ps, t * 2 + 1)
                link(dve.tensor_copy(veps[:, 0:1], bank[0][0:B, 0:1]))
                link(dve.tensor_scalar(dev[:, :], mv[:, :, 0], veps[:, 0:1], None, ALU.subtract))
                link(dve.tensor_tensor(dev[:, :], dev[:, :], dev[:, :], ALU.mult))
                dve.tensor_tensor(var[:, :], dev[:, :], mv[:, :, 1], ALU.add).then_inc(s_part, 1)

            def normalize(t, u):
                dve.wait_ge(s_ln1_ps, t * 2 + 2)
                link(dve.tensor_tensor(veps[:, 1:2], bank[0][0:B, 1:2], veps[:, 1:2], ALU.add))
                rsqrt(rstd[:, 0:1], veps[:, 1:2], half_y[:, 0:1])
                dve.tensor_scalar(xn[:, :, :], tok[:, u, :, :], veps[:, 0:1], rstd[:, 0:1],
                                  ALU.subtract, ALU.mult).then_inc(s_xn_unit, 1)

            def image_low_q(t):
                dve.wait_ge(s_qk, t * 2 + 2)
                for b in range(2):
                    dve.wait_ge(s_hi, t * 4 + (2 * b + 1))
                    dve.tensor_tensor(stack[:, b, 0:H, 2:4, :],
                                      qkn[:, b, 0:H, :][:, :, None, :].broadcast_to([B, H, 2, DH]),
                                      stack[:, b, 0:H, 0:2, :], ALU.subtract).then_inc(s_lo_q, 1)

            def image_v(t, u):
                dve.wait_ge(s_v_ps, t + 1)
                for b in range(2):
                    dve.tensor_scalar(v_ones[:, u, b, :, 0:DH], bank[1][0:B, b * D:b * D + D].rearrange(
                        "p (h d) -> p h d", h=H), keep_sb[:, b:b + 1], None, ALU.mult).then_inc(s_vo, 1)

            def image_heads_t(t, u):
                for n in range(3):
                    dve.wait_ge(s_qt_ps, t * 3 + (n + 1))
                    dve.tensor_copy(q_bd[64:128, u, 2 * n:2 * n + 2, 1, :], bank[1][64:128, 0:2 * SEQ].rearrange(
                        "p (h s) -> p h s", h=2)).then_inc(s_q_v, 1)

            def image_maxima(t, u, p):
                for b in range(2):
                    dve.wait_ge(s_sc_ps, t * (2 * HP) + (2 * p + b + 1))
                    dve.tensor_reduce(row_max[:, u, b, 2 * p:2 * p + 2], bank[2 + b][0:B, 0:2 * SEQ].rearrange(
                        "p (e s) -> p e s", e=2), AX.X, ALU.max).then_inc(s_max, 1)

            def image_rows(t, u):
                for b in range(2):
                    dve.wait_ge(s_otok_ps, t * 2 + (b + 1))
                    src = bank[4 + b][0:B, 0:3 * 128].rearrange("p (h d) -> p h d", h=H)
                    link(dve.reciprocal(r_den[:, b, :], src[:, :, DH]))
                    dve.tensor_tensor(o_n[:, b, :].rearrange("p (h d) -> p h d", h=H), src[:, :, 0:DH],
                                      r_den[:, b, :][:, :, None].broadcast_to([B, H, DH]), ALU.mult)\
                        .then_inc(s_on, 1)
                dve.wait_ge(s_on, t * 2 + 4)
                dve.wait_ge(s_h1_stored, t * 16 + 16)
                for b in range(2):
                    last = dve.scalar_tensor_tensor(out=h1[:, b, :], in0=o_n[:, b, :], scalar=keep_sb[:, b:b + 1],
                                                    in1=tok[:, u, b, :], op0=ALU.mult, op1=ALU.add)
                last.then_inc(s_h1, 1)

            def attend(t, u, nxt, nu):
                image_maxima(t, u, 0)
                if nxt is not None:
                    patches_to_columns(nxt)
                image_maxima(t, u, 1)
                if nxt is not None:
                    embed(nxt, nu)
                image_maxima(t, u, 2)
                image_maxima(t, u, 3)
                if nxt is not None:
                    variance(nxt)
                image_maxima(t, u, 4)
                if nxt is not None:
                    normalize(nxt, nu)
                image_maxima(t, u, 5)
                if nxt is not None:
                    image_low_q(nxt)
                    image_v(nxt, nu)
                    image_heads_t(nxt, nu)
                image_rows(t, u)

            base[0] = 1
            patches_to_columns(0)
            embed(0, 0)
            variance(0)
            normalize(0, 0)
            image_low_q(0)
            image_v(0, 0)
            image_heads_t(0, 0)
            assert steps[0] == STEPS_OF_TOKENS, steps[0]
            steps[0] = 0
            with dve.Fori(0, IMAGES // 2 - 1) as i:
                base[0] = i * (2 * STEPS_OF_AN_IMAGE) + (STEPS_OF_TOKENS + 1)
                attend(i * 2, 0, i * 2 + 1, 1)
                attend(i * 2 + 1, 1, i * 2 + 2, 0)
            assert steps[0] == 2 * STEPS_OF_AN_IMAGE, steps[0]
            steps[0] = 0
            base[0] = (IMAGES - 2) * STEPS_OF_AN_IMAGE + STEPS_OF_TOKENS + 1
            attend(IMAGES - 2, 0, IMAGES - 1, 1)
            attend(IMAGES - 1, 1, None, None)
            assert steps[0] == 2 * STEPS_OF_AN_IMAGE - STEPS_OF_TOKENS, steps[0]

            def layer_norms(src, done):
                for u in range(GT):
                    if src is h_in:
                        dve.wait_ge(s_h_in[u], norm_group[0] * 32 + 32)
                    last = dve.bn_stats(stats2[:, u, :], src[:, u, :])
                link(last)
                dve.memset(veps2[:, :], EPS)
                for u in range(GT):
                    last = dve.bn_aggr(mv2[:, u, :], stats2[:, u, :])
                link(last)
                link(dve.tensor_tensor(veps2[:, :], mv2[:, :, 1], veps2[:, :], ALU.add))
                rsqrt(rstd2[:, :], veps2[:, :], half_y2[:, 0:GT])
                for u in range(GT):
                    dve.tensor_scalar(xn2[:, u, :], src[:, u, :], mv2[:, u, 0:1], rstd2[:, u:u + 1],
                                      ALU.subtract, ALU.mult).then_inc(done, 1)

            norm_group = [0]

            def rows(g):
                norm_group[0] = g
                layer_norms(h_in, s_xn2)

            def v(g):
                for u in range(GT):
                    dve.wait_ge(s_qkv2_ps, g * GT + (u + 1))
                    dve.tensor_copy(v_ones2[:, u, :, 0:DH], bank[2 * u + 1][:, 0:D].rearrange(
                        "p (h d) -> p h d", h=H)).then_inc(s_v2, 1)

            def squares(g):
                for u in range(GT):
                    dve.wait_ge(s_qk2, g * GT + (u + 1))
                    last = dve.tensor_tensor(qkn2[:, u, :, :], qk2[:, u, :, :], qk2[:, u, :, :], ALU.mult)
                link(last)
                for u in range(GT):
                    last = dve.tensor_reduce(norm2[:, u, :], qkn2[:, u, :, :], AX.X, ALU.add)
                link(last)

            def unit_qk(g):
                flat = norm2[:, :, :].rearrange("p u h -> p (u h)")
                link(dve.tensor_scalar(flat, flat, NORM_EPS ** 2, None, ALU.max))
                rsqrt(rnorm[:, :, :].rearrange("p u h -> p (u h)"), flat, half_y2[:, :])
                link(dve.tensor_tensor(rnorm[:, :, 0:H], rnorm[:, :, 0:H],
                                       logit_scale[:, None, :].broadcast_to([T, GT, H]), ALU.mult))
                for u in range(GT):
                    dve.tensor_tensor(qkn2[:, u, :, :], qk2[:, u, :, :],
                                      rnorm[:, u, :][:, :, None].broadcast_to([T, 2 * H, DH]), ALU.mult)\
                        .then_inc(s_qkn2, 1)

            def low(g):
                for u in range(GT):
                    dve.wait_ge(s_qkn2, g * GT + (u + 1))
                    low_parts(stack2[:, u, :, :, :], qkn2[:, u, :, :], T, s_hi2, g * (2 * GT) + 2 * u, s_lo2)

            def heads_t(g):
                for u in range(GT):
                    dve.wait_ge(s_st2_ps, g * (3 * GT) + (2 * GT + u + 1))
                    src = bank[2 * u][:, :].rearrange("p (h s) -> p h s", h=4)
                    for e in range(2):
                        own = slice(64 * e, 64 * e + 64)
                        last = dve.tensor_copy(q_bd2[own, u, 2:6, e, :], src[own, :, :])
                    last.then_inc(s_q_bd2, 1)

            def maxima(g, n):
                for u in range(GT):
                    dve.wait_ge(s_sc2_ps, g * (3 * GT) + (GT * n + u + 1))
                    for e in range(2):
                        own = slice(64 * e, 64 * e + 64)
                        last = dve.tensor_reduce(row_max2[own, u, 4 * n:4 * n + 4],
                                                 bank[2 * u + n % 2][own, :].rearrange(
                                                     "p (h s) -> p h s", h=4)[:, :, own], AX.X, ALU.max)
                    last.then_inc(s_max2, 1)

            def divide(g):
                for u in range(GT):
                    dve.wait_ge(s_otok2_ps, g * GT + (u + 1))
                    src = bank[2 * u + 1][:, 0:3 * 128].rearrange("p (h d) -> p h d", h=H)
                    link(dve.reciprocal(r_den2[:, u, :], src[:, :, DH]))
                    dve.tensor_tensor(o_n2[:, u, :].rearrange("p (h d) -> p h d", h=H), src[:, :, 0:DH],
                                      r_den2[:, u, :][:, :, None].broadcast_to([T, H, DH]), ALU.mult)\
                        .then_inc(s_on2, 1)

            def residual(g):
                dve.wait_ge(s_y, g + 1)
                dve.wait_ge(s_h_res, g + 1)
                for u in range(GT):
                    dve.wait_ge(s_proj_ps, g * GT + (u + 1))
                    dve.tensor_tensor(h2[:, u, :], bank[2 * u + 1][:, 0:D], h_res[:, u, :], ALU.add)\
                        .then_inc(s_h2, 1)
                dve.wait_ge(s_h2, g * GT + GT)
                layer_norms(h2, s_x3n)

            def input_low(g):
                dve.wait_ge(s_x3_split, g * 2 + 1)
                dve.tensor_tensor(x3_lo[:, :, :, :].rearrange("p h u s -> p (h u s)"),
                                  x3_t[:, :, :, :].rearrange("p h u s -> p (h u s)"),
                                  x3_hi[:, :, :, :].rearrange("p h u s -> p (h u s)"), ALU.subtract)\
                    .then_inc(s_x3_split, 1)

            def spread(ap, n):
                return ap[:, :, None].broadcast_to([T, GT, n])

            def top2(values, tri, n, keep):
                cmp = g_cmp[:, :, 0:n * n].rearrange("p r (a c) -> p r a c", a=n)
                eq = g_eq[:, :, 0:n * n].rearrange("p r (a c) -> p r a c", a=n)
                for r in range(GT):
                    other = values[:, r, :][:, None, :].broadcast_to([T, n, n])
                    own = values[:, r, :][:, :, None].broadcast_to([T, n, n])
                    dve.tensor_tensor(cmp[:, r, :, :], other, own, ALU.is_gt)
                    last = dve.tensor_tensor(eq[:, r, :, :], other, own, ALU.is_equal)
                link(last)
                for r in range(GT):
                    last = dve.tensor_tensor(eq[:, r, :, :], eq[:, r, :, :], tri, ALU.mult)
                link(last)
                link(dve.tensor_tensor(g_cmp[:, :, 0:n * n], g_cmp[:, :, 0:n * n], g_eq[:, :, 0:n * n], ALU.add))
                link(dve.tensor_reduce(g_rank[:, :, 0:n], cmp, AX.X, ALU.add))
                link(dve.tensor_scalar(keep, g_rank[:, :, 0:n], 1.5, None, ALU.is_lt))

            def gate_logits(g):
                dve.wait_ge(s_gate_ps, g + 1)
                logits = bank[6][:, 0:GT * EXPERTS].rearrange("p (n e) -> p n e", n=GT)
                link(dve.tensor_reduce(g_max[:, :], logits, AX.X, ALU.max))
                dve.tensor_tensor(g_s[:, :, :], logits, spread(g_max[:, :], EXPERTS), ALU.subtract)\
                    .then_inc(s_gate_exp, 1)

            def gate(g):
                dve.wait_ge(s_gate_exp, g * 2 + 2)
                link(dve.tensor_reduce(g_sum[:, :], g_exp[:, :, :], AX.X, ALU.add))
                link(dve.reciprocal(g_rec[:, :], g_sum[:, :]))
                link(dve.tensor_tensor(g_prob[:, :, :], g_exp[:, :, :], spread(g_rec[:, :], EXPERTS), ALU.mult))
                link(dve.tensor_tensor(g_s[:, :, :], g_prob[:, :, :],
                                       gate_b_sb[:, None, :].broadcast_to([T, GT, EXPERTS]), ALU.add))
                pairs = g_s[:, :, :].rearrange("p n (g e) -> p n g e", e=2)
                link(dve.tensor_tensor(g_grp[:, :, :], pairs[:, :, :, 0], pairs[:, :, :, 1], ALU.add))
                top2(g_grp, tri4_sb[:, :, :], 4, g_grp[:, :, :])
                kept = g_keep[:, :, :].rearrange("p n (g e) -> p n g e", e=2)
                for e in range(2):
                    last = dve.tensor_copy(kept[:, :, :, e], g_grp[:, :, :])
                link(last)
                link(dve.tensor_tensor(g_s[:, :, :], g_s[:, :, :], g_keep[:, :, :], ALU.mult))
                link(dve.tensor_scalar(g_keep[:, :, :], g_keep[:, :, :], BIG, -BIG, ALU.mult, ALU.add))
                link(dve.tensor_tensor(g_s[:, :, :], g_s[:, :, :], g_keep[:, :, :], ALU.add))
                top2(g_s, tri8_sb[:, :, :], EXPERTS, g_keep[:, :, :])
                link(dve.tensor_tensor(g_keep[:, :, :], g_prob[:, :, :], g_keep[:, :, :], ALU.mult))
                link(dve.tensor_copy(combine[:, :, 0:EXPERTS], g_keep[:, :, :]))
                dve.tensor_tensor(combine[:, :, LOW:LOW + EXPERTS], g_keep[:, :, :], combine[:, :, 0:EXPERTS],
                                  ALU.subtract).then_inc(s_combine, 1)

            def times_sigmoid(g, j):
                m = chunk_rows(j)
                dve.wait_ge(s_th, g * CH + (j + 1))
                dve.scalar_tensor_tensor(out=lin[0:m, j % 2, :], in0=th[0:m, j % 2, :], scalar=1.0,
                                         in1=lin[0:m, j % 2, :], op0=ALU.add, op1=ALU.mult).then_inc(s_gated, 1)

            def up(g, j):
                m = chunk_rows(j)
                xg, ln = x_gate[0:m, j % 2, :], lin[0:m, j % 2, :]

                def product(dst, src, k, copies):
                    dve.wait_ge(s_up_copy, g * (3 * CH) + (3 * j + copies))
                    dve.wait_ge(s_up_ps, g * (UNITS * CH) + (UNITS * j + k + 1))
                    dve.tensor_tensor(dst, src[0:m, j % 2, :], bank[6 + (UNITS * j + k) % 2][0:m, 0:GC], ALU.mult)\
                        .then_inc(s_up_read, 1)

                product(xg, h1_even, 1, 1)
                if j >= 1:
                    times_sigmoid(g, j - 1)
                dve.wait_ge(s_up_read, g * (2 * CH) + (2 * j + 1))
                dve.tensor_scalar(xg, xg, LIMIT, None, ALU.min).then_inc(s_xg, 1)
                if j >= 2:
                    dve.wait_ge(s_g, g * CH + (j - 1))
                product(ln, h1_odd, 4, 3)
                dve.wait_ge(s_xg, g * CH + (j + 1))
                dve.wait_ge(s_up_read, g * (2 * CH) + (2 * j + 2))
                link(dve.tensor_scalar(ln, ln, 1.0, 1.0 - LIMIT, ALU.add, ALU.max))
                link(dve.scalar_tensor_tensor(out=ln, in0=ln, scalar=1.0 + LIMIT, in1=xg,
                                              op0=ALU.min, op1=ALU.mult))
                if j == CH - 1:
                    times_sigmoid(g, j)

            def down(g):
                dve.wait_ge(s_stored, g * (32 * GT) + 32 * GT)
                dve.wait_ge(s_down_ps, g + 1)
                dve.tensor_tensor(y_sb[:, 0:2, :].rearrange("p u d -> p (u d)"), bank[6][:, 0:2 * D],
                                  h2[:, 0:2, :].rearrange("p u d -> p (u d)"), ALU.add)
                dve.tensor_tensor(y_sb[:, 2, :], bank[7][:, 0:D], h2[:, 2, :], ALU.add).then_inc(s_y, 1)

            steps[0] = 0
            base[0] = FIRST_STEPS + 1
            dve.wait_ge(s_phase2, PHASE2_FILLS)
            rows(0)
            v(0)
            squares(0)
            unit_qk(0)
            low(0)
            heads_t(0)
            for n in range(3):
                maxima(0, n)
            divide(0)
            residual(0)
            assert steps[0] == STEPS_OF_ATTENTION, steps[0]
            steps[0] = 0
            with dve.Fori(0, GROUPS - 1) as i:
                base[0] = i * STEPS_OF_A_GROUP + (FIRST_STEPS + STEPS_OF_ATTENTION + 1)
                input_low(i)
                gate_logits(i)
                rows(i + 1)
                gate(i)
                v(i + 1)
                squares(i + 1)
                up(i, 0)
                unit_qk(i + 1)
                up(i, 1)
                low(i + 1)
                up(i, 2)
                heads_t(i + 1)
                up(i, 3)
                maxima(i + 1, 0)
                maxima(i + 1, 1)
                maxima(i + 1, 2)
                up(i, 4)
                up(i, 5)
                up(i, 6)
                divide(i + 1)
                down(i)
                residual(i + 1)
            assert steps[0] == STEPS_OF_A_GROUP, steps[0]
            steps[0] = 0
            base[0] = FIRST_STEPS + STEPS_OF_ATTENTION + (GROUPS - 1) * STEPS_OF_A_GROUP + 1
            input_low(GROUPS - 1)
            gate_logits(GROUPS - 1)
            gate(GROUPS - 1)
            for j in range(CH):
                up(GROUPS - 1, j)
            down(GROUPS - 1)


STEPS_OF_TOKENS = 16
STEPS_OF_AN_IMAGE = 18
FIRST_STEPS = IMAGES * STEPS_OF_AN_IMAGE
STEPS_OF_ATTENTION = 43
STEPS_OF_A_GROUP = 79


def kernel(**inputs):
    import concourse.bacc as bacc
    from concourse.bass_utils import run_bass_kernel_spmd

    f = {k: np.asarray(v) for k, v in inputs.items()}
    f32 = np.float32

    i, j = np.arange(SEQ - 1, dtype=f32)[:, None], np.arange(D, dtype=f32)[None, :]
    even = (np.arange(D) % 2 == 0)[None, :]
    angle = np.where(even, i / np.power(f32(1e4), j / f32(D)), i / np.power(f32(1e4), (j - f32(1)) / f32(D)))
    table = np.where(even, np.sin(angle), np.cos(angle)).astype(f32)

    def tokens(rows):
        return np.ascontiguousarray(rows.reshape(2, B, -1).transpose(1, 0, 2))

    def halves(w, bias):
        full = np.zeros((K1, 2, w.shape[1]), f32)
        full[0:HALF] = w.reshape(2, HALF, -1).transpose(1, 0, 2)
        if bias is not None:
            full[HALF, 0] = bias
        return full

    pos = tokens(np.concatenate([np.zeros((1, D), f32), table]))
    base = tokens(np.concatenate([f["cls_tok"].reshape(1, D), f["L0_tok_class_token"].reshape(1, D),
                                  np.broadcast_to(f["L0_tok_b_map"], (PATCHES, D))]))
    ln_w = tokens(np.concatenate([f["L0_tok_ln_w"][0:1], f["L0_tok_ln_w"]]))
    ln_b = tokens(np.concatenate([f["L0_tok_ln_b"][0:1], f["L0_tok_ln_b"]]))
    keep = np.ones((B, 2), f32)
    keep[0, 0] = 0
    mean_w = np.full((B, 2, B), 1.0 / (SEQ - 1), f32)
    mean_w[0, 0, :] = 0
    tri = [np.ascontiguousarray(np.broadcast_to(np.tril(np.ones((n, n), f32), -1), (T, n, n))) for n in (4, 8)]
    expand = np.zeros((EX2, CH * 128), f32)
    for e in range(EX):
        for row in (e, LOW + e):
            expand[row, e * INNER:(e + 1) * INNER] = 0.5
    w_map = np.ascontiguousarray(f["L0_tok_W_map"].T.reshape(PC, 128, D).transpose(1, 0, 2))

    w_qkv1 = np.zeros((K1, 2, 3, HALF), f32)
    for s, name in enumerate("qkv"):
        w, bias = f[f"L0_tok_W{name}"], f[f"L0_tok_b{name}"].reshape(2, HALF)
        for h in range(H):
            r = DH * (h % HP)
            w_qkv1[r:r + DH, h // HP, s, r:r + DH] = w[h].T
        w_qkv1[HALF, :, s, :] = bias
    w_qkv1 = w_qkv1.reshape(K1, 2, 3 * HALF)
    w_qkv2 = halves(f["L0_attn_in_proj_weight"].T, f["L0_attn_in_proj_bias"])
    logit = np.ascontiguousarray(np.broadcast_to(f["L0_attn_logit_scale"].reshape(1, H), (T, H)))
    w_out = halves(f["L0_attn_out_w"].T, f["L0_attn_out_b"])
    head_scale = np.ones((K1, 2), f32)
    head_scale[0:HALF] = np.repeat(f["L0_attn_head_scale"].reshape(2, HP), DH, axis=1).T
    gate_w = halves(f["L0_ffn_gate_w"].T, None)
    gate_b = np.ascontiguousarray(np.broadcast_to(f["L0_ffn_gate_b"], (T, EXPERTS)))

    def up(name):
        w = np.concatenate([f[f"L0_ffn_W{name}"], f[f"L0_ffn_Ws{name}"][None]])
        bias = np.concatenate([f[f"L0_ffn_B{name}"], f[f"L0_ffn_Bs{name}"][None]])
        return w.transpose(1, 0, 2), bias

    parts = [up("1"), up("3")]
    w_up = np.stack([w[:, :, odd::2].reshape(D, ROWS) for odd in range(2) for w, _ in parts], 1)
    b_up = np.stack([bias[:, odd::2].reshape(ROWS) for odd in range(2) for _, bias in parts])
    w_up = halves(w_up.reshape(D, KINDS * ROWS), b_up.reshape(KINDS * ROWS))
    w_down = np.zeros((CH * 128, D), f32)
    w_down[0:ROWS] = np.concatenate([f["L0_ffn_W2"], f["L0_ffn_Ws2"][None]]).reshape(ROWS, D)
    w_down = np.ascontiguousarray(w_down.reshape(CH, 128, D).transpose(1, 0, 2))
    b_down = np.zeros((EX2, D), f32)
    for row in (0, LOW):
        b_down[row:row + EX] = np.concatenate([f["L0_ffn_B2"], f["L0_ffn_Bs2"][None]])

    arrays = {
        "x": f["x"].reshape(IMAGES, PATCHES, PIX), "ident": np.eye(128, dtype=f32), "base": base, "pos": pos,
        "ln_w": ln_w, "ln_b": ln_b, "mean_w": mean_w, "keep": keep, "tri4": tri[0], "tri8": tri[1],
        "expand": expand.reshape(EX2, CH, 128), "w_map": w_map, "w_qkv1": w_qkv1, "w_qkv2": w_qkv2,
        "logit": logit, "w_out": w_out, "head_scale": head_scale, "gate_w": gate_w, "gate_b": gate_b,
        "w_up": w_up, "w_down": w_down, "b_down": b_down,
    }
    nc = bacc.Bacc("TRN2", target_bir_lowering=False, num_devices=1)
    in_map, args = {}, []
    for name, a in arrays.items():
        a = np.ascontiguousarray(a)
        in_map[f"in_{name}"] = a
        args.append(nc.dram_tensor(f"in_{name}", a.shape, mybir.dt.from_np(a.dtype), kind="ExternalInput").ap())
    out = nc.dram_tensor("out", (IMAGES, SEQ, D), F32, kind="ExternalOutput").ap()
    h1_dram = nc.dram_tensor("h1_dram", (IMAGES, SEQ, D), F32, kind="Internal").ap()
    vit_block(nc, *args, h1_dram, out)
    result = run_bass_kernel_spmd(nc, [in_map], core_ids=[0])
    return result.results[0]["out"]
```

```python
from contextlib import ExitStack

import numpy as np

import concourse.bass as bass
from concourse import mybir
from concourse.alu_op_type import AluOpType as ALU

ACT = mybir.ActivationFunctionType
AX = mybir.AxisListType
F32 = mybir.dt.float32
F32R = mybir.dt.float32r
BF16 = mybir.dt.bfloat16
I32 = mybir.dt.int32

IMAGES = 64
PATCHES = 196
PIX = 768
PC = PIX // 128
D = 192
HALF = D // 2
K1 = HALF + 1
H = 12
DH = D // H
SEQ = PATCHES + 2
B = SEQ // 2
PB = PATCHES // 2
HP = H // 2
EXPERTS = 8
EX = EXPERTS + 1
INNER = 96
ROWS = EX * INNER
CH = -(-ROWS // 128)
KINDS = 4
PART = KINDS * ROWS // 2
LIMIT = 7.0
ALPHA = 1.702
EPS = 1e-5
NORM_EPS = 1e-12
SCALE_MAX = float(np.log(100.0))
HALVES_COPIES = 4
RSQRT_GUESS = float(0x5F3759DF)
NEWTON = 3
BIG = 3.0e38
T = 128
TILES = SEQ * IMAGES // T
GT = 3
GROUPS = TILES // GT
GC = GT * T
LOW = 64
EX2 = LOW + EX
WEIGHTS = 4
WEIGHTS_BEFORE = 5
WEIGHTS_AT = KINDS * WEIGHTS_BEFORE
UNITS = [(kind, j) for j in range(WEIGHTS_BEFORE) for kind in range(KINDS)]
for _n, _j in enumerate(range(WEIGHTS_BEFORE, CH)):
    UNITS += [(0, _j), (1, _j), (WEIGHTS, 2 * _n), (2, _j), (3, _j), (WEIGHTS, 2 * _n + 1)]
UNITS += [(WEIGHTS, _j) for _j in range(2 * (CH - WEIGHTS_BEFORE), CH)]
MOMENTS = 400
PHASE2_FILLS = 5
WORK = 18048
WORK_R = 13056


def chunk_rows(j):
    return min(128, ROWS - 128 * j)


def units_of(j):
    begins = [UNITS.index((0, c)) for c in range(CH)] + [UNITS.index((3, CH - 1)) + 2, len(UNITS)]
    return range(begins[j], begins[j + 1])


def reads_until(n):
    return sum(kind in (1, 3) for kind, _ in UNITS[0:n + 1])


def copies_until(n):
    return sum(kind in (0, 2) for kind, _ in UNITS[0:n + 1])


def vit_block(nc, x, ident, base, pos, ln_w, ln_b, mean_w, keep, tri4, tri8, expand, w_map, w_qkv1, w_qkv2,
              logit, w_out, head_scale, gate_w, gate_b, w_up, w_down, b_down, h1_dram, out):
    with ExitStack() as ctx:
        def sb(name, shape, dt=F32):
            return ctx.enter_context(nc.sbuf_tensor(name, shape, dt))

        def sem(name):
            return ctx.enter_context(nc.semaphore(name))

        bank = [ctx.enter_context(nc.psum_tensor(f"bank{n}", [128, 512], F32)) for n in range(8)]

        ident_sb = sb("ident_sb", [128, 128])
        neg_ident = sb("neg_ident", [128, 128], BF16)
        keep_sb = sb("keep_sb", [B, 2])
        tri4_sb = sb("tri4_sb", [T, 4, 4])
        tri8_sb = sb("tri8_sb", [T, EXPERTS, EXPERTS])
        expand_sb = sb("expand_sb", [EX2, CH, 128], F32R)
        w_qkv2_sb = sb("w_qkv2_sb", [K1, 2, 3 * D])
        logit_sb = sb("logit_sb", [T, H])
        logit_scale = sb("logit_scale", [T, H])
        head_scale_sb = sb("head_scale_sb", [K1, 2])
        w_out_scaled = sb("w_out_scaled", [K1, 2, D])
        gate_w_sb = sb("gate_w_sb", [K1, 2, EXPERTS])
        gate_b_sb = sb("gate_b_sb", [T, EXPERTS])
        w_up_hi = sb("w_up_hi", [K1, 2, KINDS * ROWS], F32R)
        w_up_lo = sb("w_up_lo", [K1, 2, KINDS * ROWS], F32R)
        w_down_sb = sb("w_down_sb", [128, CH, D])
        b_down_sb = sb("b_down_sb", [EX2, D])

        work = sb("work", [128, WORK])
        work_r = sb("work_r", [128, WORK_R], F32R)

        def cutter(store, size):
            used = [0]

            def take(rows, *shape):
                n = int(np.prod(shape))
                assert used[0] + n <= size, used[0] + n
                flat = store[0:rows, used[0]:used[0] + n]
                used[0] += n
                names = "abcd"[0:len(shape)]
                return flat.rearrange(f"p ({' '.join(names)}) -> p {' '.join(names)}", **dict(zip(names, shape)))
            return take

        take, take_r = cutter(work, WORK), cutter(work_r, WORK_R)
        embed_add = take(B, 2, D)
        ln_w_sb = take(B, 2, D)
        ln_b_sb = take(B, 2, D)
        w_map_sb = take(128, PC, D)
        w_qkv1_sb = take(K1, 2, 3 * HALF)
        mean_w_sb = take(B, 2, B)
        patches = take(PB, 2, 2, PIX)
        patches_t = take(128, PC, SEQ)
        tok = take(B, 2, D)
        tok_kept = take(B, 2, 2, D)
        xn = take(B, 2, D)
        x_t = take(K1, 2, SEQ)
        qkn = take(B, 2, 2 * H, DH)
        v_ones = take(B, 4, H, 32)
        v_ones = v_ones[:, :, :, :].rearrange("p (u b) h d -> p u b h d", u=2)
        probs = take(B, 2, 2 * SEQ)
        o_t = take(128, 3, SEQ)
        o_n = take(B, 2, D)
        h1 = take(B, 2, D)
        pos_sb = take(B, 2, D)
        w_out_sb = take(K1, 2, D)
        w_up_part = take(K1, PART)
        expand_part = take(EX2, CH, 128)
        stack = take_r(B, 2, 2 * H, HALVES_COPIES, DH)
        k_st = take_r(128, 2, HP, SEQ)
        q_bd = take_r(128, 2, HP, 2, SEQ)
        stats = sb("stats", [B, 2, 6])
        mv = sb("mv", [B, 2, 2])
        dev = sb("dev", [B, 2])
        var = sb("var", [B, 2])
        veps = sb("veps", [B, 2])
        half_y = sb("half_y", [B, 1])
        rstd = sb("rstd", [B, 2])
        row_max = sb("row_max", [B, 2, 2, H], BF16)
        r_den = sb("r_den", [B, 2, H])

        take, take_r = cutter(work, WORK), cutter(work_r, WORK_R)
        h_in = take(T, GT, D)
        h_res = take(T, GT, D)
        xn2 = take(T, GT, D)
        x_t2 = take(K1, GT, 2, T)
        qk2 = take(T, GT, 2 * H, DH)
        qkn2 = take(T, GT, 2 * H, DH)
        v_ones2 = take(T, GT, H, 32)
        probs2 = take(T, GT, 4, T)
        o_t2 = take(128, GT, 3, T)
        o_n2 = take(T, GT, D)
        xn3 = o_n2
        h2 = take(T, GT, D)
        stack2 = take_r(T, GT, 2 * H, HALVES_COPIES, DH)
        k_st2 = take_r(128, GT, HP, T)
        q_bd2 = take_r(128, GT, HP, 2, T)
        k_st2_upper = k_st2[:, :, :, :].bitcast(BF16).rearrange("p u h (s x) -> p u h s x", x=2)
        q_bd2_upper = q_bd2[:, :, :, :, :].bitcast(BF16).rearrange("p u h e (s x) -> p u h e s x", x=2)
        stats2 = sb("stats2", [T, GT, 6])
        mv2 = sb("mv2", [T, GT, 2])
        veps2 = sb("veps2", [T, GT])
        rstd2 = sb("rstd2", [T, GT])
        half_y2 = sb("half_y2", [T, GT * 2 * H])
        norm2 = sb("norm2", [T, GT, 2 * H])
        rnorm = sb("rnorm", [T, GT, 2 * H])
        row_max2 = sb("row_max2", [T, GT, H], BF16)
        r_den2 = sb("r_den2", [T, GT, H])

        x3_t = take(K1, 2, GT, T)
        x3_hi = take_r(K1, 2, GT, T)
        x3_lo = take_r(K1, 2, GT, T)
        h1_even = take(128, 2, GC)
        h1_odd = take(128, 2, GC)
        x_gate = take(128, 2, GC)
        th = take(128, 2, GC)
        lin = take(128, GC)
        c_rows = take(128, 2, GC)
        g_t = take(128, CH, GC)
        y_sb = take(T, GT, D)
        g_max = sb("g_max", [T, GT])
        g_exp = sb("g_exp", [T, GT, EXPERTS])
        g_sum = sb("g_sum", [T, GT])
        g_rec = sb("g_rec", [T, GT])
        g_prob = sb("g_prob", [T, GT, EXPERTS])
        g_s = sb("g_s", [T, GT, EXPERTS])
        g_grp = sb("g_grp", [T, GT, 4])
        g_cmp = sb("g_cmp", [T, GT, 64])
        g_eq = sb("g_eq", [T, GT, 64])
        g_rank = sb("g_rank", [T, GT, EXPERTS])
        g_keep = sb("g_keep", [T, GT, EXPERTS])
        combine = sb("combine", [T, GT, EX2], F32R)
        combine_t = sb("combine_t", [EX2, GC], F32R)

        s_const = sem("s_const")
        s_w_part = sem("s_w_part")
        s_w_split = sem("s_w_split")
        s_setup_v = sem("s_setup_v")
        s_setup_p = sem("s_setup_p")
        s_setup_a = sem("s_setup_a")
        s_phase2 = sem("s_phase2")
        s_patches = [sem("s_patches0"), sem("s_patches1")]
        s_pt_ps = sem("s_pt_ps")
        s_pt_a = sem("s_pt_a")
        s_pt_v = sem("s_pt_v")
        s_emb_ps = sem("s_emb_ps")
        s_v = sem("s_v")
        s_ln1_ps = sem("s_ln1_ps")
        s_part = sem("s_part")
        s_tok = sem("s_tok")
        s_moments = sem("s_moments")
        s_tok_kept = sem("s_tok_kept")
        s_xn_unit = sem("s_xn_unit")
        s_xn_w = sem("s_xn_w")
        s_xn = sem("s_xn")
        s_xt_ps = sem("s_xt_ps")
        s_xt = sem("s_xt")
        s_qkv_ps = sem("s_qkv_ps")
        s_qk = sem("s_qk")
        s_v_ps = sem("s_v_ps")
        s_vo = sem("s_vo")
        s_hi = sem("s_hi")
        s_lo_q = sem("s_lo_q")
        s_lo_k = sem("s_lo_k")
        s_kt_ps = sem("s_kt_ps")
        s_qt_ps = sem("s_qt_ps")
        s_q_a = sem("s_q_a")
        s_q_v = sem("s_q_v")
        s_k_st = sem("s_k_st")
        s_sc_ps = sem("s_sc_ps")
        s_max = sem("s_max")
        s_sct_ps = sem("s_sct_ps")
        s_probs = sem("s_probs")
        s_pv = sem("s_pv")
        s_ot = sem("s_ot")
        s_on = sem("s_on")
        s_otok_ps = sem("s_otok_ps")
        s_h1 = sem("s_h1")
        s_h1_stored = sem("s_h1_stored")
        s_h_in = [sem(f"s_h_in{u}") for u in range(GT)]
        s_xn2 = sem("s_xn2")
        s_h_res = sem("s_h_res")
        s_xt2_ps = sem("s_xt2_ps")
        s_xt2 = sem("s_xt2")
        s_qkv2_ps = sem("s_qkv2_ps")
        s_qk2 = sem("s_qk2")
        s_v2 = sem("s_v2")
        s_squares = sem("s_squares")
        s_lo2_q = sem("s_lo2_q")
        s_lo2_k = sem("s_lo2_k")
        s_st2 = sem("s_st2")
        s_qkn2 = sem("s_qkn2")
        s_hi2 = sem("s_hi2")
        s_st2_ps = sem("s_st2_ps")
        s_q_bd2 = sem("s_q_bd2")
        s_sc2_ps = sem("s_sc2_ps")
        s_max2 = sem("s_max2")
        s_sct2_ps = sem("s_sct2_ps")
        s_probs2 = sem("s_probs2")
        s_pv2 = sem("s_pv2")
        s_ot2 = sem("s_ot2")
        s_otok2_ps = sem("s_otok2_ps")
        s_on2 = sem("s_on2")
        s_ont_ps = sem("s_ont_ps")
        s_ont = sem("s_ont")
        s_proj_ps = sem("s_proj_ps")
        s_h2 = sem("s_h2")
        s_x3n = sem("s_x3n")
        s_x3t_ps = sem("s_x3t_ps")
        s_x3t = sem("s_x3t")
        s_x3_split = sem("s_x3_split")
        s_gate_ps = sem("s_gate_ps")
        s_gate_exp = sem("s_gate_exp")
        s_combine = sem("s_combine")
        s_ct_ps = sem("s_ct_ps")
        s_ct = sem("s_ct")
        s_c = sem("s_c")
        s_up_ps = sem("s_up_ps")
        s_up_copy = sem("s_up_copy")
        s_up_read = sem("s_up_read")
        s_xg = sem("s_xg")
        s_th = sem("s_th")
        s_gated = sem("s_gated")
        s_g = sem("s_g")
        s_down_ps = sem("s_down_ps")
        s_y = sem("s_y")
        s_stored = sem("s_stored")

        block = ctx.enter_context(nc.Block())

        CONSTS = [(ident_sb[:, :], ident), (embed_add[:, :, :], base), (pos_sb[:, :, :], pos),
                  (ln_w_sb[:, :, :], ln_w), (ln_b_sb[:, :, :], ln_b), (mean_w_sb[:, :, :], mean_w),
                  (keep_sb[:, :], keep), (tri4_sb[:, :, :], tri4), (tri8_sb[:, :, :], tri8),
                  (expand_part[:, :, :], expand), (w_map_sb[:, :, :], w_map), (w_qkv1_sb[:, :, :], w_qkv1),
                  (w_qkv2_sb[:, :, :], w_qkv2), (logit_sb[:, :], logit), (w_out_sb[:, :, :], w_out),
                  (head_scale_sb[:, :], head_scale), (gate_w_sb[:, :, :], gate_w), (gate_b_sb[:, :], gate_b),
                  (w_down_sb[:, :, :], w_down), (b_down_sb[:, :], b_down)]
        CONST_LANDED = 16 * len(CONSTS)

        def patch_src(image):
            return x[bass.ds(image, 1), :, :].rearrange("a (b p) n -> p (a b) n", p=PB)

        def positions(array, tile):
            return array[:, bass.ds(tile * 2, 2), :].rearrange("i t d -> t i d")

        @block.sync
        def _(sp):
            for dst, src in CONSTS:
                sp.dma_start(dst, src).then_inc(s_const, 16)
            for u in range(2):
                sp.dma_start(patches[:, u, :, :], patch_src(u)).then_inc(s_patches[u], 16)
            for n in range(4):
                if n >= 1:
                    sp.wait_ge(s_w_split, 2 * n)
                sp.dma_start(w_up_part, w_up[:, n // 2, (n % 2) * PART:(n % 2) * PART + PART]).then_inc(s_w_part, 16)

            def store_h1(t):
                sp.wait_ge(s_h1, t + 1)
                sp.dma_start(h1_dram[bass.ds(t, 1), :, :].rearrange("a (b p) n -> p (a b) n", p=B),
                             h1[:, :, :]).then_inc(s_h1_stored, 16)

            with sp.Fori(0, IMAGES // 2 - 1) as i:
                for u in range(2):
                    sp.wait_ge(s_pt_ps, i * 6 + 3 * u + 3)
                    sp.dma_start(patches[:, u, :, :], patch_src(i * 2 + (2 + u))).then_inc(s_patches[u], 16)
                    store_h1(i * 2 + u)
            for u in range(2):
                store_h1(IMAGES - 2 + u)

            sp.wait_ge(s_h1_stored, 16 * IMAGES + 16)

            def load(g):
                for u in range(GT):
                    for e in range(2):
                        sp.dma_start(h_in[64 * e:64 * e + 64, u, :],
                                     h1_dram[:, bass.ds(g * (2 * GT) + (2 * u + e), 1), :].rearrange(
                                         "i t d -> i (t d)")).then_inc(s_h_in[u], 16)

            def store(i):
                sp.wait_ge(s_y, i + 2)
                for u in range(GT):
                    for e in range(2):
                        sp.dma_start(out[:, bass.ds(i * (2 * GT) + (2 * u + e), 1), :].rearrange("i t d -> i (t d)"),
                                     y_sb[64 * e:64 * e + 64, u, :]).then_inc(s_stored, 16)

            load(0)
            sp.wait_ge(s_h_res, 1)
            load(1)
            with sp.Fori(0, GROUPS - 2) as i:
                sp.wait_ge(s_h_res, i + 2)
                load(i + 2)
                store(i)
            for g in (GROUPS - 2, GROUPS - 1):
                store(g)
            sp.wait_ge(s_stored, 32 * GT * (GROUPS + 1))

        @block.tensor
        def _(pe):
            pe.wait_ge(s_const, CONST_LANDED)
            pe.wait_ge(s_setup_v, 1)
            pe.wait_ge(s_setup_p, 1)

            def patches_to_columns(t, u, landed, thirds=range(3), first=False):
                pe.wait_ge(s_patches[u], landed)
                for n in thirds:
                    if n == 2:
                        pe.wait_ge(s_pt_a, t * 2 + 1)
                    elif not first:
                        pe.wait_ge((s_qk, s_vo)[n], t * 2)
                    for c in (2 * n, 2 * n + 1):
                        for b in range(2):
                            at = (c % 2) * PATCHES + b * PB
                            last = pe.transpose(bank[n % 2][:, at:at + PB],
                                                patches[:, u, b, c * 128:c * 128 + 128], ident_sb[0:PB, 0:PB])
                    last.then_inc(s_pt_ps, 1)

            def embed(t, blocks=range(2)):
                pe.wait_ge(s_pt_a, t * 2 + 2)
                pe.wait_ge(s_pt_v, t + 1)
                for b in blocks:
                    for c in range(PC):
                        last = pe.matmul(bank[1][0:B, b * D:b * D + D], patches_t[:, c, b * B:b * B + B],
                                         w_map_sb[:, c, :], start=(b == 0 and c == 0), stop=(c == PC - 1),
                                         skip_group_check=True)
                    last.then_inc(s_emb_ps, 1)

            def tokens_t(t, first=False):
                pe.wait_ge(s_xn, t + 1)
                if not first:
                    pe.wait_ge(s_k_st, t * 3)
                for half in range(2):
                    for b in range(2):
                        last = pe.transpose(bank[0][0:HALF, half * SEQ + b * B:half * SEQ + b * B + B],
                                            xn[:, b, half * HALF:half * HALF + HALF], ident_sb[0:B, 0:B])
                last.then_inc(s_xt_ps, 1)

            def image_qkv(t, first=False):
                pe.wait_ge(s_xt, t * 2 + 2)
                if not first:
                    pe.wait_ge(s_q_a, t * 3)
                    pe.wait_ge(s_q_v, t * 3)
                for b in range(2):
                    for half in range(2):
                        last = pe.matmul(bank[1 - b][0:B, 0:2 * D].rearrange("p (s n) -> p s n", s=2)[
                            :, :, half * HALF:half * HALF + HALF], x_t[:, half, b * B:b * B + B],
                                         w_qkv1_sb[:, half, 0:2 * HALF].rearrange("p (s n) -> p s n", s=2),
                                         start=(half == 0), stop=True, skip_group_check=True)
                    last.then_inc(s_qkv_ps, 1)
                pe.wait_ge(s_qk, t * 2 + 1)
                for b in range(2):
                    for half in range(2):
                        at = b * D + half * HALF
                        last = pe.matmul(bank[1][0:B, at:at + HALF], x_t[:, half, b * B:b * B + B],
                                         w_qkv1_sb[:, half, 2 * HALF:3 * HALF],
                                         start=(b == 0 and half == 0), stop=True, skip_group_check=True)
                last.then_inc(s_v_ps, 1)

            def image_heads_t(t, n, embedded):
                if n == 0:
                    pe.wait_ge(s_hi, t * 4 + 4)
                    pe.wait_ge(s_lo_q, t * 2 + 2)
                    pe.wait_ge(s_lo_k, t * 2 + 2)
                    pe.wait_ge(s_vo, t * 2 + 2)
                    pe.wait_ge(s_tok, embedded)
                for dst, side, done, used in ((bank[0], H, s_kt_ps, (s_k_st,)), (bank[1], 0, s_qt_ps, (s_q_a, s_q_v))):
                    if n >= 1:
                        for copied in used:
                            pe.wait_ge(copied, t * 3 + n)
                    for m in range(2):
                        head = side + 4 * n + 2 * m
                        for b in range(2):
                            last = pe.transpose(dst[:, m * SEQ + b * B:m * SEQ + b * B + B],
                                                stack[:, b, head:head + 2, :, :].bitcast(F32).rearrange(
                                                    "p h c d -> p (h c d)"), ident_sb[0:B, 0:B])
                    last.then_inc(done, 1)

            def write_moment(t, n):
                pe.wait_ge(s_part, t * 2 + (n + 1))
                for b in range(2):
                    col = (mv[:, b, 0:1], var[:, b:b + 1])[n]
                    last = pe.matmul(bank[2][0:B, MOMENTS + n:MOMENTS + n + 1], mean_w_sb[:, b, :], col,
                                     start=(b == 0), stop=(b == 1))
                return last

            def image_scores(t, u, p, moment=None, last_image=False):
                if p == 0:
                    pe.wait_ge(s_moments, t + (1 if last_image else 2))
                if p % 2 == 0:
                    for copied in (s_k_st, s_q_a, s_q_v):
                        pe.wait_ge(copied, t * 3 + (p // 2 + 1))
                for b in range(2):
                    if p >= 1:
                        pe.wait_ge(s_max, t * (2 * HP) + (2 * p - 1 + b))
                    if b == 0 and moment is not None:
                        write_moment(t + 2, moment)
                    for e in range(2):
                        last = pe.matmul(bank[2 + b][0:B, e * SEQ:e * SEQ + SEQ], q_bd[:, u, p, e, b * B:b * B + B],
                                         k_st[:, u, p, :], start=(e == 0), stop=True, skip_group_check=True)
                    last.then_inc(s_sc_ps, 1)

            def image_scores_t(t, u, p):
                pe.wait_ge(s_max, t * (2 * HP) + (2 * p + 2))
                for b in range(2):
                    if p == 0:
                        pe.wait_ge(s_on, t * 2 + (b + 1))
                    else:
                        pe.wait_ge(s_probs, t * (2 * HP) + (2 * p - 1 + b))
                    sc = bank[4 + b]
                    pe.matmul(sc[0:B, 0:2 * SEQ], k_st[:, u, p, b * B:b * B + B],
                              q_bd[:, u, p, :, :].rearrange("p e s -> p (e s)"), start=True, stop=False,
                              skip_group_check=True)
                    for e in range(2):
                        for qb in range(2):
                            at = e * SEQ + qb * B
                            last = pe.matmul(sc[0:B, at:at + B],
                                             row_max[:, u, qb, 2 * p + e:2 * p + e + 1].broadcast_to([B, B]),
                                             neg_ident[0:B, 0:B], start=False, stop=True, skip_group_check=True)
                    last.then_inc(s_sct_ps, 1)

            def image_values(t, u, p):
                j = p // 2
                for b in range(2):
                    pe.wait_ge(s_probs, t * (2 * HP) + (2 * p + b + 1))
                    for e in range(2):
                        head = 2 * p + e
                        row, at = 32 * (head % 4), (j % 2) * SEQ
                        last = pe.matmul(bank[6 + j // 2][row:row + 32, at:at + SEQ], v_ones[:, u, b, head, :],
                                         probs[:, b, e * SEQ:e * SEQ + SEQ], start=(b == 0), stop=(b == 1),
                                         skip_group_check=True)
                    last.then_inc(s_pv, 1)

            def image_rows(t):
                pe.wait_ge(s_ot, t * 2 + 2)
                for b in range(2):
                    for j in range(3):
                        last = pe.transpose(bank[4 + b][0:B, j * 128:j * 128 + 128], o_t[:, j, b * B:b * B + B],
                                            ident_sb[:, :])
                    last.then_inc(s_otok_ps, 1)

            def attend(t, u, heads, tokens, landed):
                image_scores(t, u, 1)
                image_scores_t(t, u, 0)
                if heads:
                    tokens_t(t + 1)
                image_scores(t, u, 2)
                image_values(t, u, 0)
                if heads:
                    image_qkv(t + 1)
                image_scores_t(t, u, 1)
                if tokens:
                    patches_to_columns(t + 2, u, landed, (0, 1))
                image_scores(t, u, 3)
                if tokens:
                    patches_to_columns(t + 2, u, landed, (2,))
                image_values(t, u, 1)
                if tokens:
                    embed(t + 2, (0,))
                image_scores_t(t, u, 2)
                if tokens:
                    embed(t + 2, (1,))
                image_values(t, u, 2)
                image_scores_t(t, u, 3)
                if heads:
                    image_heads_t(t + 1, 0, t + (3 if tokens else 2))
                image_scores(t, u, 4, 0 if tokens else None)
                image_values(t, u, 3)
                image_scores_t(t, u, 4)
                if heads:
                    image_heads_t(t + 1, 1, None)
                image_scores(t, u, 5, 1 if tokens else None)
                image_values(t, u, 4)
                if heads:
                    image_heads_t(t + 1, 2, None)
                image_scores_t(t, u, 5)
                if heads:
                    image_scores(t + 1, 1 - u, 0, last_image=not tokens)
                image_values(t, u, 5)
                image_rows(t)

            patches_to_columns(0, 0, 16, first=True)
            embed(0)
            for n in range(2):
                write_moment(0, n).then_inc(s_ln1_ps, 1)
            tokens_t(0, first=True)
            image_qkv(0, first=True)
            patches_to_columns(1, 1, 16)
            embed(1)
            for n in range(2):
                write_moment(1, n).then_inc(s_ln1_ps, 1)
            for n in range(3):
                image_heads_t(0, n, 2)
            image_scores(0, 0, 0)
            with pe.Fori(0, IMAGES // 2 - 1) as i:
                attend(i * 2, 0, True, True, i * 16 + 32)
                attend(i * 2 + 1, 1, True, True, i * 16 + 32)
            attend(IMAGES - 2, 0, True, False, None)
            attend(IMAGES - 1, 1, False, False, None)

            def rows_t(g):
                for u in range(GT):
                    pe.wait_ge(s_xn2, g * GT + (u + 1))
                    for half in range(2):
                        last = pe.transpose(bank[2 * u][0:HALF, half * T:half * T + T],
                                            xn2[:, u, half * HALF:half * HALF + HALF], ident_sb[:, :])
                    last.then_inc(s_xt2_ps, 1)

            def qkv(g, tiles=range(GT), first=False):
                for u in tiles:
                    pe.wait_ge(s_xt2, g * GT + (u + 1))
                    if not first:
                        pe.wait_ge(s_h2, g * GT + (u + 1 - GT))
                    for half in range(2):
                        pe.matmul(bank[2 * u][:, 0:2 * D], x_t2[:, u, half, :], w_qkv2_sb[:, half, 0:2 * D],
                                  start=(half == 0), stop=(half == 1))
                        last = pe.matmul(bank[2 * u + 1][:, 0:D], x_t2[:, u, half, :],
                                         w_qkv2_sb[:, half, 2 * D:3 * D], start=(half == 0), stop=(half == 1))
                    last.then_inc(s_qkv2_ps, 1)

            def heads_t(g):
                units = ([(H, p) for p in range(4)], [(H, 4), (H, 5), (0, 0), (0, 1)], [(0, p) for p in range(2, 6)])
                for n, unit in enumerate(units):
                    for u in range(GT):
                        if n == 0:
                            pe.wait_ge(s_hi2, g * (2 * GT) + (2 * u + 2))
                            pe.wait_ge(s_lo2_q, g * GT + (u + 1))
                            pe.wait_ge(s_lo2_k, g * GT + (u + 1))
                        if n == 2:
                            pe.wait_ge(s_st2, g * (3 * GT) + (u + 1))
                        for at, (side, p) in enumerate(unit):
                            head = side + 2 * p
                            last = pe.transpose(bank[2 * u + n % 2][:, at * T:at * T + T],
                                                stack2[:, u, head:head + 2, :, :].bitcast(F32).rearrange(
                                                    "p h c d -> p (h c d)"), ident_sb[:, :])
                        last.then_inc(s_st2_ps, 1)

            def scores(g):
                for n in range(2):
                    for u in range(GT):
                        if n == 0:
                            pe.wait_ge(s_st2, g * (3 * GT) + (2 * GT + u + 1))
                            pe.wait_ge(s_q_bd2, g * GT + (u + 1))
                        for head in range(8 * n, min(8 * n + 8, H)):
                            at = head % 8 * IMAGES
                            for e in range(2):
                                own = slice(64 * e, 64 * e + 64)
                                last = pe.matmul(bank[2 * u + n][own, at:at + IMAGES],
                                                 q_bd2_upper[:, u, head // 2, head % 2, own, 1],
                                                 k_st2_upper[:, u, head // 2, own, 1], start=(head % 8 == 0),
                                                 stop=True, skip_group_check=True)
                        last.then_inc(s_sc2_ps, 1)

            def scores_t(g, n):
                for u in range(GT):
                    if n == 0:
                        pe.wait_ge(s_max2, g * (2 * GT) + (GT + u + 1))
                    if n == 2:
                        pe.wait_ge(s_probs2, g * (3 * GT) + (GT + u + 1))
                    dst = bank[2 * u + min(n, 1)]
                    for m in range(2):
                        p = 2 * n + m
                        pe.matmul(dst[:, m * 2 * T:(m + 1) * 2 * T], k_st2[:, u, p, :],
                                  q_bd2[:, u, p, :, :].rearrange("p e s -> p (e s)"), start=(m == 0), stop=False,
                                  skip_group_check=True)
                    for m in range(4):
                        head = 4 * n + m
                        last = pe.matmul(dst[:, m * T:m * T + T],
                                         row_max2[:, u, head:head + 1].broadcast_to([T, T]), neg_ident[:, :],
                                         start=False, stop=True, skip_group_check=True)
                    last.then_inc(s_sct2_ps, 1)

            def values(g, n):
                for u in range(GT):
                    pe.wait_ge(s_probs2, g * (3 * GT) + (GT * n + u + 1))
                    if n == 0:
                        pe.wait_ge(s_v2, g * GT + (u + 1))
                    for m in range(4):
                        last = pe.matmul(bank[2 * u][32 * m:32 * m + 32, n * T:n * T + T],
                                         v_ones2[:, u, 4 * n + m, :], probs2[:, u, m, :],
                                         start=True, stop=True, skip_group_check=True)
                    last.then_inc(s_pv2, 1)

            def attended_rows(g):
                for u in range(GT):
                    pe.wait_ge(s_ot2, g * GT + (u + 1))
                    for j in range(3):
                        last = pe.transpose(bank[2 * u + 1][:, j * 128:j * 128 + 128], o_t2[:, u, j, :],
                                            ident_sb[:, :])
                    last.then_inc(s_otok2_ps, 1)

            def project(g):
                for u in range(GT):
                    pe.wait_ge(s_on2, g * GT + (u + 1))
                    for half in range(2):
                        last = pe.transpose(bank[2 * u][0:HALF, half * T:half * T + T],
                                            o_n2[:, u, half * HALF:half * HALF + HALF], ident_sb[:, :])
                    last.then_inc(s_ont_ps, 1)
                for u in range(GT):
                    pe.wait_ge(s_ont, g * GT + (u + 1))
                    for half in range(2):
                        last = pe.matmul(bank[2 * u + 1][:, 0:D], x_t2[:, u, half, :], w_out_scaled[:, half, :],
                                         start=(half == 0), stop=(half == 1))
                    last.then_inc(s_proj_ps, 1)

            def experts_input_t(g, front):
                for u in range(GT):
                    if front and u < GT - 1:
                        pe.wait_ge(s_squares, g * GT + (GT + u + 1))
                    elif front:
                        pe.wait_ge(s_xt2, g * GT + 2 * GT)
                    pe.wait_ge(s_x3n, g * GT + (u + 1))
                    for half in range(2):
                        last = pe.transpose(bank[2 * u][0:HALF, half * T:half * T + T],
                                            xn3[:, u, half * HALF:half * HALF + HALF], ident_sb[:, :])
                    last.then_inc(s_x3t_ps, 1)

            def gate(g):
                pe.wait_ge(s_x3t, g * GT + GT)
                pe.wait_ge(s_y, g + 1)
                for u in range(GT):
                    for half in range(2):
                        last = pe.matmul(bank[7][:, u * EXPERTS:u * EXPERTS + EXPERTS],
                                         x3_t[:, half, u, :], gate_w_sb[:, half, :],
                                         start=(u == 0 and half == 0), stop=(half == 1), skip_group_check=True)
                last.then_inc(s_gate_ps, 1)

            def weights_t(g):
                pe.wait_ge(s_combine, g + 1)
                pe.wait_ge(s_up_read, g * (2 * CH) + reads_until(WEIGHTS_AT - 1))
                for u in range(GT):
                    last = pe.transpose(bank[7][0:EX2, u * T:u * T + T], combine[:, u, :].bitcast(F32),
                                        ident_sb[:, :])
                last.then_inc(s_ct_ps, 1)

            def up(g, j):
                xh = [x3_hi[:, half, :, :].rearrange("p u s -> p (u s)") for half in range(2)]
                xl = [x3_lo[:, half, :, :].rearrange("p u s -> p (u s)") for half in range(2)]
                for n in units_of(j):
                    kind, c = UNITS[n]
                    m = chunk_rows(c)
                    if n == 0:
                        pe.wait_ge(s_x3_split, g * 2 + 2)
                    elif n == 1:
                        pe.wait_ge(s_gate_exp, g * 2 + 1)
                    elif UNITS[n - 2][0] in (1, 3):
                        pe.wait_ge(s_up_read, g * (2 * CH) + reads_until(n - 2))
                    elif UNITS[n - 2][0] == WEIGHTS:
                        pe.wait_ge(s_c, g * CH + (UNITS[n - 2][1] + 1))
                    else:
                        pe.wait_ge(s_up_copy, g * (2 * CH) + copies_until(n - 2))
                    if n == WEIGHTS_AT + 1:
                        pe.wait_ge(s_ct, g + 1)
                    dst = bank[6 + n % 2][0:m, 0:GC]
                    if kind == WEIGHTS:
                        last = pe.matmul(dst, expand_sb[:, c, 0:m], combine_t[:, :], start=True, stop=True)
                    else:
                        at = kind * ROWS + 128 * c
                        for half in range(2):
                            pe.matmul(dst, w_up_hi[:, half, at:at + m], xh[half], start=(half == 0), stop=False)
                            pe.matmul(dst, w_up_hi[:, half, at:at + m], xl[half], start=False, stop=False)
                            last = pe.matmul(dst, w_up_lo[:, half, at:at + m], xh[half],
                                             start=False, stop=(half == 1))
                    last.then_inc(s_up_ps, 1)

            def down(g):
                pe.wait_ge(s_up_read, g * (2 * CH) + 2 * CH)
                pe.wait_ge(s_c, g * CH + CH)
                for j in range(CH):
                    m = chunk_rows(j)
                    pe.wait_ge(s_g, g * CH + (j + 1))
                    for u in range(GT):
                        dst = bank[6 + u // 2][:, (u % 2) * D:(u % 2) * D + D]
                        if j == 0:
                            pe.matmul(dst, combine_t[:, u * T:u * T + T].bitcast(F32), b_down_sb[:, :],
                                      start=(u % 2 == 0), stop=False, skip_group_check=True)
                        last = pe.matmul(dst, g_t[0:m, j, u * T:u * T + T], w_down_sb[0:m, j, :],
                                         start=False, stop=(j == CH - 1), skip_group_check=True)
                last.then_inc(s_down_ps, 1)

            pe.wait_ge(s_phase2, PHASE2_FILLS)
            rows_t(0)
            qkv(0, first=True)
            heads_t(0)
            scores(0)
            scores_t(0, 0)
            scores_t(0, 1)
            values(0, 0)
            scores_t(0, 2)
            values(0, 1)
            values(0, 2)
            attended_rows(0)
            project(0)
            rows_t(1)
            qkv(1, range(GT - 1))
            experts_input_t(0, True)
            pe.wait_ge(s_x3t, GT)
            qkv(1, (GT - 1,))

            def turn(i, front):
                gate(i)
                up(i, 0)
                up(i, 1)
                up(i, 2)
                heads_t(i + 1)
                up(i, 3)
                scores(i + 1)
                up(i, 4)
                scores_t(i + 1, 0)
                scores_t(i + 1, 1)
                values(i + 1, 0)
                scores_t(i + 1, 2)
                weights_t(i)
                up(i, 5)
                values(i + 1, 1)
                up(i, 6)
                values(i + 1, 2)
                up(i, CH)
                attended_rows(i + 1)
                down(i)
                project(i + 1)
                if front:
                    rows_t(i + 2)
                    qkv(i + 2, range(GT - 1))
                experts_input_t(i + 1, front)
                if front:
                    pe.wait_ge(s_x3t, i * GT + 2 * GT)
                    qkv(i + 2, (GT - 1,))

            with pe.Fori(0, GROUPS - 2) as i:
                turn(i, True)
            turn(GROUPS - 2, False)
            gate(GROUPS - 1)
            for j in range(CH + 1):
                if j == WEIGHTS_BEFORE:
                    weights_t(GROUPS - 1)
                up(GROUPS - 1, j)
            down(GROUPS - 1)

        @block.scalar
        def _(act):
            act.wait_ge(s_const, CONST_LANDED)
            act.wait_ge(s_setup_v, 1)
            act.activation(logit_scale[:, :], logit_sb[:, :], ACT.Exp).then_inc(s_setup_a, 1)

            def patches_to_columns(t, thirds=(0, 2)):
                for n in thirds:
                    act.wait_ge(s_pt_ps, t * 3 + (n + 1))
                    act.activation(patches_t[:, 2 * n:2 * n + 2, 2:SEQ], bank[0][:, 0:2 * PATCHES].rearrange(
                        "p (c s) -> p c s", c=2), ACT.Copy).then_inc(s_pt_a, 1)

            def tokens_t(t):
                act.wait_ge(s_xt_ps, t + 1)
                src = bank[0][0:HALF, 0:2 * SEQ].rearrange("p (h s) -> p h s", h=2)
                act.activation(x_t[0:HALF, :, 1:SEQ], src[:, :, 1:SEQ], ACT.Copy).then_inc(s_xt, 1)
                act.activation(x_t[0:HALF, :, 0:1], src[:, :, 1:2], ACT.Copy).then_inc(s_xt, 1)

            def image_qk(t):
                for b in range(2):
                    act.wait_ge(s_qkv_ps, t * 2 + (b + 1))
                    act.activation(qkn[:, b, :, :].rearrange("p h d -> p (h d)"), bank[1 - b][0:B, 0:2 * D],
                                   ACT.Copy).then_inc(s_qk, 1)

            def image_high_parts(t):
                act.wait_ge(s_qk, t * 2 + 2)
                for b in range(2):
                    for side, rows in enumerate((slice(0, 2), slice(0, 4, 2))):
                        heads = slice(side * H, side * H + H)
                        src = qkn[:, b, heads, :][:, :, None, :].broadcast_to([B, H, 2, DH])
                        act.activation(stack[:, b, heads, rows, :], src, ACT.Copy).then_inc(s_hi, 1)

            def image_heads_t(t, u, n):
                act.wait_ge(s_kt_ps, t * 3 + (n + 1))
                act.activation(k_st[:, u, 2 * n:2 * n + 2, :].rearrange("p h s -> p (h s)"),
                               bank[0][:, 0:2 * SEQ], ACT.Copy).then_inc(s_k_st, 1)
                act.wait_ge(s_qt_ps, t * 3 + (n + 1))
                act.activation(q_bd[0:64, u, 2 * n:2 * n + 2, 0, :], bank[1][0:64, 0:2 * SEQ].rearrange(
                    "p (h s) -> p h s", h=2), ACT.Copy).then_inc(s_q_a, 1)

            def image_exponentials(t, p):
                for b in range(2):
                    act.wait_ge(s_sct_ps, t * (2 * HP) + (2 * p + b + 1))
                    if p >= 1:
                        act.wait_ge(s_pv, t * (2 * HP) + (2 * p - 1 + b))
                    act.activation(probs[:, b, :], bank[4 + b][0:B, 0:2 * SEQ], ACT.Exp).then_inc(s_probs, 1)

            def image_attended(t, n):
                act.wait_ge(s_pv, t * (2 * HP) + (8, 12)[n])
                own = (slice(0, 2), slice(2, 3))[n]
                act.activation(o_t[:, own, :].rearrange("p j s -> p (j s)"), bank[6 + n][:, 0:(2 - n) * SEQ],
                               ACT.Copy).then_inc(s_ot, 1)

            def keep_tokens(t, u):
                act.activation(tok_kept[:, u, :, :], tok[:, :, :], ACT.Copy).then_inc(s_tok_kept, 1)

            def attend(t, u, heads, tokens):
                image_exponentials(t, 0)
                if heads:
                    tokens_t(t + 1)
                    image_qk(t + 1)
                    image_high_parts(t + 1)
                if tokens:
                    patches_to_columns(t + 2, (0,))
                image_exponentials(t, 1)
                if tokens:
                    patches_to_columns(t + 2, (2,))
                if heads:
                    keep_tokens(t + 1, 1 - u)
                image_exponentials(t, 2)
                image_exponentials(t, 3)
                if heads:
                    image_heads_t(t + 1, 1 - u, 0)
                image_exponentials(t, 4)
                if heads:
                    image_heads_t(t + 1, 1 - u, 1)
                image_attended(t, 0)
                if heads:
                    image_heads_t(t + 1, 1 - u, 2)
                image_exponentials(t, 5)
                image_attended(t, 1)

            patches_to_columns(0)
            tokens_t(0)
            image_qk(0)
            image_high_parts(0)
            keep_tokens(0, 0)
            patches_to_columns(1)
            for n in range(3):
                image_heads_t(0, 0, n)
            with act.Fori(0, IMAGES // 2 - 1) as i:
                attend(i * 2, 0, True, True)
                attend(i * 2 + 1, 1, True, True)
            attend(IMAGES - 2, 0, True, False)
            attend(IMAGES - 1, 1, False, False)

            def copy_halves(dst, src_bank):
                return act.activation(dst, src_bank[0:HALF, 0:2 * T].rearrange("p (h s) -> p h s", h=2), ACT.Copy)

            def rows_t(g, first=False):
                for u in range(GT):
                    act.wait_ge(s_xt2_ps, g * GT + (u + 1))
                    copy_halves(x_t2[0:HALF, u, :, :], bank[2 * u]).then_inc(s_xt2, 1)
                if not first:
                    act.wait_ge(s_h2, g * GT)
                act.wait_ge(s_xn2, g * GT + GT)
                act.activation(h_res[:, :, :], h_in[:, :, :], ACT.Copy).then_inc(s_h_res, 1)

            def qkv(g, tiles=range(GT)):
                for u in tiles:
                    act.wait_ge(s_qkv2_ps, g * GT + (u + 1))
                    src = bank[2 * u][:, 0:2 * D]
                    act.activation(qk2[:, u, :, :].rearrange("p h d -> p (h d)"), src, ACT.Copy).then_inc(s_qk2, 1)
                    act.activation(qkn2[:, u, :, :].rearrange("p h d -> p (h d)"), src, ACT.Square)\
                        .then_inc(s_squares, 1)
                    act.activation(v_ones2[:, u, :, 0:DH], bank[2 * u + 1][:, 0:D].rearrange(
                        "p (h d) -> p h d", h=H), ACT.Copy).then_inc(s_v2, 1)

            def high_parts(g):
                for u in range(GT):
                    act.wait_ge(s_qkn2, g * GT + (u + 1))
                    for side, rows in enumerate((slice(0, 2), slice(0, 4, 2))):
                        heads = slice(side * H, side * H + H)
                        src = qkn2[:, u, heads, :][:, :, None, :].broadcast_to([T, H, 2, DH])
                        act.activation(stack2[:, u, heads, rows, :], src, ACT.Copy).then_inc(s_hi2, 1)

            def heads_t(g):
                for u in range(GT):
                    act.wait_ge(s_st2_ps, g * (3 * GT) + (u + 1))
                    act.activation(k_st2[:, u, 0:4, :].rearrange("p h s -> p (h s)"), bank[2 * u][:, :], ACT.Copy)\
                        .then_inc(s_st2, 1)
                for u in range(GT):
                    act.wait_ge(s_st2_ps, g * (3 * GT) + (GT + u + 1))
                    act.activation(k_st2[:, u, 4:6, :].rearrange("p h s -> p (h s)"), bank[2 * u + 1][:, 0:2 * T],
                                   ACT.Copy)
                    for e in range(2):
                        own = slice(64 * e, 64 * e + 64)
                        last = act.activation(q_bd2[own, u, 0:2, e, :], bank[2 * u + 1][own, 2 * T:4 * T].rearrange(
                            "p (h s) -> p h s", h=2), ACT.Copy)
                    last.then_inc(s_st2, 1)

            def heads_t_rest(g):
                for u in range(GT):
                    act.wait_ge(s_st2_ps, g * (3 * GT) + (2 * GT + u + 1))
                    act.activation(q_bd2[0:64, u, 2:6, 0, :], bank[2 * u][0:64, :].rearrange(
                        "p (h s) -> p h s", h=4), ACT.Copy).then_inc(s_st2, 1)

            def exponentials(g, n):
                for u in range(GT):
                    act.wait_ge(s_sct2_ps, g * (3 * GT) + (GT * n + u + 1))
                    if n >= 1:
                        act.wait_ge(s_pv2, g * (3 * GT) + (GT * (n - 1) + u + 1))
                    for e in range(2):
                        own = slice(64 * e, 64 * e + 64)
                        last = act.activation(probs2[own, u, :, own], bank[2 * u + min(n, 1)][own, :].rearrange(
                            "p (h s) -> p h s", h=4)[:, :, own], ACT.Exp)
                    last.then_inc(s_probs2, 1)

            def attended(g):
                for u in range(GT):
                    act.wait_ge(s_pv2, g * (3 * GT) + (2 * GT + u + 1))
                    act.activation(o_t2[:, u, :, :].rearrange("p j s -> p (j s)"), bank[2 * u][:, 0:3 * T], ACT.Copy)\
                        .then_inc(s_ot2, 1)

            def project(g):
                for u in range(GT):
                    act.wait_ge(s_ont_ps, g * GT + (u + 1))
                    copy_halves(x_t2[0:HALF, u, :, :], bank[2 * u]).then_inc(s_ont, 1)

            def experts_input_t(g):
                for u in range(GT):
                    act.wait_ge(s_x3t_ps, g * GT + (u + 1))
                    copy_halves(x3_t[0:HALF, :, u, :], bank[2 * u]).then_inc(s_x3t, 1)

            def input_high(g):
                act.wait_ge(s_x3t, g * GT + GT)
                act.wait_ge(s_y, g + 1)
                act.activation(x3_hi[:, :, :, :].rearrange("p h u s -> p (h u s)"),
                               x3_t[:, :, :, :].rearrange("p h u s -> p (h u s)"), ACT.Copy)\
                    .then_inc(s_x3_split, 1)

            def gate(g):
                act.wait_ge(s_gate_exp, g * 2 + 1)
                act.activation(g_exp[:, :, :], g_s[:, :, :], ACT.Exp).then_inc(s_gate_exp, 1)

            def weights_t(g):
                act.wait_ge(s_ct_ps, g + 1)
                act.activation(combine_t[:, :], bank[7][0:EX2, 0:GC], ACT.Copy).then_inc(s_ct, 1)

            def tanh(g, j):
                m = chunk_rows(j)
                act.wait_ge(s_xg, g * CH + (j + 1))
                act.activation(th[0:m, j % 2, :], x_gate[0:m, j % 2, :], ACT.Tanh, scale=ALPHA / 2)\
                    .then_inc(s_th, 1)

            def up(g, j):
                for n in units_of(j):
                    kind, c = UNITS[n]
                    m = chunk_rows(c)
                    if kind in (0, 2, WEIGHTS):
                        dst, copied = {0: (h1_even[0:m, c % 2, :], s_up_copy), 2: (h1_odd[0:m, c % 2, :], s_up_copy),
                                       WEIGHTS: (c_rows[0:m, c % 2, :], s_c)}[kind]
                        act.wait_ge(s_up_ps, g * len(UNITS) + (n + 1))
                        if kind == WEIGHTS and c > 1:
                            act.wait_ge(s_g, g * CH + (c - 1))
                        act.activation(dst, bank[6 + n % 2][0:m, 0:GC], ACT.Copy).then_inc(copied, 1)
                if j < CH:
                    tanh(g, j)

            act.wait_ge(s_phase2, PHASE2_FILLS)
            rows_t(0, first=True)
            qkv(0)
            high_parts(0)
            heads_t(0)
            heads_t_rest(0)
            for n in range(3):
                exponentials(0, n)
            attended(0)
            project(0)
            rows_t(1)
            qkv(1, range(GT - 1))
            experts_input_t(0)
            input_high(0)
            qkv(1, (GT - 1,))

            def turn(i, front):
                gate(i)
                up(i, 0)
                up(i, 1)
                high_parts(i + 1)
                up(i, 2)
                heads_t(i + 1)
                heads_t_rest(i + 1)
                up(i, 3)
                up(i, 4)
                exponentials(i + 1, 0)
                exponentials(i + 1, 1)
                weights_t(i)
                up(i, 5)
                exponentials(i + 1, 2)
                up(i, 6)
                attended(i + 1)
                up(i, CH)
                project(i + 1)
                if front:
                    rows_t(i + 2)
                    qkv(i + 2, range(GT - 1))
                experts_input_t(i + 1)
                input_high(i + 1)
                if front:
                    qkv(i + 2, (GT - 1,))

            with act.Fori(0, GROUPS - 2) as i:
                turn(i, True)
            turn(GROUPS - 2, False)
            gate(GROUPS - 1)
            for j in range(CH + 1):
                if j == WEIGHTS_BEFORE:
                    weights_t(GROUPS - 1)
                up(GROUPS - 1, j)

        @block.gpsimd
        def _(pool):
            pool.memset(v_ones[:, :, :, :, :].rearrange("p u b h d -> p (u b h d)"), 1.0).then_inc(s_setup_p, 1)
            pool.wait_ge(s_setup_p, 1)
            for u in range(2):
                pool.memset(v_ones[0:1, u, 0, :, :], 0.0).then_inc(s_setup_p, 1)
                pool.wait_ge(s_setup_p, u + 2)
            pool.wait_ge(s_setup_v, 1)

            def image_affine(t):
                pool.wait_ge(s_xn_unit, t + 1)
                pool.tensor_tensor(xn[:, :, :], xn[:, :, :], ln_w_sb[:, :, :], ALU.mult).then_inc(s_xn_w, 1)
                pool.wait_ge(s_xn_w, t + 1)
                pool.tensor_tensor(xn[:, :, :], xn[:, :, :], ln_b_sb[:, :, :], ALU.add).then_inc(s_xn, 1)

            def image_low_k(t):
                for b in range(2):
                    pool.wait_ge(s_hi, t * 4 + (2 * b + 2))
                    pool.tensor_tensor(stack[:, b, H:2 * H, 1:4:2, :],
                                       qkn[:, b, H:2 * H, :][:, :, None, :].broadcast_to([B, H, 2, DH]),
                                       stack[:, b, H:2 * H, 0:4:2, :], ALU.subtract).then_inc(s_lo_k, 1)

            image_affine(0)
            with pool.Fori(0, IMAGES - 1) as i:
                image_low_k(i)
                image_affine(i + 1)
            image_low_k(IMAGES - 1)

            pool.wait_ge(s_h1_stored, 16 * IMAGES + 16)
            pool.memset(v_ones2[:, :, :, :].rearrange("p u h d -> p (u h d)"), 1.0).then_inc(s_phase2, 1)
            pool.memset(probs2[:, :, :, :].rearrange("p u h s -> p (u h s)"), 0.0).then_inc(s_phase2, 1)
            pool.memset(q_bd2[:, :, :, :, :].rearrange("p u h e s -> p (u h e s)").bitcast(F32), 0.0)\
                .then_inc(s_phase2, 1)
            pool.wait_ge(s_phase2, 3)
            pool.memset(x_t2[HALF:K1, :, :, :], 1.0).then_inc(s_phase2, 1)
            pool.wait_ge(s_phase2, 4)
            pool.memset(x3_t[HALF:K1, :, :, :], 1.0).then_inc(s_phase2, 1)

            def low_k(g):
                for u in range(GT):
                    pool.wait_ge(s_hi2, g * (2 * GT) + (2 * u + 2))
                    pool.tensor_tensor(stack2[:, u, H:2 * H, 1:4:2, :],
                                       qkn2[:, u, H:2 * H, :][:, :, None, :].broadcast_to([T, H, 2, DH]),
                                       stack2[:, u, H:2 * H, 0:4:2, :], ALU.subtract).then_inc(s_lo2_k, 1)

            def weigh(g, j):
                m = chunk_rows(j)
                pool.wait_ge(s_gated, g * CH + (j + 1))
                pool.wait_ge(s_c, g * CH + (j + 1))
                pool.tensor_tensor(g_t[0:m, j, :], g_t[0:m, j, :], c_rows[0:m, j % 2, :], ALU.mult).then_inc(s_g, 1)

            low_k(0)
            with pool.Fori(0, GROUPS - 1) as i:
                low_k(i + 1)
                for j in range(CH):
                    weigh(i, j)
            for j in range(CH):
                weigh(GROUPS - 1, j)

        @block.vector
        def _(dve):
            steps = [0]

            dve.memset(q_bd[:, :, :, :, :].rearrange("p u h e s -> p (u h e s)").bitcast(F32), 0.0)
            dve.memset(patches_t[:, :, 0:2], 0.0)
            dve.memset(x_t[HALF:K1, :, :], 1.0)
            dve.memset(combine[:, :, EX:EX2].bitcast(F32), 0.0)
            dve.memset(combine[:, :, EXPERTS:EX].bitcast(F32), 1.0)
            dve.wait_ge(s_const, CONST_LANDED)
            dve.tensor_copy(expand_sb[:, :, :], expand_part[:, :, :])
            dve.tensor_scalar(w_qkv1_sb[:, :, 0:HALF], w_qkv1_sb[:, :, 0:HALF], DH ** -0.5, None, ALU.mult)
            dve.tensor_scalar(neg_ident[:, :], ident_sb[:, :], -1.0, None, ALU.mult)
            for half in range(2):
                dve.tensor_scalar(w_out_scaled[:, half, :], w_out_sb[:, half, :], head_scale_sb[:, half:half + 1],
                                  None, ALU.mult)
            dve.tensor_tensor(embed_add[:, :, :], embed_add[:, :, :], pos_sb[:, :, :], ALU.add)
            dve.tensor_scalar(logit_sb[:, :], logit_sb[:, :], SCALE_MAX, None, ALU.min).then_inc(s_v, 1)
            for n in range(4):
                hi, lo = (w[:, n // 2, (n % 2) * PART:(n % 2) * PART + PART] for w in (w_up_hi, w_up_lo))
                dve.wait_ge(s_w_part, 16 * n + 16)
                dve.tensor_copy(hi, w_up_part).then_inc(s_w_split, 1)
                dve.wait_ge(s_w_split, 2 * n + 1)
                dve.tensor_tensor(lo, w_up_part, hi, ALU.subtract).then_inc(s_w_split, 1)
            dve.wait_ge(s_w_split, 8)
            dve.wait_ge(s_setup_p, 3)
            dve.sem_inc(s_y, 1)
            dve.sem_inc(s_on, 2)
            dve.sem_inc(s_stored, 32 * GT)
            dve.sem_inc(s_h1_stored, 16)
            dve.sem_inc(s_setup_v, 1)
            dve.wait_ge(s_setup_a, 1)

            base = [1]

            def link(ins):
                steps[0] += 1
                ins.then_inc(s_v, 1)
                dve.wait_ge(s_v, base[0] + steps[0])

            def rsqrt(y, v, w):
                link(dve.tensor_scalar(y.bitcast(I32), v.bitcast(I32), -0.5, RSQRT_GUESS, ALU.mult, ALU.add))
                for _ in range(NEWTON):
                    link(dve.scalar_tensor_tensor(out=w, in0=y, scalar=-0.5, in1=y, op0=ALU.mult, op1=ALU.mult))
                    link(dve.tensor_tensor(w, w, v, ALU.mult))
                    link(dve.scalar_tensor_tensor(out=y, in0=w, scalar=1.5, in1=y, op0=ALU.add, op1=ALU.mult))

            def patches_to_columns(t):
                dve.wait_ge(s_pt_ps, t * 3 + 2)
                dve.tensor_copy(patches_t[:, 2:4, 2:SEQ], bank[1][:, 0:2 * PATCHES].rearrange(
                    "p (c s) -> p c s", c=2)).then_inc(s_pt_v, 1)

            def embed(t, first=False):
                dve.wait_ge(s_emb_ps, t * 2 + 2)
                if not first:
                    dve.wait_ge(s_tok_kept, t)
                dve.tensor_tensor(tok[:, :, :].rearrange("p b d -> p (b d)"), bank[1][0:B, 0:2 * D],
                                       embed_add[:, :, :].rearrange("p b d -> p (b d)"), ALU.add)\
                    .then_inc(s_tok, 1)
                dve.wait_ge(s_tok, t + 1)
                for b in range(2):
                    last = dve.bn_stats(stats[:, b, :], tok[:, b, :])
                link(last)
                dve.memset(veps[:, 1:2], EPS)
                for b in range(2):
                    last = dve.bn_aggr(mv[:, b, :], stats[:, b, :])
                last.then_inc(s_part, 1)

            def variance(t, sem=s_sc_ps, count=None):
                dve.wait_ge(sem, count)
                link(dve.tensor_copy(veps[:, 0:1], bank[2][0:B, MOMENTS:MOMENTS + 1]))
                link(dve.tensor_scalar(dev[:, :], mv[:, :, 0], veps[:, 0:1], None, ALU.subtract))
                link(dve.tensor_tensor(dev[:, :], dev[:, :], dev[:, :], ALU.mult))
                dve.tensor_tensor(var[:, :], dev[:, :], mv[:, :, 1], ALU.add).then_inc(s_part, 1)

            def normalize(t, sem=s_sc_ps, count=None):
                dve.wait_ge(sem, count)
                dve.tensor_tensor(veps[:, 1:2], bank[2][0:B, MOMENTS + 1:MOMENTS + 2], veps[:, 1:2], ALU.add)\
                    .then_inc(s_moments, 1)
                dve.wait_ge(s_moments, t + 1)
                rsqrt(rstd[:, 0:1], veps[:, 1:2], half_y[:, 0:1])
                dve.tensor_scalar(xn[:, :, :], tok[:, :, :], veps[:, 0:1], rstd[:, 0:1],
                                  ALU.subtract, ALU.mult).then_inc(s_xn_unit, 1)

            def image_low_q(t):
                dve.wait_ge(s_qk, t * 2 + 2)
                for b in range(2):
                    dve.wait_ge(s_hi, t * 4 + (2 * b + 1))
                    dve.tensor_tensor(stack[:, b, 0:H, 2:4, :],
                                      qkn[:, b, 0:H, :][:, :, None, :].broadcast_to([B, H, 2, DH]),
                                      stack[:, b, 0:H, 0:2, :], ALU.subtract).then_inc(s_lo_q, 1)

            def image_v(t, u):
                dve.wait_ge(s_v_ps, t + 1)
                for b in range(2):
                    dve.tensor_scalar(v_ones[:, u, b, :, 0:DH], bank[1][0:B, b * D:b * D + D].rearrange(
                        "p (h d) -> p h d", h=H), keep_sb[:, b:b + 1], None, ALU.mult).then_inc(s_vo, 1)

            def image_heads_t(t, u, n):
                dve.wait_ge(s_qt_ps, t * 3 + (n + 1))
                dve.tensor_copy(q_bd[64:128, u, 2 * n:2 * n + 2, 1, :], bank[1][64:128, 0:2 * SEQ].rearrange(
                    "p (h s) -> p h s", h=2)).then_inc(s_q_v, 1)

            def image_maxima(t, u, p):
                for b in range(2):
                    dve.wait_ge(s_sc_ps, t * (2 * HP) + (2 * p + b + 1))
                    dve.tensor_reduce(row_max[:, u, b, 2 * p:2 * p + 2], bank[2 + b][0:B, 0:2 * SEQ].rearrange(
                        "p (e s) -> p e s", e=2), AX.X, ALU.max).then_inc(s_max, 1)

            def image_rows(t, u):
                for b in range(2):
                    dve.wait_ge(s_otok_ps, t * 2 + (b + 1))
                    src = bank[4 + b][0:B, 0:3 * 128].rearrange("p (h d) -> p h d", h=H)
                    link(dve.reciprocal(r_den[:, b, :], src[:, :, DH]))
                    dve.tensor_tensor(o_n[:, b, :].rearrange("p (h d) -> p h d", h=H), src[:, :, 0:DH],
                                      r_den[:, b, :][:, :, None].broadcast_to([B, H, DH]), ALU.mult)\
                        .then_inc(s_on, 1)
                dve.wait_ge(s_on, t * 2 + 4)
                dve.wait_ge(s_h1_stored, t * 16 + 16)
                for b in range(2):
                    last = dve.scalar_tensor_tensor(out=h1[:, b, :], in0=o_n[:, b, :], scalar=keep_sb[:, b:b + 1],
                                                    in1=tok_kept[:, u, b, :], op0=ALU.mult, op1=ALU.add)
                last.then_inc(s_h1, 1)

            def attend(t, u, heads, tokens):
                image_maxima(t, u, 1)
                image_maxima(t, u, 2)
                if heads:
                    image_v(t + 1, 1 - u)
                if tokens:
                    patches_to_columns(t + 2)
                image_maxima(t, u, 3)
                if heads:
                    image_low_q(t + 1)
                if tokens:
                    embed(t + 2)
                image_maxima(t, u, 4)
                if heads:
                    image_heads_t(t + 1, 1 - u, 0)
                if tokens:
                    variance(t + 2, count=t * (2 * HP) + 9)
                if heads:
                    image_heads_t(t + 1, 1 - u, 1)
                image_maxima(t, u, 5)
                if tokens:
                    normalize(t + 2, count=t * (2 * HP) + 11)
                if heads:
                    image_heads_t(t + 1, 1 - u, 2)
                    image_maxima(t + 1, 1 - u, 0)
                image_rows(t, u)

            base[0] = 1
            patches_to_columns(0)
            embed(0, first=True)
            variance(0, s_ln1_ps, 1)
            normalize(0, s_ln1_ps, 2)
            image_v(0, 0)
            patches_to_columns(1)
            image_low_q(0)
            embed(1)
            variance(1, s_ln1_ps, 3)
            normalize(1, s_ln1_ps, 4)
            for n in range(3):
                image_heads_t(0, 0, n)
            image_maxima(0, 0, 0)
            assert steps[0] == 2 * STEPS_OF_TOKENS, steps[0]
            steps[0] = 0
            with dve.Fori(0, IMAGES // 2 - 1) as i:
                base[0] = i * (2 * STEPS_OF_AN_IMAGE) + (2 * STEPS_OF_TOKENS + 1)
                attend(i * 2, 0, True, True)
                attend(i * 2 + 1, 1, True, True)
            assert steps[0] == 2 * STEPS_OF_AN_IMAGE, steps[0]
            steps[0] = 0
            base[0] = (IMAGES - 2) * STEPS_OF_AN_IMAGE + 2 * STEPS_OF_TOKENS + 1
            attend(IMAGES - 2, 0, True, False)
            attend(IMAGES - 1, 1, False, False)
            assert steps[0] == 2 * (STEPS_OF_AN_IMAGE - STEPS_OF_TOKENS), steps[0]

            def layer_norms(dst, src, landed, done):
                for u in range(GT):
                    if landed is not None:
                        dve.wait_ge(s_h_in[u], landed)
                    last = dve.bn_stats(stats2[:, u, :], src[:, u, :])
                link(last)
                dve.memset(veps2[:, :], EPS)
                for u in range(GT):
                    last = dve.bn_aggr(mv2[:, u, :], stats2[:, u, :])
                link(last)
                link(dve.tensor_tensor(veps2[:, :], mv2[:, :, 1], veps2[:, :], ALU.add))
                rsqrt(rstd2[:, :], veps2[:, :], half_y2[:, 0:GT])
                for u in range(GT):
                    dve.tensor_scalar(dst[:, u, :], src[:, u, :], mv2[:, u, 0:1], rstd2[:, u:u + 1],
                                      ALU.subtract, ALU.mult).then_inc(done, 1)

            def rows(g):
                layer_norms(xn2, h_in, g * 32 + 32, s_xn2)

            def norms(g, tiles=range(GT)):
                for u in tiles:
                    dve.wait_ge(s_squares, g * GT + (u + 1))
                    last = dve.tensor_reduce(norm2[:, u, :], qkn2[:, u, :, :], AX.X, ALU.add)
                link(last)

            def scales(g):
                flat = norm2[:, :, :].rearrange("p u h -> p (u h)")
                link(dve.tensor_scalar(flat, flat, NORM_EPS ** 2, None, ALU.max))
                rsqrt(rnorm[:, :, :].rearrange("p u h -> p (u h)"), flat, half_y2[:, :])
                link(dve.tensor_tensor(rnorm[:, :, 0:H], rnorm[:, :, 0:H],
                                       logit_scale[:, None, :].broadcast_to([T, GT, H]), ALU.mult))

            def unit_qk(g):
                for u in range(GT):
                    dve.tensor_tensor(qkn2[:, u, :, :], qk2[:, u, :, :],
                                      rnorm[:, u, :][:, :, None].broadcast_to([T, 2 * H, DH]), ALU.mult)\
                        .then_inc(s_qkn2, 1)

            def low_q(g):
                for u in range(GT):
                    dve.wait_ge(s_hi2, g * (2 * GT) + (2 * u + 1))
                    dve.tensor_tensor(stack2[:, u, 0:H, 2:4, :],
                                      qkn2[:, u, 0:H, :][:, :, None, :].broadcast_to([T, H, 2, DH]),
                                      stack2[:, u, 0:H, 0:2, :], ALU.subtract).then_inc(s_lo2_q, 1)

            def heads_t(g):
                for u in range(GT):
                    dve.wait_ge(s_st2_ps, g * (3 * GT) + (2 * GT + u + 1))
                    dve.tensor_copy(q_bd2[64:128, u, 2:6, 1, :], bank[2 * u][64:128, :].rearrange(
                        "p (h s) -> p h s", h=4)).then_inc(s_q_bd2, 1)

            def maxima(g):
                for n, heads in enumerate((slice(0, 8), slice(8, H))):
                    for u in range(GT):
                        dve.wait_ge(s_sc2_ps, g * (2 * GT) + (GT * n + u + 1))
                        src = bank[2 * u + n][:, 0:(heads.stop - heads.start) * IMAGES]
                        dve.tensor_reduce(row_max2[:, u, heads], src.rearrange("p (h s) -> p h s", s=IMAGES),
                                          AX.X, ALU.max).then_inc(s_max2, 1)

            def divide(g):
                for u in range(GT):
                    dve.wait_ge(s_otok2_ps, g * GT + (u + 1))
                    src = bank[2 * u + 1][:, 0:3 * 128].rearrange("p (h d) -> p h d", h=H)
                    link(dve.reciprocal(r_den2[:, u, :], src[:, :, DH]))
                    dve.tensor_tensor(o_n2[:, u, :].rearrange("p (h d) -> p h d", h=H), src[:, :, 0:DH],
                                      r_den2[:, u, :][:, :, None].broadcast_to([T, H, DH]), ALU.mult)\
                        .then_inc(s_on2, 1)

            def residual(g):
                dve.wait_ge(s_y, g + 1)
                dve.wait_ge(s_h_res, g + 1)
                for u in range(GT):
                    dve.wait_ge(s_proj_ps, g * GT + (u + 1))
                    dve.tensor_tensor(h2[:, u, :], bank[2 * u + 1][:, 0:D], h_res[:, u, :], ALU.add)\
                        .then_inc(s_h2, 1)
                dve.wait_ge(s_h2, g * GT + GT)
                layer_norms(xn3, h2, None, s_x3n)

            def input_low(g):
                dve.wait_ge(s_x3_split, g * 2 + 1)
                dve.tensor_tensor(x3_lo[:, :, :, :].rearrange("p h u s -> p (h u s)"),
                                  x3_t[:, :, :, :].rearrange("p h u s -> p (h u s)"),
                                  x3_hi[:, :, :, :].rearrange("p h u s -> p (h u s)"), ALU.subtract)\
                    .then_inc(s_x3_split, 1)

            def spread(ap, n):
                return ap[:, :, None].broadcast_to([T, GT, n])

            def top2(values, tri, n, keep):
                cmp = g_cmp[:, :, 0:n * n].rearrange("p r (a c) -> p r a c", a=n)
                eq = g_eq[:, :, 0:n * n].rearrange("p r (a c) -> p r a c", a=n)
                for r in range(GT):
                    other = values[:, r, :][:, None, :].broadcast_to([T, n, n])
                    own = values[:, r, :][:, :, None].broadcast_to([T, n, n])
                    dve.tensor_tensor(cmp[:, r, :, :], other, own, ALU.is_gt)
                    last = dve.tensor_tensor(eq[:, r, :, :], other, own, ALU.is_equal)
                link(last)
                for r in range(GT):
                    last = dve.tensor_tensor(eq[:, r, :, :], eq[:, r, :, :], tri, ALU.mult)
                link(last)
                link(dve.tensor_tensor(g_cmp[:, :, 0:n * n], g_cmp[:, :, 0:n * n], g_eq[:, :, 0:n * n], ALU.add))
                link(dve.tensor_reduce(g_rank[:, :, 0:n], cmp, AX.X, ALU.add))
                link(dve.tensor_scalar(keep, g_rank[:, :, 0:n], 1.5, None, ALU.is_lt))

            def gate_logits(g):
                dve.wait_ge(s_gate_ps, g + 1)
                logits = bank[7][:, 0:GT * EXPERTS].rearrange("p (n e) -> p n e", n=GT)
                link(dve.tensor_reduce(g_max[:, :], logits, AX.X, ALU.max))
                dve.tensor_tensor(g_s[:, :, :], logits, spread(g_max[:, :], EXPERTS), ALU.subtract)\
                    .then_inc(s_gate_exp, 1)

            def gate_groups(g):
                dve.wait_ge(s_gate_exp, g * 2 + 2)
                link(dve.tensor_reduce(g_sum[:, :], g_exp[:, :, :], AX.X, ALU.add))
                link(dve.reciprocal(g_rec[:, :], g_sum[:, :]))
                link(dve.tensor_tensor(g_prob[:, :, :], g_exp[:, :, :], spread(g_rec[:, :], EXPERTS), ALU.mult))
                link(dve.tensor_tensor(g_s[:, :, :], g_prob[:, :, :],
                                       gate_b_sb[:, None, :].broadcast_to([T, GT, EXPERTS]), ALU.add))
                pairs = g_s[:, :, :].rearrange("p n (g e) -> p n g e", e=2)
                link(dve.tensor_tensor(g_grp[:, :, :], pairs[:, :, :, 0], pairs[:, :, :, 1], ALU.add))
                top2(g_grp, tri4_sb[:, :, :], 4, g_grp[:, :, :])

            def gate_experts(g):
                kept = g_keep[:, :, :].rearrange("p n (g e) -> p n g e", e=2)
                for e in range(2):
                    last = dve.tensor_copy(kept[:, :, :, e], g_grp[:, :, :])
                link(last)
                link(dve.tensor_tensor(g_s[:, :, :], g_s[:, :, :], g_keep[:, :, :], ALU.mult))
                link(dve.tensor_scalar(g_keep[:, :, :], g_keep[:, :, :], BIG, -BIG, ALU.mult, ALU.add))
                link(dve.tensor_tensor(g_s[:, :, :], g_s[:, :, :], g_keep[:, :, :], ALU.add))
                top2(g_s, tri8_sb[:, :, :], EXPERTS, g_keep[:, :, :])
                link(dve.tensor_tensor(g_keep[:, :, :], g_prob[:, :, :], g_keep[:, :, :], ALU.mult))
                link(dve.tensor_copy(combine[:, :, 0:EXPERTS], g_keep[:, :, :]))
                dve.tensor_tensor(combine[:, :, LOW:LOW + EXPERTS], g_keep[:, :, :], combine[:, :, 0:EXPERTS],
                                  ALU.subtract).then_inc(s_combine, 1)

            def product(g, j, dst, src, kind):
                m = chunk_rows(j)
                n = UNITS.index((kind, j))
                dve.wait_ge(s_up_copy, g * (2 * CH) + copies_until(n))
                dve.wait_ge(s_up_ps, g * len(UNITS) + (n + 1))
                dve.tensor_tensor(dst, src[0:m, j % 2, :], bank[6 + n % 2][0:m, 0:GC], ALU.mult)\
                    .then_inc(s_up_read, 1)

            def up_even(g, j):
                if j < CH:
                    product(g, j, x_gate[0:chunk_rows(j), j % 2, :], h1_even, 1)
                if j >= 1:
                    m = chunk_rows(j - 1)
                    ln = lin[0:m, :]
                    link(dve.scalar_tensor_tensor(out=ln, in0=ln, scalar=1.0 + LIMIT, in1=x_gate[0:m, (j - 1) % 2, :],
                                                  op0=ALU.min, op1=ALU.mult))
                if j < CH:
                    m = chunk_rows(j)
                    dve.wait_ge(s_up_read, g * (2 * CH) + (2 * j + 1))
                    dve.tensor_scalar(x_gate[0:m, j % 2, :], x_gate[0:m, j % 2, :], LIMIT, None, ALU.min)\
                        .then_inc(s_xg, 1)
                    dve.wait_ge(s_xg, g * CH + (j + 1))

            def up_odd(g, j):
                if j >= 1:
                    m = chunk_rows(j - 1)
                    dve.wait_ge(s_th, g * CH + j)
                    dve.scalar_tensor_tensor(out=g_t[0:m, j - 1, :], in0=th[0:m, (j - 1) % 2, :], scalar=1.0,
                                             in1=lin[0:m, :], op0=ALU.add, op1=ALU.mult).then_inc(s_gated, 1)
                if j < CH:
                    m = chunk_rows(j)
                    if j >= 1:
                        dve.wait_ge(s_gated, g * CH + j)
                    product(g, j, lin[0:m, :], h1_odd, 3)
                    dve.wait_ge(s_up_read, g * (2 * CH) + (2 * j + 2))
                    link(dve.tensor_scalar(lin[0:m, :], lin[0:m, :], 1.0, 1.0 - LIMIT, ALU.add, ALU.max))

            def down(g):
                dve.wait_ge(s_stored, g * (32 * GT) + 32 * GT)
                dve.wait_ge(s_down_ps, g + 1)
                dve.tensor_tensor(y_sb[:, 0:2, :].rearrange("p u d -> p (u d)"), bank[6][:, 0:2 * D],
                                  h2[:, 0:2, :].rearrange("p u d -> p (u d)"), ALU.add)
                dve.tensor_tensor(y_sb[:, 2, :], bank[7][:, 0:D], h2[:, 2, :], ALU.add).then_inc(s_y, 1)

            steps[0] = 0
            base[0] = FIRST_STEPS + 1
            dve.wait_ge(s_phase2, PHASE2_FILLS)
            rows(0)
            norms(0)
            scales(0)
            unit_qk(0)
            low_q(0)
            heads_t(0)
            maxima(0)
            divide(0)
            rows(1)
            residual(0)
            norms(1, range(GT - 1))
            input_low(0)
            assert steps[0] == STEPS_OF_FIRST_GROUP, steps[0]

            def turn(i, front):
                gate_logits(i)
                norms(i + 1, (GT - 1,))
                up_even(i, 0)
                up_odd(i, 0)
                scales(i + 1)
                up_even(i, 1)
                unit_qk(i + 1)
                up_odd(i, 1)
                up_even(i, 2)
                low_q(i + 1)
                up_odd(i, 2)
                gate_groups(i)
                heads_t(i + 1)
                up_even(i, 3)
                up_odd(i, 3)
                maxima(i + 1)
                up_even(i, 4)
                up_odd(i, 4)
                gate_experts(i)
                for j in range(5, CH + 1):
                    up_even(i, j)
                    up_odd(i, j)
                divide(i + 1)
                if front:
                    rows(i + 2)
                down(i)
                residual(i + 1)
                if front:
                    norms(i + 2, range(GT - 1))
                input_low(i + 1)

            steps[0] = 0
            with dve.Fori(0, GROUPS - 2) as i:
                base[0] = i * STEPS_OF_A_GROUP + (FIRST_STEPS + STEPS_OF_FIRST_GROUP + 1)
                turn(i, True)
            assert steps[0] == STEPS_OF_A_GROUP, steps[0]
            steps[0] = 0
            base[0] = FIRST_STEPS + STEPS_OF_FIRST_GROUP + (GROUPS - 2) * STEPS_OF_A_GROUP + 1
            turn(GROUPS - 2, False)
            gate_logits(GROUPS - 1)
            gate_groups(GROUPS - 1)
            gate_experts(GROUPS - 1)
            for j in range(CH + 1):
                up_even(GROUPS - 1, j)
                up_odd(GROUPS - 1, j)
            down(GROUPS - 1)


STEPS_OF_TOKENS = 14
STEPS_OF_AN_IMAGE = 16
FIRST_STEPS = IMAGES * STEPS_OF_AN_IMAGE
STEPS_OF_FIRST_GROUP = 56
STEPS_OF_A_GROUP = 79


def kernel(**inputs):
    import concourse.bacc as bacc
    from concourse.bass_utils import run_bass_kernel_spmd

    f = {k: np.asarray(v) for k, v in inputs.items()}
    f32 = np.float32

    i, j = np.arange(SEQ - 1, dtype=f32)[:, None], np.arange(D, dtype=f32)[None, :]
    even = (np.arange(D) % 2 == 0)[None, :]
    angle = np.where(even, i / np.power(f32(1e4), j / f32(D)), i / np.power(f32(1e4), (j - f32(1)) / f32(D)))
    table = np.where(even, np.sin(angle), np.cos(angle)).astype(f32)

    def tokens(rows):
        return np.ascontiguousarray(rows.reshape(2, B, -1).transpose(1, 0, 2))

    def halves(w, bias):
        full = np.zeros((K1, 2, w.shape[1]), f32)
        full[0:HALF] = w.reshape(2, HALF, -1).transpose(1, 0, 2)
        if bias is not None:
            full[HALF, 0] = bias
        return full

    pos = tokens(np.concatenate([np.zeros((1, D), f32), table]))
    base = tokens(np.concatenate([f["cls_tok"].reshape(1, D), f["L0_tok_class_token"].reshape(1, D),
                                  np.broadcast_to(f["L0_tok_b_map"], (PATCHES, D))]))
    ln_w = tokens(np.concatenate([f["L0_tok_ln_w"][0:1], f["L0_tok_ln_w"]]))
    ln_b = tokens(np.concatenate([f["L0_tok_ln_b"][0:1], f["L0_tok_ln_b"]]))
    keep = np.ones((B, 2), f32)
    keep[0, 0] = 0
    mean_w = np.full((B, 2, B), 1.0 / (SEQ - 1), f32)
    mean_w[0, 0, :] = 0
    tri = [np.ascontiguousarray(np.broadcast_to(np.tril(np.ones((n, n), f32), -1), (T, n, n))) for n in (4, 8)]
    expand = np.zeros((EX2, CH * 128), f32)
    for e in range(EX):
        for row in (e, LOW + e):
            expand[row, e * INNER:(e + 1) * INNER] = 0.5
    w_map = np.ascontiguousarray(f["L0_tok_W_map"].T.reshape(PC, 128, D).transpose(1, 0, 2))

    w_qkv1 = np.zeros((K1, 2, 3, HALF), f32)
    for s, name in enumerate("qkv"):
        w, bias = f[f"L0_tok_W{name}"], f[f"L0_tok_b{name}"].reshape(2, HALF)
        for h in range(H):
            r = DH * (h % HP)
            w_qkv1[r:r + DH, h // HP, s, r:r + DH] = w[h].T
        w_qkv1[HALF, :, s, :] = bias
    w_qkv1 = w_qkv1.reshape(K1, 2, 3 * HALF)
    w_qkv2 = halves(f["L0_attn_in_proj_weight"].T, f["L0_attn_in_proj_bias"])
    logit = np.ascontiguousarray(np.broadcast_to(f["L0_attn_logit_scale"].reshape(1, H), (T, H)))
    w_out = halves(f["L0_attn_out_w"].T, f["L0_attn_out_b"])
    head_scale = np.ones((K1, 2), f32)
    head_scale[0:HALF] = np.repeat(f["L0_attn_head_scale"].reshape(2, HP), DH, axis=1).T
    gate_w = halves(f["L0_ffn_gate_w"].T, None)
    gate_b = np.ascontiguousarray(np.broadcast_to(f["L0_ffn_gate_b"], (T, EXPERTS)))

    def up(name):
        w = np.concatenate([f[f"L0_ffn_W{name}"], f[f"L0_ffn_Ws{name}"][None]])
        bias = np.concatenate([f[f"L0_ffn_B{name}"], f[f"L0_ffn_Bs{name}"][None]])
        return w.transpose(1, 0, 2), bias

    parts = [up("1"), up("3")]
    w_up = np.stack([w[:, :, odd::2].reshape(D, ROWS) for odd in range(2) for w, _ in parts], 1)
    b_up = np.stack([bias[:, odd::2].reshape(ROWS) for odd in range(2) for _, bias in parts])
    w_up = halves(w_up.reshape(D, KINDS * ROWS), b_up.reshape(KINDS * ROWS))
    w_down = np.zeros((CH * 128, D), f32)
    w_down[0:ROWS] = np.concatenate([f["L0_ffn_W2"], f["L0_ffn_Ws2"][None]]).reshape(ROWS, D)
    w_down = np.ascontiguousarray(w_down.reshape(CH, 128, D).transpose(1, 0, 2))
    b_down = np.zeros((EX2, D), f32)
    for row in (0, LOW):
        b_down[row:row + EX] = np.concatenate([f["L0_ffn_B2"], f["L0_ffn_Bs2"][None]])

    arrays = {
        "x": f["x"].reshape(IMAGES, PATCHES, PIX), "ident": np.eye(128, dtype=f32), "base": base, "pos": pos,
        "ln_w": ln_w, "ln_b": ln_b, "mean_w": mean_w, "keep": keep, "tri4": tri[0], "tri8": tri[1],
        "expand": expand.reshape(EX2, CH, 128), "w_map": w_map, "w_qkv1": w_qkv1, "w_qkv2": w_qkv2,
        "logit": logit, "w_out": w_out, "head_scale": head_scale, "gate_w": gate_w, "gate_b": gate_b,
        "w_up": w_up, "w_down": w_down, "b_down": b_down,
    }
    nc = bacc.Bacc("TRN2", target_bir_lowering=False, num_devices=1)
    in_map, args = {}, []
    for name, a in arrays.items():
        a = np.ascontiguousarray(a)
        in_map[f"in_{name}"] = a
        args.append(nc.dram_tensor(f"in_{name}", a.shape, mybir.dt.from_np(a.dtype), kind="ExternalInput").ap())
    out = nc.dram_tensor("out", (IMAGES, SEQ, D), F32, kind="ExternalOutput").ap()
    h1_dram = nc.dram_tensor("h1_dram", (IMAGES, SEQ, D), F32, kind="Internal").ap()
    vit_block(nc, *args, h1_dram, out)
    result = run_bass_kernel_spmd(nc, [in_map], core_ids=[0])
    return result.results[0]["out"]
```
